# Optimizing a Trainium2 kernel written in Bass

```python
import numpy as np
import jax
import jax.numpy as jnp

def _softmax(x, axis=-1):
    return jax.nn.softmax(x, axis=axis)

def _gelu(x):
    return jax.nn.gelu(x, approximate=True)

def _silu(x):
    return jax.nn.silu(x)

def _sigmoid(x):
    return jax.nn.sigmoid(x)

def _layernorm(x, axis=-1, eps=1e-05):
    m = jnp.mean(x, axis=axis, keepdims=True)
    v = jnp.var(x, axis=axis, keepdims=True)
    return (x - m) / jnp.sqrt(v + eps)

def _scatter_add(tgt, idx, src, axis=0):
    return tgt.at[idx].add(src)

def _segment_sum(src, seg, n):
    return jax.ops.segment_sum(src, seg, n)
kernel_name = 'mk_xattn_ffn_d4_seqx_r8_b1a780'

def setup_inputs(seed: int=0):
    np.random.seed(seed)
    _w = jnp.asarray

    def _rec_inputs():
        import jax
        import jax.numpy as jnp
        _rk = jax.random.key(seed)
        x = -0.0002928 + 1 * jax.random.normal(jax.random.fold_in(_rk, 1), (4, 512, 128), jnp.float32)
        _lenS = 512 - jax.random.randint(jax.random.fold_in(_rk, 7), (4,), 0, max(1, 512 // 4) + 1, jnp.int32)
        _lenS2 = 77 - jax.random.randint(jax.random.fold_in(_rk, 8), (4,), 0, max(1, 77 // 4) + 1, jnp.int32)
        _ctx_1024P = jax.random.normal(jax.random.fold_in(_rk, 11), (4, 16, 128), jnp.float32)
        _ctx_1024c = jax.random.dirichlet(jax.random.fold_in(_rk, 511), 0.3 * jnp.ones((16,), jnp.float32), (4, 77))
        _ctx_1024t = jnp.einsum('bsk,bkd->bsd', _ctx_1024c, _ctx_1024P)
        _ctx_1024t = _ctx_1024t * jax.lax.rsqrt(jnp.mean(jnp.square(_ctx_1024t)) + 1e-12) * 0.953939
        ctx_1024 = -1.39393e-06 + 0.999914 * (_ctx_1024t + 0.3 * jax.random.normal(jax.random.fold_in(_rk, 611), (4, 77, 128), jnp.float32))
        itok_BxS_0_7 = jax.random.randint(jax.random.fold_in(_rk, 14), (4, 512), 0, 8, jnp.int32)
        itok_BxS_0_4092 = jax.random.randint(jax.random.fold_in(_rk, 15), (4, 512), 0, 4093, jnp.int32)
        _validS = jnp.arange(512)[None, :] < _lenS[:, None]
        _validS2 = jnp.arange(77)[None, :] < _lenS2[:, None]
        _causal = jnp.tril(jnp.ones((512, 512), dtype=bool))
        mask_SxS2_bk1 = jnp.broadcast_to(_validS2[0:1, :], (512, 77))
        mask_BxS2_bf0 = jnp.logical_not(jnp.ones((4, 77), dtype=bool))
        mask_SxS2_fk1 = jnp.where(jnp.broadcast_to(_validS2[0:1, :], (512, 77)), 1.0, 0.0).astype(jnp.float32)
        return (x, ctx_1024, itok_BxS_0_7, itok_BxS_0_4092, mask_SxS2_bk1, mask_BxS2_bf0, mask_SxS2_fk1)
    x, ctx_1024, itok_BxS_0_7, itok_BxS_0_4092, mask_SxS2_bk1, mask_BxS2_bf0, mask_SxS2_fk1 = _rec_inputs()

    def _L0_xattn_setup():
        import jax, jax.numpy as jnp
        import numpy as np
        B, T, D, H = (2, 256, 128, 16)
        DK = D // H
        SCALE = 1.0 / float(np.sqrt(DK))
        key0 = jax.random.key(seed)
        ks = jax.random.split(key0, 12)
        std = 0.02
        inp = {'query': jax.random.normal(ks[0], (B, T, D), jnp.float32), 'key': jax.random.normal(ks[1], (B, T, D), jnp.float32), 'value': jax.random.normal(ks[2], (B, T, D), jnp.float32), 'Wq': jax.random.normal(ks[3], (D, D), jnp.float32) * std, 'bq': jnp.zeros((D,), jnp.float32), 'Wk': jax.random.normal(ks[4], (D, D), jnp.float32) * std, 'bk': jnp.zeros((D,), jnp.float32), 'Wv': jax.random.normal(ks[5], (D, D), jnp.float32) * std, 'bv': jnp.zeros((D,), jnp.float32), 'Wo': jax.random.normal(ks[6], (D, D), jnp.float32) * std, 'bo': jnp.zeros((D,), jnp.float32), 'attn_mask': jnp.triu(jnp.ones((T, T), jnp.bool_), k=1), 'key_padding_mask': jnp.zeros((B, T), jnp.bool_)}
        return inp
    _L0_xattn_all = _L0_xattn_setup()
    _L0_xattn_in = {k: v for k, v in _L0_xattn_all.items() if k in ('Wq', 'bq', 'Wk', 'bk', 'Wv', 'bv', 'Wo', 'bo')}
    del _L0_xattn_all

    def _L0_ffn_setup():
        import jax, jax.numpy as jnp
        import numpy as np
        B, S, D = (4, 512, 128)
        E, I = (8, 256)
        CAPACITY = 2
        K = max(1, int(S / E * CAPACITY))
        key = jax.random.key(seed)
        k1, k2, k3, k4, k5 = jax.random.split(key, 5)
        x = jax.random.normal(k1, (B, S, D), dtype=jnp.float32)
        gate_w = jax.random.normal(k2, (D, E), dtype=jnp.float32) * 0.006
        Wg = jax.random.normal(k3, (E, D, I), dtype=jnp.float32) * 0.02
        Wu = jax.random.normal(k4, (E, D, I), dtype=jnp.float32) * 0.02
        Wd = jax.random.normal(k5, (E, I, D), dtype=jnp.float32) * 0.02
        return {'x': x, 'gate_w': gate_w, 'Wg': Wg, 'Wu': Wu, 'Wd': Wd}
    _L0_ffn_all = _L0_ffn_setup()
    _L0_ffn_in = {k: v for k, v in _L0_ffn_all.items() if k in ('gate_w', 'Wg', 'Wu', 'Wd')}
    del _L0_ffn_all

    def _L1_xattn_setup():
        import math
        import jax, jax.numpy as jnp
        import numpy as np
        B, T, L, H = (4, 512, 512, 128)

        def _forward(hidden_states, advisor_states, advisor_ids, pointer_ids, Wqj, Wkj, Wvj, Wqi, Wki, Wvi, Wout, gain, council_weights):
            b, t, h = hidden_states.shape
            l = advisor_states.shape[1]
            inv_sqrt_h = 1.0 / math.sqrt(float(h))
            p = pointer_ids[:, :, None]
            indices = jnp.clip(jnp.concatenate([p, p + 1, p + 2], axis=-1), 0, l - 1)
            win_states = jax.vmap(lambda a, idx: a[idx])(advisor_states, indices)
            win_ids = jax.vmap(lambda a, idx: a[idx])(advisor_ids, indices)
            qj = hidden_states @ Wqj.T
            kj = win_states @ Wkj.T
            vj = win_states @ Wvj.T
            sj = jnp.einsum('bth,btwh->btw', qj, kj) * inv_sqrt_h
            l_rel, l_v1, l_v2 = (sj[:, :, 0], sj[:, :, 1], sj[:, :, 2])
            rel_ids = win_ids[:, :, 0]
            is_and = (rel_ids == 0).astype(sj.dtype)
            is_or = (rel_ids == 1).astype(sj.dtype)
            is_not = (rel_ids == 2).astype(sj.dtype)
            is_implies = (rel_ids == 3).astype(sj.dtype)
            is_xor = (rel_ids == 4).astype(sj.dtype)
            l_new = is_and * (l_v1 + l_v2) + is_or * jnp.maximum(l_v1, l_v2) + is_not * -l_v1 + is_implies * jnp.maximum(-l_v1, l_v2) + is_xor * jnp.abs(l_v1 - l_v2)
            mask_any = jnp.clip(is_and + is_or + is_not + is_implies + is_xor, 0.0, 1.0)
            l_final = mask_any * l_new + (1.0 - mask_any) * l_rel
            sj = jnp.stack([l_final, l_v1, l_v2], axis=-1)
            aj = jax.nn.softmax(sj, axis=-1)
            cj = jnp.einsum('btw,btwh->bth', aj, vj)
            qi = hidden_states @ Wqi.T
            ki = win_states @ Wki.T
            vi = win_states @ Wvi.T
            si = jnp.einsum('bth,btwh->btw', qi, ki) * inv_sqrt_h
            ai = jax.nn.softmax(si, axis=-1)
            ci = jnp.einsum('btw,btwh->bth', ai, vi)
            w = jax.nn.softmax(council_weights, axis=0)
            context = w[0] * cj + w[1] * ci
            return context @ Wout.T * gain
        key = jax.random.key(seed)
        ks = jax.random.split(key, 12)
        inp = {'hidden_states': jax.random.normal(ks[0], (B, T, H), jnp.float32), 'advisor_states': jax.random.normal(ks[1], (B, L, H), jnp.float32), 'advisor_ids': jax.random.randint(ks[2], (B, L), 0, 8, jnp.int32), 'pointer_ids': jax.random.randint(ks[3], (B, T), 0, L - 2, jnp.int32)}
        s = 1.0 / math.sqrt(H)
        names = ['Wqj', 'Wkj', 'Wvj', 'Wqi', 'Wki', 'Wvi', 'Wout']
        for i, n in enumerate(names):
            inp[n] = jax.random.normal(ks[4 + i], (H, H), jnp.float32) * s
        inp['gain'] = jnp.asarray(0.1, jnp.float32)
        inp['council_weights'] = jnp.ones((2,), jnp.float32)
        return inp
    _L1_xattn_all = _L1_xattn_setup()
    _L1_xattn_in = {k: v for k, v in _L1_xattn_all.items() if k in ('Wqj', 'Wkj', 'Wvj', 'Wqi', 'Wki', 'Wvi', 'Wout', 'gain', 'council_weights')}
    del _L1_xattn_all

    def _L1_ffn_setup():
        import jax, jax.numpy as jnp
        import numpy as np
        DIM = 128
        DEPTH = 6
        HEADS = 16
        DIM_HEAD = 64
        WINDOW = 32
        INNER = HEADS * DIM_HEAD
        DIM_INNER = int(DIM * 4 * 2 / 3)
        QK_SCALE = 8.0

        def shift_tokens(t):
            a, s = jnp.split(t, 2, -1)
            s = jnp.pad(s, ((0, 0), (1, 0), (0, 0)))[:, :-1]
            return jnp.concatenate([a, s], -1)

        def l2norm(t):
            return t / jnp.maximum(jnp.linalg.norm(t, axis=-1, keepdims=True), 1e-12)

        def rotate_half(x):
            x1, x2 = jnp.split(x, 2, -1)
            return jnp.concatenate([-x2, x1], -1)

        def rotary_tables(n):
            half = jnp.arange(0, DIM_HEAD, 2, dtype=jnp.float32)
            inv_freq = 1.0 / 10000.0 ** (half / DIM_HEAD)
            t = jnp.arange(n, dtype=jnp.float32)
            freqs = t[:, None] * inv_freq[None, :]
            freqs = jnp.concatenate([freqs, freqs], -1)
            base_scale = (half + 0.4 * DIM_HEAD) / (1.4 * DIM_HEAD)
            power = (t - n // 2) / (WINDOW // 2)
            scale = base_scale[None, :] ** power[:, None]
            scale = jnp.concatenate([scale, scale], -1)
            return (freqs, scale)

        def local_attention(q, k, v):
            b, h, n, d = q.shape
            w = WINDOW
            nw = n // w
            bq = q.reshape(b, h, nw, w, d)
            bk = k.reshape(b, h, nw, w, d)
            bv = v.reshape(b, h, nw, w, d)

            def look(t):
                p = jnp.pad(t, ((0, 0), (0, 0), (1, 0), (0, 0), (0, 0)))
                return jnp.concatenate([p[:, :, :nw], p[:, :, 1:]], axis=3)
            bk2, bv2 = (look(bk), look(bv))
            seq = jnp.arange(n).reshape(nw, w)
            seq_p = jnp.pad(seq, ((1, 0), (0, 0)), constant_values=-1)
            jt = jnp.concatenate([seq_p[:nw], seq_p[1:]], axis=1)
            it = seq[:, :, None]
            jb = jt[:, None, :]
            mask = (it < jb) | (it > jb + w) | (jb == -1)
            sim = jnp.einsum('bhwie,bhwje->bhwij', bq, bk2) * QK_SCALE
            sim = jnp.where(mask, -jnp.finfo(sim.dtype).max, sim)
            attn = jax.nn.softmax(sim, -1)
            out = jnp.einsum('bhwij,bhwje->bhwie', attn, bv2)
            return out.reshape(b, h, n, d)

        def attn_layer(x, Wqkv, qs, ksc, Wo):
            b, n, _ = x.shape
            qkv = x @ Wqkv
            q, k, v = jnp.split(qkv, 3, -1)
            sh = lambda t: t.reshape(b, n, HEADS, DIM_HEAD).transpose(0, 2, 1, 3)
            q, k, v = (sh(q), sh(k), sh(v))
            q = l2norm(q) * qs
            k = l2norm(k) * ksc
            freqs, scale = rotary_tables(n)
            cos, sin = (jnp.cos(freqs), jnp.sin(freqs))
            q = q * cos * scale + rotate_half(q) * sin * scale
            inv = 1.0 / scale
            k = k * cos * inv + rotate_half(k) * sin * inv
            out = local_attention(q, k, v)
            out = out.transpose(0, 2, 1, 3).reshape(b, n, INNER)
            return out @ Wo

        def ffn_layer(x, g, bln, W1, b1, W2, b2):
            mu = x.mean(-1, keepdims=True)
            var = ((x - mu) ** 2).mean(-1, keepdims=True)
            xn = (x - mu) / jnp.sqrt(var + 1e-05) * g + bln
            hg = xn @ W1 + b1
            a, gate = jnp.split(hg, 2, -1)
            return a * jax.nn.gelu(gate, approximate=False) @ W2 + b2
        key = jax.random.key(seed)
        ks = jax.random.split(key, 8)
        B, N = (2, 256)
        init = lambda k, shape: jax.random.normal(k, shape, jnp.float32) * 0.02
        return {'x': jax.random.normal(ks[0], (B, N, DIM), jnp.float32), 'Wqkv': init(ks[1], (DEPTH, DIM, 3 * INNER)), 'q_scale': jnp.ones((DEPTH, DIM_HEAD), jnp.float32), 'k_scale': jnp.ones((DEPTH, DIM_HEAD), jnp.float32), 'Wo': init(ks[2], (DEPTH, INNER, DIM)), 'ln_g': jnp.ones((DEPTH, DIM), jnp.float32), 'ln_b': jnp.zeros((DEPTH, DIM), jnp.float32), 'W1': init(ks[3], (DEPTH, DIM, 2 * DIM_INNER)), 'b1': jnp.zeros((DEPTH, 2 * DIM_INNER), jnp.float32), 'W2': init(ks[4], (DEPTH, DIM_INNER, DIM)), 'b2': jnp.zeros((DEPTH, DIM), jnp.float32)}
    _L1_ffn_all = _L1_ffn_setup()
    _L1_ffn_in = {k: v for k, v in _L1_ffn_all.items() if k in ('Wqkv', 'q_scale', 'k_scale', 'Wo', 'ln_g', 'ln_b', 'W1', 'b1', 'W2', 'b2')}
    del _L1_ffn_all

    def _L2_xattn_setup():
        import jax, jax.numpy as jnp
        import numpy as np
        D_MODEL = 128
        B, S = (4, 256)
        key = jax.random.key(seed)
        ks = jax.random.split(key, 10)
        s = 1.0 / np.sqrt(D_MODEL)
        return {'k': jax.random.normal(ks[0], (B, S, D_MODEL), jnp.float32), 'v': jax.random.normal(ks[1], (B, S, D_MODEL), jnp.float32), 'q': jax.random.normal(ks[2], (B, S, D_MODEL), jnp.float32), 'Wk': jax.random.normal(ks[3], (D_MODEL, D_MODEL), jnp.float32) * s, 'Wv': jax.random.normal(ks[4], (D_MODEL, D_MODEL), jnp.float32) * s, 'bv': jnp.zeros((D_MODEL,), jnp.float32), 'Wq': jax.random.normal(ks[5], (D_MODEL, D_MODEL), jnp.float32) * s, 'bq': jnp.zeros((D_MODEL,), jnp.float32), 'Wo': jax.random.normal(ks[6], (D_MODEL, D_MODEL), jnp.float32) * s, 'bo': jnp.zeros((D_MODEL,), jnp.float32)}
    _L2_xattn_all = _L2_xattn_setup()
    _L2_xattn_in = {k: v for k, v in _L2_xattn_all.items() if k in ('Wk', 'Wv', 'bv', 'Wq', 'bq', 'Wo', 'bo')}
    del _L2_xattn_all

    def _L2_ffn_setup():
        import jax, jax.numpy as jnp
        import numpy as np
        D_MODEL = 128
        D_FF = 512
        NUM_EXPERTS = 8
        TOP_K = 2
        key = jax.random.key(seed)
        ks = jax.random.split(key, 8)
        s_in = 1.0 / np.sqrt(D_MODEL)
        s_ff = 1.0 / np.sqrt(D_FF)
        x = jax.random.normal(ks[0], (2, 256, D_MODEL), dtype=jnp.float32)
        Wg = jax.random.uniform(ks[1], (D_MODEL, NUM_EXPERTS), minval=-s_in, maxval=s_in, dtype=jnp.float32)
        bg = jax.random.uniform(ks[2], (NUM_EXPERTS,), minval=-s_in, maxval=s_in, dtype=jnp.float32)
        W1 = jax.random.uniform(ks[3], (NUM_EXPERTS, D_MODEL, D_FF), minval=-s_in, maxval=s_in, dtype=jnp.float32)
        b1 = jax.random.uniform(ks[4], (NUM_EXPERTS, D_FF), minval=-s_in, maxval=s_in, dtype=jnp.float32)
        W2 = jax.random.uniform(ks[5], (NUM_EXPERTS, D_FF, D_MODEL), minval=-s_ff, maxval=s_ff, dtype=jnp.float32)
        b2 = jax.random.uniform(ks[6], (NUM_EXPERTS, D_MODEL), minval=-s_ff, maxval=s_ff, dtype=jnp.float32)
        return {'x': x, 'Wg': Wg, 'bg': bg, 'W1': W1, 'b1': b1, 'W2': W2, 'b2': b2}
    _L2_ffn_all = _L2_ffn_setup()
    _L2_ffn_in = {k: v for k, v in _L2_ffn_all.items() if k in ('Wg', 'bg', 'W1', 'b1', 'W2', 'b2')}
    del _L2_ffn_all

    def _L3_xattn_setup():
        import jax, jax.numpy as jnp
        import numpy as np
        D_MODEL = 128
        B, T = (4, 256)
        NEG = -1000000000.0
        key = jax.random.key(seed)
        kq, kk, kv = jax.random.split(key, 3)
        query = jax.random.normal(kq, (B, T, D_MODEL), dtype=jnp.float32)
        k = jax.random.normal(kk, (B, T, D_MODEL), dtype=jnp.float32)
        value = jax.random.normal(kv, (B, T, D_MODEL), dtype=jnp.float32)
        mask = jnp.triu(jnp.ones((T, T), dtype=jnp.float32), k=1)
        return {'query': query, 'key': k, 'value': value, 'mask': mask}
    _L3_xattn_all = _L3_xattn_setup()
    _L3_xattn_in = {k: v for k, v in _L3_xattn_all.items() if k in ()}
    del _L3_xattn_all

    def _L3_ffn_setup():
        import jax, jax.numpy as jnp
        import numpy as np
        DIM, HEADS, EXPERTS, DFF = (128, 16, 8, 512)
        EPS = 1e-05

        def layernorm(x, g, b):
            mu = jnp.mean(x, -1, keepdims=True)
            var = jnp.mean(jnp.square(x - mu), -1, keepdims=True)
            return (x - mu) * jax.lax.rsqrt(var + EPS) * g + b
        key = jax.random.key(seed)
        ks = jax.random.split(key, 12)
        s = lambda d: 1.0 / np.sqrt(d)
        return {'x': jax.random.normal(ks[0], (2, 256, DIM), jnp.float32), 'conv_w': jax.random.normal(ks[1], (DIM, DIM, 3), jnp.float32) * s(DIM * 3), 'conv_b': jnp.zeros((DIM,), jnp.float32), 'wqkv': jax.random.normal(ks[2], (3 * DIM, DIM), jnp.float32) * s(DIM), 'bqkv': jnp.zeros((3 * DIM,), jnp.float32), 'wo': jax.random.normal(ks[3], (DIM, DIM), jnp.float32) * s(DIM), 'bo': jnp.zeros((DIM,), jnp.float32), 'ln1_g': jnp.ones((DIM,), jnp.float32), 'ln1_b': jnp.zeros((DIM,), jnp.float32), 'gate_w': jax.random.normal(ks[4], (DIM, EXPERTS), jnp.float32) * s(DIM), 'gate_b': jnp.zeros((EXPERTS,), jnp.float32), 'w1': jax.random.normal(ks[5], (EXPERTS, DIM, DFF), jnp.float32) * s(DIM), 'b1': jnp.zeros((EXPERTS, DFF), jnp.float32), 'w2': jax.random.normal(ks[6], (EXPERTS, DFF, DIM), jnp.float32) * s(DFF), 'b2': jnp.zeros((EXPERTS, DIM), jnp.float32), 'ln2_g': jnp.ones((DIM,), jnp.float32), 'ln2_b': jnp.zeros((DIM,), jnp.float32)}
    _L3_ffn_all = _L3_ffn_setup()
    _L3_ffn_in = {k: v for k, v in _L3_ffn_all.items() if k in ('conv_w', 'conv_b', 'wqkv', 'bqkv', 'wo', 'bo', 'ln1_g', 'ln1_b', 'gate_w', 'gate_b', 'w1', 'b1', 'w2', 'b2', 'ln2_g', 'ln2_b')}
    del _L3_ffn_all
    return {'x': x, 'ctx_1024': ctx_1024, 'itok_BxS_0_7': itok_BxS_0_7, 'itok_BxS_0_4092': itok_BxS_0_4092, 'mask_SxS2_bk1': mask_SxS2_bk1, 'mask_BxS2_bf0': mask_BxS2_bf0, 'mask_SxS2_fk1': mask_SxS2_fk1, 'L0_xattn_Wq': _L0_xattn_in['Wq'], 'L0_xattn_bq': _L0_xattn_in['bq'], 'L0_xattn_Wk': _L0_xattn_in['Wk'], 'L0_xattn_bk': _L0_xattn_in['bk'], 'L0_xattn_Wv': _L0_xattn_in['Wv'], 'L0_xattn_bv': _L0_xattn_in['bv'], 'L0_xattn_Wo': _L0_xattn_in['Wo'], 'L0_xattn_bo': _L0_xattn_in['bo'], 'L0_ffn_gate_w': _L0_ffn_in['gate_w'], 'L0_ffn_Wg': _L0_ffn_in['Wg'], 'L0_ffn_Wu': _L0_ffn_in['Wu'], 'L0_ffn_Wd': _L0_ffn_in['Wd'], 'L1_xattn_Wqj': _L1_xattn_in['Wqj'], 'L1_xattn_Wkj': _L1_xattn_in['Wkj'], 'L1_xattn_Wvj': _L1_xattn_in['Wvj'], 'L1_xattn_Wqi': _L1_xattn_in['Wqi'], 'L1_xattn_Wki': _L1_xattn_in['Wki'], 'L1_xattn_Wvi': _L1_xattn_in['Wvi'], 'L1_xattn_Wout': _L1_xattn_in['Wout'], 'L1_xattn_gain': _L1_xattn_in['gain'], 'L1_xattn_council_weights': _L1_xattn_in['council_weights'], 'L1_ffn_Wqkv': _L1_ffn_in['Wqkv'], 'L1_ffn_q_scale': _L1_ffn_in['q_scale'], 'L1_ffn_k_scale': _L1_ffn_in['k_scale'], 'L1_ffn_Wo': _L1_ffn_in['Wo'], 'L1_ffn_ln_g': _L1_ffn_in['ln_g'], 'L1_ffn_ln_b': _L1_ffn_in['ln_b'], 'L1_ffn_W1': _L1_ffn_in['W1'], 'L1_ffn_b1': _L1_ffn_in['b1'], 'L1_ffn_W2': _L1_ffn_in['W2'], 'L1_ffn_b2': _L1_ffn_in['b2'], 'L2_xattn_Wk': _L2_xattn_in['Wk'], 'L2_xattn_Wv': _L2_xattn_in['Wv'], 'L2_xattn_bv': _L2_xattn_in['bv'], 'L2_xattn_Wq': _L2_xattn_in['Wq'], 'L2_xattn_bq': _L2_xattn_in['bq'], 'L2_xattn_Wo': _L2_xattn_in['Wo'], 'L2_xattn_bo': _L2_xattn_in['bo'], 'L2_ffn_Wg': _L2_ffn_in['Wg'], 'L2_ffn_bg': _L2_ffn_in['bg'], 'L2_ffn_W1': _L2_ffn_in['W1'], 'L2_ffn_b1': _L2_ffn_in['b1'], 'L2_ffn_W2': _L2_ffn_in['W2'], 'L2_ffn_b2': _L2_ffn_in['b2'], 'L3_ffn_conv_w': _L3_ffn_in['conv_w'], 'L3_ffn_conv_b': _L3_ffn_in['conv_b'], 'L3_ffn_wqkv': _L3_ffn_in['wqkv'], 'L3_ffn_bqkv': _L3_ffn_in['bqkv'], 'L3_ffn_wo': _L3_ffn_in['wo'], 'L3_ffn_bo': _L3_ffn_in['bo'], 'L3_ffn_ln1_g': _L3_ffn_in['ln1_g'], 'L3_ffn_ln1_b': _L3_ffn_in['ln1_b'], 'L3_ffn_gate_w': _L3_ffn_in['gate_w'], 'L3_ffn_gate_b': _L3_ffn_in['gate_b'], 'L3_ffn_w1': _L3_ffn_in['w1'], 'L3_ffn_b1': _L3_ffn_in['b1'], 'L3_ffn_w2': _L3_ffn_in['w2'], 'L3_ffn_b2': _L3_ffn_in['b2'], 'L3_ffn_ln2_g': _L3_ffn_in['ln2_g'], 'L3_ffn_ln2_b': _L3_ffn_in['ln2_b']}

def reference(x, ctx_1024, itok_BxS_0_7, itok_BxS_0_4092, mask_SxS2_bk1, mask_BxS2_bf0, mask_SxS2_fk1, L0_xattn_Wq, L0_xattn_bq, L0_xattn_Wk, L0_xattn_bk, L0_xattn_Wv, L0_xattn_bv, L0_xattn_Wo, L0_xattn_bo, L0_ffn_gate_w, L0_ffn_Wg, L0_ffn_Wu, L0_ffn_Wd, L1_xattn_Wqj, L1_xattn_Wkj, L1_xattn_Wvj, L1_xattn_Wqi, L1_xattn_Wki, L1_xattn_Wvi, L1_xattn_Wout, L1_xattn_gain, L1_xattn_council_weights, L1_ffn_Wqkv, L1_ffn_q_scale, L1_ffn_k_scale, L1_ffn_Wo, L1_ffn_ln_g, L1_ffn_ln_b, L1_ffn_W1, L1_ffn_b1, L1_ffn_W2, L1_ffn_b2, L2_xattn_Wk, L2_xattn_Wv, L2_xattn_bv, L2_xattn_Wq, L2_xattn_bq, L2_xattn_Wo, L2_xattn_bo, L2_ffn_Wg, L2_ffn_bg, L2_ffn_W1, L2_ffn_b1, L2_ffn_W2, L2_ffn_b2, L3_ffn_conv_w, L3_ffn_conv_b, L3_ffn_wqkv, L3_ffn_bqkv, L3_ffn_wo, L3_ffn_bo, L3_ffn_ln1_g, L3_ffn_ln1_b, L3_ffn_gate_w, L3_ffn_gate_b, L3_ffn_w1, L3_ffn_b1, L3_ffn_w2, L3_ffn_b2, L3_ffn_ln2_g, L3_ffn_ln2_b):
    import jax
    import jax.numpy as jnp

    def _L0_xattn_ref(query, key, value, Wq, bq, Wk, bk, Wv, bv, Wo, bo, attn_mask, key_padding_mask):
        import jax, jax.numpy as jnp
        import numpy as np
        B, T, D, H = (2, 256, 128, 16)
        DK = D // H
        SCALE = 1.0 / float(np.sqrt(DK))
        Bq, Tq, _ = query.shape
        Tk = key.shape[1]
        q = (query @ Wq.T + bq).reshape(Bq, Tq, H, DK)
        k = (key @ Wk.T + bk).reshape(Bq, Tk, H, DK)
        v = (value @ Wv.T + bv).reshape(Bq, Tk, H, DK)
        scores = jnp.einsum('bqhd,bkhd->bhqk', q, k) * jnp.float32(SCALE)
        neg_inf = jnp.float32(-jnp.inf)
        scores = jnp.where(attn_mask[None, None, :, :], neg_inf, scores)
        scores = jnp.where(key_padding_mask[:, None, None, :], neg_inf, scores)
        attn = jax.nn.softmax(scores, axis=-1)
        out = jnp.einsum('bhqk,bkhd->bqhd', attn, v).reshape(Bq, Tq, D)
        return out @ Wo.T + bo

    def _L0_ffn_ref(x, gate_w, Wg, Wu, Wd):
        import jax, jax.numpy as jnp
        import numpy as np
        B, S, D = (4, 512, 128)
        E, I = (8, 256)
        CAPACITY = 2
        K = max(1, int(S / E * CAPACITY))
        logits = jnp.einsum('bsd,de->bse', x, gate_w)
        affinity = jax.nn.softmax(logits, axis=-1)
        affinity_T = jnp.transpose(affinity, (0, 2, 1))
        gating, index = jax.lax.top_k(affinity_T, K)
        b_idx = jnp.arange(x.shape[0])[:, None, None]
        x_sel = x[b_idx, index]
        g = jnp.einsum('bekd,edi->beki', x_sel, Wg)
        u = jnp.einsum('bekd,edi->beki', x_sel, Wu)
        h = jax.nn.silu(g) * u
        out = jnp.einsum('beki,eid->bekd', h, Wd)
        contrib = out * gating[..., None]
        x_out = jnp.zeros_like(x).at[b_idx, index].add(contrib)
        return x_out

    def _L1_xattn_ref(hidden_states, advisor_states, advisor_ids, pointer_ids, Wqj, Wkj, Wvj, Wqi, Wki, Wvi, Wout, gain, council_weights):
        import math
        import jax, jax.numpy as jnp
        import numpy as np
        B, T, L, H = (4, 512, 512, 128)

        def _forward(hidden_states, advisor_states, advisor_ids, pointer_ids, Wqj, Wkj, Wvj, Wqi, Wki, Wvi, Wout, gain, council_weights):
            b, t, h = hidden_states.shape
            l = advisor_states.shape[1]
            inv_sqrt_h = 1.0 / math.sqrt(float(h))
            p = pointer_ids[:, :, None]
            indices = jnp.clip(jnp.concatenate([p, p + 1, p + 2], axis=-1), 0, l - 1)
            win_states = jax.vmap(lambda a, idx: a[idx])(advisor_states, indices)
            win_ids = jax.vmap(lambda a, idx: a[idx])(advisor_ids, indices)
            qj = hidden_states @ Wqj.T
            kj = win_states @ Wkj.T
            vj = win_states @ Wvj.T
            sj = jnp.einsum('bth,btwh->btw', qj, kj) * inv_sqrt_h
            l_rel, l_v1, l_v2 = (sj[:, :, 0], sj[:, :, 1], sj[:, :, 2])
            rel_ids = win_ids[:, :, 0]
            is_and = (rel_ids == 0).astype(sj.dtype)
            is_or = (rel_ids == 1).astype(sj.dtype)
            is_not = (rel_ids == 2).astype(sj.dtype)
            is_implies = (rel_ids == 3).astype(sj.dtype)
            is_xor = (rel_ids == 4).astype(sj.dtype)
            l_new = is_and * (l_v1 + l_v2) + is_or * jnp.maximum(l_v1, l_v2) + is_not * -l_v1 + is_implies * jnp.maximum(-l_v1, l_v2) + is_xor * jnp.abs(l_v1 - l_v2)
            mask_any = jnp.clip(is_and + is_or + is_not + is_implies + is_xor, 0.0, 1.0)
            l_final = mask_any * l_new + (1.0 - mask_any) * l_rel
            sj = jnp.stack([l_final, l_v1, l_v2], axis=-1)
            aj = jax.nn.softmax(sj, axis=-1)
            cj = jnp.einsum('btw,btwh->bth', aj, vj)
            qi = hidden_states @ Wqi.T
            ki = win_states @ Wki.T
            vi = win_states @ Wvi.T
            si = jnp.einsum('bth,btwh->btw', qi, ki) * inv_sqrt_h
            ai = jax.nn.softmax(si, axis=-1)
            ci = jnp.einsum('btw,btwh->bth', ai, vi)
            w = jax.nn.softmax(council_weights, axis=0)
            context = w[0] * cj + w[1] * ci
            return context @ Wout.T * gain
        return _forward(hidden_states, advisor_states, advisor_ids, pointer_ids, Wqj, Wkj, Wvj, Wqi, Wki, Wvi, Wout, gain, council_weights)

    def _L1_ffn_ref(x, Wqkv, q_scale, k_scale, Wo, ln_g, ln_b, W1, b1, W2, b2):
        import jax, jax.numpy as jnp
        import numpy as np
        DIM = 128
        DEPTH = 6
        HEADS = 16
        DIM_HEAD = 64
        WINDOW = 32
        INNER = HEADS * DIM_HEAD
        DIM_INNER = int(DIM * 4 * 2 / 3)
        QK_SCALE = 8.0

        def shift_tokens(t):
            a, s = jnp.split(t, 2, -1)
            s = jnp.pad(s, ((0, 0), (1, 0), (0, 0)))[:, :-1]
            return jnp.concatenate([a, s], -1)

        def l2norm(t):
            return t / jnp.maximum(jnp.linalg.norm(t, axis=-1, keepdims=True), 1e-12)

        def rotate_half(x):
            x1, x2 = jnp.split(x, 2, -1)
            return jnp.concatenate([-x2, x1], -1)

        def rotary_tables(n):
            half = jnp.arange(0, DIM_HEAD, 2, dtype=jnp.float32)
            inv_freq = 1.0 / 10000.0 ** (half / DIM_HEAD)
            t = jnp.arange(n, dtype=jnp.float32)
            freqs = t[:, None] * inv_freq[None, :]
            freqs = jnp.concatenate([freqs, freqs], -1)
            base_scale = (half + 0.4 * DIM_HEAD) / (1.4 * DIM_HEAD)
            power = (t - n // 2) / (WINDOW // 2)
            scale = base_scale[None, :] ** power[:, None]
            scale = jnp.concatenate([scale, scale], -1)
            return (freqs, scale)

        def local_attention(q, k, v):
            b, h, n, d = q.shape
            w = WINDOW
            nw = n // w
            bq = q.reshape(b, h, nw, w, d)
            bk = k.reshape(b, h, nw, w, d)
            bv = v.reshape(b, h, nw, w, d)

            def look(t):
                p = jnp.pad(t, ((0, 0), (0, 0), (1, 0), (0, 0), (0, 0)))
                return jnp.concatenate([p[:, :, :nw], p[:, :, 1:]], axis=3)
            bk2, bv2 = (look(bk), look(bv))
            seq = jnp.arange(n).reshape(nw, w)
            seq_p = jnp.pad(seq, ((1, 0), (0, 0)), constant_values=-1)
            jt = jnp.concatenate([seq_p[:nw], seq_p[1:]], axis=1)
            it = seq[:, :, None]
            jb = jt[:, None, :]
            mask = (it < jb) | (it > jb + w) | (jb == -1)
            sim = jnp.einsum('bhwie,bhwje->bhwij', bq, bk2) * QK_SCALE
            sim = jnp.where(mask, -jnp.finfo(sim.dtype).max, sim)
            attn = jax.nn.softmax(sim, -1)
            out = jnp.einsum('bhwij,bhwje->bhwie', attn, bv2)
            return out.reshape(b, h, n, d)

        def attn_layer(x, Wqkv, qs, ksc, Wo):
            b, n, _ = x.shape
            qkv = x @ Wqkv
            q, k, v = jnp.split(qkv, 3, -1)
            sh = lambda t: t.reshape(b, n, HEADS, DIM_HEAD).transpose(0, 2, 1, 3)
            q, k, v = (sh(q), sh(k), sh(v))
            q = l2norm(q) * qs
            k = l2norm(k) * ksc
            freqs, scale = rotary_tables(n)
            cos, sin = (jnp.cos(freqs), jnp.sin(freqs))
            q = q * cos * scale + rotate_half(q) * sin * scale
            inv = 1.0 / scale
            k = k * cos * inv + rotate_half(k) * sin * inv
            out = local_attention(q, k, v)
            out = out.transpose(0, 2, 1, 3).reshape(b, n, INNER)
            return out @ Wo

        def ffn_layer(x, g, bln, W1, b1, W2, b2):
            mu = x.mean(-1, keepdims=True)
            var = ((x - mu) ** 2).mean(-1, keepdims=True)
            xn = (x - mu) / jnp.sqrt(var + 1e-05) * g + bln
            hg = xn @ W1 + b1
            a, gate = jnp.split(hg, 2, -1)
            return a * jax.nn.gelu(gate, approximate=False) @ W2 + b2
        for i in range(DEPTH):
            x = attn_layer(shift_tokens(x), Wqkv[i], q_scale[i], k_scale[i], Wo[i]) + x
            x = ffn_layer(shift_tokens(x), ln_g[i], ln_b[i], W1[i], b1[i], W2[i], b2[i]) + x
        return x

    def _L2_xattn_ref(k, v, q, Wk, Wv, bv, Wq, bq, Wo, bo):
        import jax, jax.numpy as jnp
        import numpy as np
        D_MODEL = 128
        B, S = (4, 256)
        kp = jnp.einsum('bsd,ed->bse', k, Wk)
        vp = jnp.einsum('bsd,ed->bse', v, Wv) + bv
        qp = jnp.einsum('bsd,ed->bse', q, Wq) + bq
        scale = 1.0 / jnp.sqrt(jnp.float32(kp.shape[-1]))
        scores = jnp.einsum('bqd,bkd->bqk', qp, kp) * scale
        probs = jax.nn.softmax(scores, axis=-1)
        ctx = jnp.einsum('bqk,bkd->bqd', probs, vp)
        return jnp.einsum('bqd,ed->bqe', ctx, Wo) + bo

    def _L2_ffn_ref(x, Wg, bg, W1, b1, W2, b2):
        import jax, jax.numpy as jnp
        import numpy as np
        D_MODEL = 128
        D_FF = 512
        NUM_EXPERTS = 8
        TOP_K = 2
        gate_logits = jnp.einsum('bsd,de->bse', x, Wg) + bg
        gate_probs = jax.nn.softmax(gate_logits, axis=-1)
        topk_probs, topk_idx = jax.lax.top_k(gate_probs, TOP_K)
        topk_probs = topk_probs / jnp.sum(topk_probs, axis=-1, keepdims=True)
        onehot = jax.nn.one_hot(topk_idx, NUM_EXPERTS, dtype=x.dtype)
        weights = jnp.einsum('bske,bsk->bse', onehot, topk_probs)
        h = jnp.einsum('bsd,edf->bsef', x, W1) + b1
        h = jax.nn.gelu(h, approximate=False)
        y = jnp.einsum('bsef,efd->bsed', h, W2) + b2
        return jnp.einsum('bsed,bse->bsd', y, weights)

    def _L3_xattn_ref(query, key, value, mask):
        import jax, jax.numpy as jnp
        import numpy as np
        D_MODEL = 128
        B, T = (4, 256)
        NEG = -1000000000.0
        dk = jnp.sqrt(jnp.float32(1.0) / jnp.float32(D_MODEL))
        attn_logits = jnp.einsum('btc,bsc->bts', query, key) / dk
        attn_logits = attn_logits + mask * NEG
        score = jax.nn.softmax(attn_logits, axis=-1)
        attention = jnp.einsum('bts,bsc->btc', score, value)
        return attention

    def _L3_ffn_ref(x, conv_w, conv_b, wqkv, bqkv, wo, bo, ln1_g, ln1_b, gate_w, gate_b, w1, b1, w2, b2, ln2_g, ln2_b):
        import jax, jax.numpy as jnp
        import numpy as np
        DIM, HEADS, EXPERTS, DFF = (128, 16, 8, 512)
        EPS = 1e-05

        def layernorm(x, g, b):
            mu = jnp.mean(x, -1, keepdims=True)
            var = jnp.mean(jnp.square(x - mu), -1, keepdims=True)
            return (x - mu) * jax.lax.rsqrt(var + EPS) * g + b
        B, S, D = x.shape
        H, dh = (HEADS, D // HEADS)
        xt = jnp.transpose(x, (0, 2, 1))
        xt = jax.lax.conv_general_dilated(xt, conv_w, (1,), [(1, 1)], dimension_numbers=('NCH', 'OIH', 'NCH'))
        x = jnp.transpose(xt + conv_b[None, :, None], (0, 2, 1))
        qkv = x @ wqkv.T + bqkv
        q, k, v = jnp.split(qkv, 3, axis=-1)
        q = q.reshape(B, S, H, dh).transpose(0, 2, 1, 3)
        k = k.reshape(B, S, H, dh).transpose(0, 2, 1, 3)
        v = v.reshape(B, S, H, dh).transpose(0, 2, 1, 3)
        scores = jnp.einsum('bhqd,bhkd->bhqk', q, k) / jnp.sqrt(jnp.float32(dh))
        attn = jax.nn.softmax(scores, axis=-1)
        ctx = jnp.einsum('bhqk,bhkd->bhqd', attn, v)
        ctx = ctx.transpose(0, 2, 1, 3).reshape(B, S, D)
        attn_out = ctx @ wo.T + bo
        x = layernorm(x + attn_out, ln1_g, ln1_b)
        probs = jax.nn.softmax(x @ gate_w + gate_b, axis=-1)
        h = jax.nn.relu(jnp.einsum('bsd,edf->bsef', x, w1) + b1)
        y = jnp.einsum('bsef,efd->bsed', h, w2) + b2
        moe_out = jnp.einsum('bse,bsed->bsd', probs, y)
        x = layernorm(x + moe_out, ln2_g, ln2_b)
        return x
    x = x + _L0_xattn_ref(_layernorm(x, axis=-1), ctx_1024, ctx_1024, L0_xattn_Wq, L0_xattn_bq, L0_xattn_Wk, L0_xattn_bk, L0_xattn_Wv, L0_xattn_bv, L0_xattn_Wo, L0_xattn_bo, mask_SxS2_bk1, mask_BxS2_bf0)
    x = x + _L0_ffn_ref(_layernorm(x, axis=-1), L0_ffn_gate_w, L0_ffn_Wg, L0_ffn_Wu, L0_ffn_Wd)
    x = x + _L1_xattn_ref(_layernorm(x, axis=-1), ctx_1024, itok_BxS_0_7, itok_BxS_0_4092, L1_xattn_Wqj, L1_xattn_Wkj, L1_xattn_Wvj, L1_xattn_Wqi, L1_xattn_Wki, L1_xattn_Wvi, L1_xattn_Wout, L1_xattn_gain, L1_xattn_council_weights)
    x = x + _L1_ffn_ref(_layernorm(x, axis=-1), L1_ffn_Wqkv, L1_ffn_q_scale, L1_ffn_k_scale, L1_ffn_Wo, L1_ffn_ln_g, L1_ffn_ln_b, L1_ffn_W1, L1_ffn_b1, L1_ffn_W2, L1_ffn_b2)
    x = x + _L2_xattn_ref(ctx_1024, ctx_1024, _layernorm(x, axis=-1), L2_xattn_Wk, L2_xattn_Wv, L2_xattn_bv, L2_xattn_Wq, L2_xattn_bq, L2_xattn_Wo, L2_xattn_bo)
    x = x + _L2_ffn_ref(_layernorm(x, axis=-1), L2_ffn_Wg, L2_ffn_bg, L2_ffn_W1, L2_ffn_b1, L2_ffn_W2, L2_ffn_b2)
    x = x + _L3_xattn_ref(_layernorm(x, axis=-1), ctx_1024, ctx_1024, mask_SxS2_fk1)
    x = x + _L3_ffn_ref(_layernorm(x, axis=-1), L3_ffn_conv_w, L3_ffn_conv_b, L3_ffn_wqkv, L3_ffn_bqkv, L3_ffn_wo, L3_ffn_bo, L3_ffn_ln1_g, L3_ffn_ln1_b, L3_ffn_gate_w, L3_ffn_gate_b, L3_ffn_w1, L3_ffn_b1, L3_ffn_w2, L3_ffn_b2, L3_ffn_ln2_g, L3_ffn_ln2_b)
    return x

_drawn_inputs = setup_inputs


def setup_inputs(seed=0):
    import zlib

    import numpy as np

    out = dict(_drawn_inputs(seed))
    spreads = {'L0_xattn_bq': (0.0, 0.8),
     'L0_xattn_bk': (0.0, 2.0),
     'L0_xattn_bv': (0.0, 0.1),
     'L0_xattn_bo': (0.0, 0.1),
     'L1_xattn_council_weights': (1.0, 0.6),
     'L1_ffn_q_scale': (1.0, 0.6),
     'L1_ffn_k_scale': (1.0, 0.6),
     'L1_ffn_ln_g': (1.0, 0.6),
     'L1_ffn_ln_b': (0.0, 0.8),
     'L1_ffn_b1': (0.0, 0.504),
     'L1_ffn_b2': (0.0, 0.1),
     'L2_xattn_bv': (0.0, 0.1),
     'L2_xattn_bq': (0.0, 0.579),
     'L2_xattn_bo': (0.0, 0.1),
     'L3_ffn_conv_b': (0.0, 0.1),
     'L3_ffn_bqkv': (0.0, 0.272),
     'L3_ffn_bo': (0.0, 0.1),
     'L3_ffn_ln1_g': (1.0, 0.2),
     'L3_ffn_ln1_b': (0.0, 0.1),
     'L3_ffn_gate_b': (0.0, 0.781),
     'L3_ffn_b1': (0.0, 0.645),
     'L3_ffn_b2': (0.0, 0.45),
     'L3_ffn_ln2_g': (1.0, 0.2),
     'L3_ffn_ln2_b': (0.0, 0.274)}
    factors = {'L0_xattn_Wq': 8.0,
     'L0_xattn_Wk': 8.0,
     'L0_ffn_gate_w': 8.0,
     'L0_ffn_Wg': 8.0,
     'L0_ffn_Wu': 8.0,
     'L0_ffn_Wd': 8.0,
     'L1_xattn_Wqj': 64.0,
     'L1_xattn_Wkj': 64.0,
     'L1_xattn_Wqi': 64.0,
     'L1_xattn_Wki': 64.0,
     'L2_ffn_b1': 5.283,
     'L1_xattn_Wvi': 3.439,
     'L2_ffn_bg': 4.166,
     'L2_ffn_b2': 4.82}
    for name, (base, spread) in spreads.items():
        noise = np.random.default_rng([zlib.crc32(name.encode()), seed]).standard_normal(out[name].shape)
        drawn = base * np.exp(spread * noise) if base else spread * noise
        out[name] = jnp.asarray(drawn.astype(out[name].dtype))
    for name, factor in factors.items():
        out[name] = (out[name] * factor).astype(out[name].dtype)
    return out
```

```python
from contextlib import ExitStack

import concourse.bass as bass
from concourse import mybir

F32 = mybir.dt.float32
BF16 = mybir.dt.bfloat16
I32 = mybir.dt.int32
U8 = mybir.dt.uint8
ALU = mybir.AluOpType
ACT = mybir.ActivationFunctionType
AX = mybir.AxisListType.X


P = 128
B, T, S2 = 4, 512, 77
NT = T // P
H0, DK0 = 16, 8
NEG = -1.0e30
EPS = 1e-5


class Steps:

    def __init__(self, eng, sem):
        self.eng, self.sem, self.base, self.n = eng, sem, 0, 0

    def body(self, turn, per):
        self.base, self.n, self.per = turn * per, 0, per

    def done(self, ins):
        self.n += 1
        return ins.then_inc(self.sem, 1)

    def settle(self):
        self.eng.wait_ge(self.sem, self.base + self.n)

    def end(self):
        assert self.n == self.per, (self.sem, self.n, self.per)


def over(ap, n):
    return ap.rearrange("p (o k) -> p o k", o=1).to_broadcast([ap.shape[0], n, ap.shape[1]])


def along(ap, n):
    return ap.rearrange("p (h o) -> p h o", o=1).to_broadcast([ap.shape[0], ap.shape[1], n])


def build(nc, a, out):
    with ExitStack() as ctx:
        def sb(name, shape, dt=F32):
            return ctx.enter_context(nc.sbuf_tensor(name, shape, dt))

        def sem(name):
            return ctx.enter_context(nc.semaphore(name))

        PS = ctx.enter_context(nc.psum_tensor("PS", [P, 8, 512], F32))
        X = sb("X", [P, B, T])
        XN = sb("XN", [P, T + 2])
        xn = XN[:, 1:T + 1]
        LN_C = sb("LN_C", [P, T])
        LN_Q = sb("LN_Q", [P, T])
        LN_S = sb("LN_S", [P, NT])
        LN_R = sb("LN_R", [P, NT])
        EPSC = sb("EPSC", [P, 1])
        AVG = sb("AVG", [P, P])
        IDF = sb("IDF", [P, P])
        IDB = sb("IDB", [P, P], BF16)
        CT = sb("CT", [P, B, S2])
        HMASK = sb("HMASK", [P, H0])
        ARENA_COLS = 27 * 1024
        ARENA = sb("ARENA", [P, ARENA_COLS])

        def carver():
            at = [0]

            def carve(cols, dt=F32):
                n = cols if dt == F32 else (cols + 1) // 2
                v = ARENA[:, at[0]:at[0] + n]
                at[0] += n
                assert at[0] <= ARENA_COLS, at[0]
                return v if dt == F32 else v.bitcast(dt)
            return carve

        x_loaded, const_loaded, out_stored = sem("x_loaded"), sem("const_loaded"), sem("out_stored")
        x_done = sem("x_done")
        pool_const = sem("pool_const")
        ln_mean, ln_cen, ln_sq, ln_var, ln_sd, ln_rs, ln_bc, ln_out = [sem(n) for n in (
            "ln_mean", "ln_cen", "ln_sq", "ln_var", "ln_sd", "ln_rs", "ln_bc", "ln_out")]

        def ln_tensor(pe, k, src):
            pe.wait_ge(ln_out, k + 1)
            pe.matmul(PS[:, 6, :], AVG[:, :], src, start=True, stop=True).then_inc(ln_mean, 1)
            pe.wait_ge(ln_sq, k + 1)
            for t in range(NT):
                mm = pe.matmul(PS[:, 7, t:t + 1], LN_Q[:, t * P:(t + 1) * P], AVG[:, 0:1], start=True, stop=True)
            mm.then_inc(ln_var, 1)
            pe.wait_ge(ln_rs, k + 1)
            for t in range(NT):
                mm = pe.matmul(PS[:, 6, t * P:(t + 1) * P], LN_R[:, t:t + 1].to_broadcast([P, P]), IDF[:, :],
                               start=True, stop=True)
            mm.then_inc(ln_bc, 1)

        def ln_scalar(act, k):
            act.wait_ge(ln_cen, k + 1)
            act.activation(LN_Q[:, :], LN_C[:, :], ACT.Square).then_inc(ln_sq, 1)
            act.wait_ge(ln_var, k + 1)
            act.activation(LN_S[:, :], PS[:, 7, 0:NT], ACT.Sqrt, bias=EPSC[:, 0:1]).then_inc(ln_sd, 1)

        def ln_vector(dve, k, src, dst):
            dve.wait_ge(ln_mean, k + 1)
            dve.tensor_tensor(LN_C[:, :], src, PS[:, 6, :], ALU.subtract).then_inc(ln_cen, 1)
            dve.wait_ge(ln_sd, k + 1)
            dve.reciprocal(LN_R[:, :], LN_S[:, :]).then_inc(ln_rs, 1)
            dve.wait_ge(ln_bc, k + 1)
            dve.tensor_tensor(dst, LN_C[:, :], PS[:, 6, :], ALU.mult).then_inc(ln_out, 1)

        L0W = sb("L0W", [P, 4, P])
        L0B = sb("L0B", [P, 3])
        BVROW = sb("BVROW", [1, P])
        ONEROW = sb("ONEROW", [1, P])
        MSK_Q = sb("MSK_Q", [P, NT, S2], U8)
        MSK_T = sb("MSK_T", [S2, T], U8)
        PAD_Q = sb("PAD_Q", [P, B, S2], U8)
        PAD_T = sb("PAD_T", [S2, B], U8)
        l0_loaded = sem("l0_loaded")
        c = carver()
        XM_Q = c(T)
        XM_K = c(S2)
        XM_C = c(S2)
        XM_KB = c(H0 * S2).rearrange("p (h k) -> p h k", h=H0)
        VSTEP = P + DK0
        XM_VB = c(H0 * VSTEP)
        XM_MQ32 = c(NT * S2).rearrange("p (t k) -> p t k", t=NT)
        XM_MQ = c(NT * S2, BF16).rearrange("p (t k) -> p t k", t=NT)
        XM_MT32 = c(T)
        XM_MT = c(T, BF16)
        XM_PADQ = c(B * S2).rearrange("p (b k) -> p b k", b=B)
        XM_PADT = c(B)
        XM_NM = c(NT * H0).rearrange("p (t h) -> p t h", t=NT)
        XM_NMT = c(T)
        XM_P = [c(T), c(T)]
        XM_RC = c(T)
        XM_CX = c(T)
        HG = [(0, 6), (6, 12), (12, 16)]
        l0_ctx, l0_proj, l0_q, l0_k, l0_v, l0_mask, l0_kb = [sem(n) for n in (
            "l0_ctx", "l0_proj", "l0_q", "l0_k", "l0_v", "l0_mask", "l0_kb")]
        l0_score, l0_max, l0_turn, l0_nmt, l0_st, l0_exp, l0_pv, l0_cx, l0_wo = [sem(n) for n in (
            "l0_score", "l0_max", "l0_turn", "l0_nmt", "l0_st", "l0_exp", "l0_pv", "l0_cx", "l0_wo")]
        l0_vec, l0_masks_vec = sem("l0_vec"), sem("l0_masks_vec")

        def l0x_tensor(pe):
            pe.wait_ge(l0_loaded, 16 * 8)
            with pe.Fori(0, B) as b:
                ln_tensor(pe, b, X[:, b, :])
                pe.wait_ge(l0_ctx, b + 1)
                pe.matmul(PS[:, 3, 0:S2], L0W[:, 1, :], XM_C, start=True, stop=True).then_inc(l0_proj, 1)
                pe.matmul(PS[0:S2, 4, 0:P], XM_C, L0W[:, 2, :], start=True, stop=False)
                pe.matmul(PS[0:S2, 4, 0:P], ONEROW[0:1, 0:S2], BVROW[:, :], start=False, stop=True).then_inc(l0_proj, 1)
                pe.wait_ge(ln_out, b + 2)
                pe.matmul(PS[:, 5, :], L0W[:, 0, :], xn, start=True, stop=True).then_inc(l0_proj, 1)
                pe.wait_ge(l0_q, b + 1)
                pe.wait_ge(l0_kb, b + 1)
                pe.wait_ge(l0_mask, 2 * b + 2)
                for t in range(NT):
                    if t:
                        pe.wait_ge(l0_max, b * NT + t)
                    for g, (h0, h1) in enumerate(HG):
                        o = PS[:, g, 0:(h1 - h0) * S2]
                        pe.matmul(o, XM_Q[:, t * P:(t + 1) * P], XM_KB[:, h0:h1, :], start=True, stop=False)
                        mm = pe.matmul(o, IDB[:, :], over(XM_MQ[:, t, :], h1 - h0),
                                       start=False, stop=True)
                    mm.then_inc(l0_score, 1)
                pe.wait_ge(l0_max, b * NT + NT)
                for t in range(NT):
                    mm = pe.transpose(PS[0:H0, 5, t * P:(t + 1) * P], XM_NM[:, t, :], IDF[:, :])
                mm.then_inc(l0_turn, 1)
                pe.wait_ge(l0_nmt, b + 1)
                pe.wait_ge(l0_v, 2 * b + 2)
                for h in range(H0):
                    o = PS[0:S2, 3 + h % 2, :]
                    if h >= 2:
                        pe.wait_ge(l0_exp, b * H0 + h - 1)
                    pe.matmul(o, XM_KB[:, h, :], XM_Q, start=True, stop=False)
                    pe.matmul(o, IDB[0:S2, 0:S2], XM_MT[0:S2, :], start=False, stop=False)
                    pe.matmul(o, IDF[0:H0, h:h + 1].to_broadcast([H0, S2]), XM_NMT[0:H0, :], start=False, stop=True).then_inc(l0_st, 1)
                    if h >= 1:
                        l0x_pv(pe, b, h - 1)
                l0x_pv(pe, b, H0 - 1)
                pe.wait_ge(l0_cx, 2 * b + 2)
                pe.matmul(PS[:, 0, :], L0W[:, 3, :], XM_CX, start=True, stop=True).then_inc(l0_wo, 1)

        def l0x_pv(pe, b, h):
            pe.wait_ge(l0_exp, b * H0 + h + 1)
            pe.matmul(PS[:, 1 + h // 8, :], XM_VB[0:S2, h * P:(h + 1) * P], XM_P[h % 2][0:S2, :],
                      start=h % 8 == 0, stop=h % 8 == 7).then_inc(l0_pv, 1)

        def l0x_scalar(act):
            with act.Fori(0, B) as b:
                ln_scalar(act, b)
                for h in range(H0):
                    act.wait_ge(l0_st, b * H0 + h + 1)
                    if h >= 2:
                        act.wait_ge(l0_pv, b * H0 + h - 1)
                    act.activation(XM_P[h % 2][0:S2, :], PS[0:S2, 3 + h % 2, :], ACT.Exp).then_inc(l0_exp, 1)

        def l0x_vector(dve):
            st = Steps(dve, l0_masks_vec)
            dve.wait_ge(l0_loaded, 16 * 8)
            st.body(0, 5)
            st.done(dve.tensor_scalar(XM_MQ32, MSK_Q[:, :, :], NEG, None, ALU.mult))
            st.done(dve.tensor_scalar(XM_MT32[0:S2, :], MSK_T[:, :], NEG, None, ALU.mult))
            st.done(dve.tensor_scalar(XM_PADQ, PAD_Q[:, :, :], NEG, None, ALU.mult))
            st.done(dve.tensor_scalar(XM_PADT[0:S2, :], PAD_T[:, :], NEG, None, ALU.mult))
            st.done(dve.memset(XM_VB, 0.0))
            st.settle()
            for h in range(H0):
                at = h * P + 64 + DK0 * (h % 8)
                dve.memset(XM_VB[:, at:at + DK0], 1.0)
            with dve.Fori(0, B) as b:
                st = Steps(dve, l0_vec)
                st.body(b, 2)
                ln_vector(dve, b, X[:, b, :], xn)
                dve.tensor_tensor(XM_MQ, XM_MQ32, over(XM_PADQ[:, b, :], NT), ALU.min).then_inc(l0_mask, 1)
                dve.tensor_scalar(XM_MT[0:S2, :], XM_MT32[0:S2, :], XM_PADT[0:S2, bass.ts(b, 1)], None, ALU.min).then_inc(l0_mask, 1)
                dve.wait_ge(l0_proj, 3 * b + 2)
                dve.tensor_scalar(XM_K, PS[:, 3, 0:S2], L0B[:, 1:2], None, ALU.add).then_inc(l0_k, 1)
                dve.wait_ge(l0_k, b + 1)
                dve.tensor_tensor(XM_KB, over(XM_K, H0),
                                  along(HMASK[:, :], S2),
                                  ALU.mult).then_inc(l0_kb, 1)
                for g in range(2):
                    vg = XM_VB[0:S2, g * 8 * P:g * 8 * P + 8 * VSTEP].rearrange("p (h e) -> p h e", e=VSTEP)[:, :, 0:DK0]
                    dve.tensor_copy(vg, PS[0:S2, 4, g * 64:(g + 1) * 64].rearrange("p (h e) -> p h e", e=DK0)).then_inc(l0_v, 1)
                dve.wait_ge(l0_proj, 3 * b + 3)
                dve.tensor_scalar(XM_Q, PS[:, 5, :], L0B[:, 0:1], DK0 ** -0.5, ALU.add, ALU.mult).then_inc(l0_q, 1)
                for t in range(NT):
                    dve.wait_ge(l0_score, b * NT + t + 1)
                    for g, (h0, h1) in enumerate(HG):
                        ins = dve.tensor_reduce(XM_NM[:, t, h0:h1],
                                                PS[:, g, 0:(h1 - h0) * S2].rearrange("p (h k) -> p h k", k=S2),
                                                AX, ALU.max, negate=True)
                    ins.then_inc(l0_max, 1)
                dve.wait_ge(l0_turn, b + 1)
                dve.tensor_copy(XM_NMT[0:H0, :], PS[0:H0, 5, :]).then_inc(l0_nmt, 1)
                for g in range(2):
                    dve.wait_ge(l0_pv, b * H0 + 8 * g + 8)
                    if g:
                        dve.wait_ge(l0_cx, 2 * b + g)
                    st.done(dve.reciprocal(XM_RC[0:64, :], PS[64:P, 1 + g, :]))
                    st.settle()
                    dve.tensor_tensor(XM_CX[64 * g:64 * g + 64, :], PS[0:64, 1 + g, :], XM_RC[0:64, :],
                                      ALU.mult).then_inc(l0_cx, 1)
                dve.wait_ge(l0_wo, b + 2)
                dve.scalar_tensor_tensor(out=X[:, b, :], in0=PS[:, 0, :], scalar=L0B[:, 2:3], in1=X[:, b, :],
                                         op0=ALU.add, op1=ALU.add).then_inc(x_done, 1)
                st.end()

        def l0x_pool(pool):
            pool.wait_ge(x_loaded, 16)
            pool.memset(XM_C, 0.0).then_inc(l0_wo, 1)
            with pool.Fori(0, B) as b:
                pool.wait_ge(l0_wo, b + 1)
                pool.tensor_copy(XM_C, CT[:, b, :]).then_inc(l0_ctx, 1)

        NE, CAP = 8, 128
        MOEW = sb("MOEW", [P, 8192])
        GW0 = sb("GW0", [P, NE])
        E_G = MOEW[:, 0:2048].rearrange("p (e c m) -> p e c m", e=NE, c=2)
        E_U = MOEW[:, 2048:4096].rearrange("p (e c m) -> p e c m", e=NE, c=2)
        E_D = MOEW[:, 4096:6144].rearrange("p (e c m) -> p e c m", e=NE, c=2)
        l0f_loaded = sem("l0f_loaded")
        c = carver()
        F_XA = c(B * T).rearrange("p (b n) -> p b n", b=B)
        F_E = c(NT * NE).rearrange("p (t e) -> p t e", t=NT)
        F_M = c(NT)
        F_S = c(NT)
        F_R = c(NT)
        F_AFF = c(NT * B * NE).rearrange("p (t j) -> p t j", t=NT)
        F_A = c(T)
        F_W = c(T)
        F_M8 = c(8)
        F_G = c(T)
        F_GB = c(B * T).rearrange("p (b n) -> p b n", b=B)
        F_GS = c(T)
        F_SG = [c(T), c(T)]
        F_T = [c(T), c(T)]
        F_H = [c(T), c(T)]
        f_logit, f_neg, f_sub, f_exp, f_sum, f_aff, f_xa, f_turn, f_gate, f_gb = [sem(n) for n in (
            "f_logit", "f_neg", "f_sub", "f_exp", "f_sum", "f_aff", "f_xa", "f_turn", "f_gate", "f_gb")]
        f_gs = sem("f_gs")
        f_bc, f_gu, f_silu, f_h, f_down, f_vec, f_topk = [sem(n) for n in (
            "f_bc", "f_gu", "f_silu", "f_h", "f_down", "f_vec", "f_topk")]
        N0 = NE * 2

        def l0f_tensor(pe):
            pe.wait_ge(l0f_loaded, 16 * 4)
            with pe.Fori(0, B) as b:
                ln_tensor(pe, b + 4, X[:, b, :])
                pe.wait_ge(ln_out, b + 6)
                for t in range(NT):
                    mm = pe.matmul(PS[:, 0, t * NE:(t + 1) * NE], xn[:, t * P:(t + 1) * P], GW0[:, :], start=True, stop=True)
                mm.then_inc(f_logit, 1)
            pe.wait_ge(f_aff, B)
            for t in range(NT):
                mm = pe.transpose(PS[0:B * NE, 1, t * P:(t + 1) * P], F_AFF[:, t, :], IDF[:, :])
            mm.then_inc(f_turn, 1)
            pe.wait_ge(f_xa, B)
            with pe.Fori(0, B) as b:
                pe.wait_ge(f_gs, b + 1)
                for i in range(N0):
                    e, h = i // 2, i % 2
                    if h == 0:
                        if e >= 2:
                            pe.wait_ge(f_h, b * N0 + 2 * (e - 1))
                        pe.matmul(PS[:, 5 * (e % 2), :], IDF[0:NE, e:e + 1].to_broadcast([NE, P]), F_GS[0:NE, :], start=True, stop=True).then_inc(f_bc, 1)
                    if i >= 2:
                        pe.wait_ge(f_h, b * N0 + i - 1)
                    pe.matmul(PS[:, 2 + i % 2, :], E_G[:, e, h, :], F_XA[:, b, :], start=True, stop=True)
                    pe.matmul(PS[:, [4, 6][i % 2], :], E_U[:, e, h, :], F_XA[:, b, :], start=True, stop=True).then_inc(f_gu, 1)
                    if i >= 1:
                        l0f_down(pe, b, i - 1)
                l0f_down(pe, b, N0 - 1)

        def l0f_down(pe, b, i):
            pe.wait_ge(f_h, b * N0 + i + 1)
            pe.matmul(PS[:, 1, :], E_D[:, i // 2, i % 2, :], F_H[i % 2], start=i == 0, stop=i == N0 - 1).then_inc(f_down, 1)

        def l0f_scalar(act):
            with act.Fori(0, B) as b:
                ln_scalar(act, b + 4)
                act.wait_ge(f_sub, b + 1)
                act.activation(F_E, F_E, ACT.Exp).then_inc(f_exp, 1)
            with act.Fori(0, B) as b:
                for i in range(N0):
                    act.wait_ge(f_gu, b * N0 + i + 1)
                    if i >= 2:
                        act.wait_ge(f_h, b * N0 + i - 1)
                    act.activation(F_SG[i % 2], PS[:, 2 + i % 2, :], ACT.Silu).then_inc(f_silu, 1)

        def l0f_vector(dve):
            st = Steps(dve, f_vec)
            with dve.Fori(0, B) as b:
                st.body(b, 2)
                ln_vector(dve, b + 4, X[:, b, :], xn)
                dve.wait_ge(f_logit, b + 1)
                lg = PS[:, 0, 0:NT * NE].rearrange("p (t e) -> p t e", t=NT)
                dve.tensor_reduce(F_M, lg, AX, ALU.max, negate=True).then_inc(f_neg, 1)
                dve.wait_ge(f_neg, b + 1)
                dve.tensor_tensor(F_E, lg, along(F_M, NE), ALU.add).then_inc(f_sub, 1)
                dve.wait_ge(f_exp, b + 1)
                st.done(dve.tensor_reduce(F_S, F_E, AX, ALU.add))
                st.settle()
                st.done(dve.reciprocal(F_R, F_S))
                st.settle()
                dve.tensor_tensor(F_AFF[:, :, bass.ts(b, NE)], F_E, along(F_R, NE), ALU.mult).then_inc(f_aff, 1)
                dve.wait_ge(f_aff, b + 1)
                dve.wait_ge(f_xa, b + 1)
                st.end()
            dve.wait_ge(f_turn, 1)
            tk = Steps(dve, f_topk)
            tk.done(dve.tensor_copy(F_A[0:B * NE, :], PS[0:B * NE, 1, :]))
            tk.done(dve.tensor_copy(F_W[0:B * NE, :], PS[0:B * NE, 1, :]))
            tk.settle()
            for r in range(CAP // 8):
                tk.done(dve.max(F_M8[0:B * NE, :], F_W[0:B * NE, :]))
                tk.settle()
                tk.done(dve.match_replace(out=F_W[0:B * NE, :], in_to_replace=F_M8[0:B * NE, :], in_values=F_W[0:B * NE, :], imm_value=-1.0))
                tk.settle()
            dve.scalar_tensor_tensor(out=F_G[0:B * NE, :], in0=F_W[0:B * NE, :], scalar=0.0, in1=F_A[0:B * NE, :],
                                     op0=ALU.is_lt, op1=ALU.mult).then_inc(f_gate, 1)
            with dve.Fori(0, B) as b:
                for i in range(N0):
                    dve.wait_ge(f_silu, b * N0 + i + 1)
                    st2 = F_T[i % 2]
                    dve.tensor_tensor(st2, F_SG[i % 2], PS[:, [4, 6][i % 2], :], ALU.mult).then_inc(f_neg, 1)
                    dve.wait_ge(f_neg, b * N0 + i + 1 + B)
                    dve.wait_ge(f_bc, b * NE + i // 2 + 1)
                    if i >= 2:
                        dve.wait_ge(f_down, b * N0 + i - 1)
                    dve.tensor_tensor(F_H[i % 2], st2, PS[:, 5 * (i // 2 % 2), :], ALU.mult).then_inc(f_h, 1)
                dve.wait_ge(f_down, (b + 1) * N0)
                dve.tensor_tensor(X[:, b, :], X[:, b, :], PS[:, 1, :], ALU.add).then_inc(x_done, 1)

        def l0f_pool(pool):
            with pool.Fori(0, B) as b:
                pool.wait_ge(ln_out, b + 6)
                pool.tensor_copy(F_XA[:, b, :], xn).then_inc(f_xa, 1)
            pool.wait_ge(f_gb, 16 * B)
            with pool.Fori(0, B) as b:
                pool.wait_ge(x_done, b + 4)
                pool.tensor_copy(F_GS[0:NE, :], F_GB[0:NE, b, :]).then_inc(f_gs, 1)

        L1W = sb("L1W", [P, 7, P])
        L1CW = sb("L1CW", [P, 2])
        L1G = sb("L1G", [P, 1])
        PTR_I = sb("PTR_I", [P, B * NT], I32)
        IDS_I = sb("IDS_I", [P, B, S2], I32)
        IOTA = sb("IOTA", [P, S2])
        l1x_loaded = sem("l1x_loaded")
        c = carver()
        A_C = c(S2)
        A_Q = c(2 * T).rearrange("p (j n) -> p j n", j=2)
        A_K = c(2 * S2).rearrange("p (j k) -> p j k", j=2)
        A_V = c(2 * P).rearrange("p (j d) -> p j d", j=2)
        A_PTR = c(B * NT)
        A_IX = c(3 * B * NT).rearrange("p (w b t) -> p w b t", w=3, b=B)
        A_IDS = c(B * S2).rearrange("p (b k) -> p b k", b=B)
        A_OH = c(3 * NT * S2).rearrange("p (w k) -> p w k", w=3 * NT)
        A_T = c(3 * NT * S2).rearrange("p (w k) -> p w k", w=3 * NT)
        A_L = c(2 * 3 * NT).rearrange("p (j w) -> p j w", j=2)
        A_N = c(16 * NT).rearrange("p (i t) -> p i t", t=NT)
        A_M = c(2 * NT).rearrange("p (j t) -> p j t", j=2)
        A_P = c(2 * NT * S2).rearrange("p (j t k) -> p j t k", j=2, t=NT)
        A_PT = c(2 * T).rearrange("p (j n) -> p j n", j=2)
        A_CX = c(T)
        A_W = c(2)
        A_WM = c(4)
        a_ctx, a_proj, a_q, a_kv, a_score, a_sub, a_exp, a_p, a_turn, a_pt, a_cx, a_cxs, a_out, a_vec, a_pre, a_we = [
            sem(n) for n in ("a_ctx", "a_proj", "a_q", "a_kv", "a_score", "a_sub", "a_exp", "a_p", "a_turn", "a_pt",
                             "a_cx", "a_cxs", "a_out", "a_vec", "a_pre", "a_we")]
        PSC = PS[:, 0:2, :].rearrange("p g (u j z) -> p (g u) j z", u=2, j=2)[:, :, :, 0:S2]

        def l1x_tensor(pe):
            pe.wait_ge(l1x_loaded, 16 * 6)
            with pe.Fori(0, B) as b:
                ln_tensor(pe, b + 8, X[:, b, :])
                pe.wait_ge(a_ctx, b + 1)
                for j in range(2):
                    pe.matmul(PS[:, 4, j * P:j * P + S2], L1W[:, 2 + j, :], A_C, start=True, stop=True)
                for j in range(2):
                    mm = pe.matmul(PS[0:S2, 5, j * P:(j + 1) * P], A_C, L1W[:, 4 + j, :], start=True, stop=True)
                mm.then_inc(a_proj, 1)
                pe.wait_ge(ln_out, b + 10)
                for j in range(2):
                    mm = pe.matmul(PS[:, 2 + j, :], L1W[:, j, :], xn, start=True, stop=True)
                mm.then_inc(a_proj, 1)
                pe.wait_ge(a_q, 2 * b + 2)
                pe.wait_ge(a_kv, b + 1)
                for t in range(NT):
                    for j in range(2):
                        mm = pe.matmul(PSC[:, t, j, :], A_Q[:, j, t * P:(t + 1) * P], A_K[:, j, :], start=True, stop=True)
                mm.then_inc(a_score, 1)
                pe.wait_ge(a_p, b + 1)
                for j in range(2):
                    for t in range(NT):
                        mm = pe.transpose(PS[0:S2, 2 + j, t * P:(t + 1) * P], A_P[:, j, t, :], IDF[:, :])
                mm.then_inc(a_turn, 1)
                pe.wait_ge(a_pt, 2 * b + 2)
                for j in range(2):
                    mm = pe.matmul(PS[:, 4, :], A_V[0:S2, j, :], A_PT[0:S2, j, :], start=j == 0, stop=j == 1)
                mm.then_inc(a_cx, 1)
                pe.wait_ge(a_cxs, b + 1)
                pe.matmul(PS[:, 5, :], L1W[:, 6, :], A_CX, start=True, stop=True).then_inc(a_out, 1)

        def l1x_scalar(act):
            act.wait_ge(a_sub, 1)
            act.activation(A_W, A_W, ACT.Exp).then_inc(a_we, 1)
            with act.Fori(0, B) as b:
                ln_scalar(act, b + 8)
                act.wait_ge(a_proj, 2 * b + 2)
                for j in range(2):
                    act.activation(A_Q[:, j, :], PS[:, 2 + j, :], ACT.Copy, scale=P ** -0.5).then_inc(a_q, 1)
                act.wait_ge(a_sub, b + 2)
                act.activation(A_L, A_L, ACT.Exp).then_inc(a_exp, 1)
                act.wait_ge(a_turn, b + 1)
                for j in range(2):
                    act.activation(A_PT[0:S2, j, :], PS[0:S2, 2 + j, :], ACT.Copy).then_inc(a_pt, 1)
                act.wait_ge(a_cx, b + 1)
                act.activation(A_CX, PS[:, 4, :], ACT.Copy).then_inc(a_cxs, 1)

        def l1x_vector(dve):
            dve.wait_ge(l1x_loaded, 16 * 6)
            pre = Steps(dve, a_pre)

            def once(ins):
                pre.done(ins)
                pre.settle()
            once(dve.tensor_reduce(A_WM[:, 0:1], L1CW[:, :], AX, ALU.max, negate=True))
            dve.tensor_scalar(A_W, L1CW[:, :], A_WM[:, 0:1], None, ALU.add).then_inc(a_sub, 1)
            dve.wait_ge(a_we, 1)
            once(dve.tensor_reduce(A_WM[:, 1:2], A_W, AX, ALU.add))
            once(dve.reciprocal(A_WM[:, 2:3], A_WM[:, 1:2]))
            once(dve.tensor_scalar(A_W, A_W, A_WM[:, 2:3], None, ALU.mult))
            once(dve.tensor_copy(A_PTR, PTR_I[:, :]))
            once(dve.tensor_copy(A_IDS, IDS_I[:, :, :]))
            for w in range(3):
                ix = A_IX[:, w, :, :]
                once(dve.tensor_scalar(ix, A_PTR.rearrange("p (b t) -> p b t", b=B), float(w), float(S2 - 1), ALU.add, ALU.min))
                once(dve.tensor_scalar(ix, ix, 0.0, None, ALU.max))
            st = Steps(dve, a_vec)
            with dve.Fori(0, B) as b:
                st.body(b, 45)

                def step(ins):
                    st.done(ins)
                    st.settle()
                ln_vector(dve, b + 8, X[:, b, :], xn)
                dve.wait_ge(a_proj, 2 * b + 1)
                step(dve.tensor_copy(A_K, PS[:, 4, 0:2 * P].rearrange("p (j z) -> p j z", j=2)[:, :, 0:S2]))
                for j in range(2):
                    ins = dve.tensor_scalar(A_V[0:S2, j, :], PS[0:S2, 5, j * P:(j + 1) * P], A_W[0:S2, j:j + 1], None, ALU.mult)
                    if j == 0:
                        step(ins)
                ins.then_inc(a_kv, 1)
                for w in range(3):
                    step(dve.tensor_tensor(A_OH[:, w * NT:(w + 1) * NT, :], over(IOTA[:, :], NT), along(A_IX[:, w, b, :], S2), ALU.is_equal))
                step(dve.tensor_tensor(A_T[:, 0:NT, :], A_OH[:, 0:NT, :], over(A_IDS[:, b, :], NT), ALU.mult))
                rel, acc = A_N[:, 0, :], A_N[:, 1, :]
                step(dve.tensor_reduce(rel, A_T[:, 0:NT, :], AX, ALU.add))
                dve.wait_ge(a_score, b + 1)
                for j in range(2):
                    s = PSC[:, :, j, :].rearrange("p t (o k) -> p o t k", o=1).to_broadcast([P, 3, NT, S2])
                    step(dve.tensor_tensor(A_T.rearrange("p (w t) k -> p w t k", w=3), A_OH.rearrange("p (w t) k -> p w t k", w=3), s, ALU.mult))
                    step(dve.tensor_reduce(A_L[:, j, :], A_T, AX, ALU.add))
                l_rel, v1, v2 = [A_L[:, 0, w * NT:(w + 1) * NT] for w in range(3)]
                plus, most, less, imply, diff, xor = [A_N[:, i, :] for i in range(2, 8)]
                none, tmp = A_N[:, 8, :], A_N[:, 9, :]
                step(dve.tensor_tensor(plus, v1, v2, ALU.add))
                step(dve.tensor_tensor(most, v1, v2, ALU.max))
                step(dve.tensor_scalar(less, v1, -1.0, None, ALU.mult))
                step(dve.tensor_tensor(imply, less, v2, ALU.max))
                step(dve.tensor_tensor(diff, v1, v2, ALU.subtract))
                step(dve.scalar_tensor_tensor(out=xor, in0=diff, scalar=-1.0, in1=diff, op0=ALU.mult, op1=ALU.max))
                step(dve.tensor_scalar(tmp, rel, 4.0, None, ALU.is_gt))
                step(dve.scalar_tensor_tensor(out=none, in0=rel, scalar=0.0, in1=tmp, op0=ALU.is_lt, op1=ALU.max))
                step(dve.tensor_tensor(acc, none, l_rel, ALU.mult))
                for rule, term in enumerate((plus, most, less, imply, xor)):
                    step(dve.scalar_tensor_tensor(out=tmp, in0=rel, scalar=float(rule), in1=term, op0=ALU.is_equal, op1=ALU.mult))
                    step(dve.tensor_tensor(l_rel if rule == 4 else acc, acc, tmp, ALU.add))
                L = A_L.rearrange("p j (w t) -> p j w t", w=3)
                step(dve.tensor_tensor(A_M, L[:, :, 0, :], L[:, :, 1, :], ALU.max))
                step(dve.tensor_tensor(A_M, A_M, L[:, :, 2, :], ALU.max))
                for w in range(3):
                    ins = dve.tensor_tensor(L[:, :, w, :], L[:, :, w, :], A_M, ALU.subtract)
                    if w < 2:
                        step(ins)
                ins.then_inc(a_sub, 1)
                dve.wait_ge(a_exp, b + 1)
                step(dve.tensor_tensor(A_M, L[:, :, 0, :], L[:, :, 1, :], ALU.add))
                step(dve.tensor_tensor(A_M, A_M, L[:, :, 2, :], ALU.add))
                step(dve.reciprocal(A_M, A_M))
                for w in range(3):
                    step(dve.tensor_tensor(L[:, :, w, :], L[:, :, w, :], A_M, ALU.mult))
                for j in range(2):
                    step(dve.tensor_tensor(A_T, A_OH, along(A_L[:, j, :], S2), ALU.mult))
                    step(dve.tensor_tensor(A_P[:, j, :, :], A_T[:, 0:NT, :], A_T[:, NT:2 * NT, :], ALU.add))
                    ins = dve.tensor_tensor(A_P[:, j, :, :], A_P[:, j, :, :], A_T[:, 2 * NT:3 * NT, :], ALU.add)
                    if j == 0:
                        step(ins)
                ins.then_inc(a_p, 1)
                dve.wait_ge(a_out, b + 1)
                dve.scalar_tensor_tensor(out=X[:, b, :], in0=PS[:, 5, :], scalar=L1G[:, 0:1], in1=X[:, b, :],
                                         op0=ALU.mult, op1=ALU.add).then_inc(x_done, 1)
                st.end()

        def l1x_pool(pool):
            with pool.Fori(0, B) as b:
                pool.wait_ge(x_done, b + 8)
                pool.tensor_copy(A_C, CT[:, b, :]).then_inc(a_ctx, 1)

        DEPTH, NH, DH, WIN = 6, 16, 64, 32
        NPAIR = NH // 2
        DI = 341
        FF = [(0, 128), (128, 128), (256, DI - 256)]
        SPAN = P + WIN
        Y = sb("Y", [P, B, T + 1])
        WQKV = sb("WQKV", [P, 3 * NH * DH])
        WO = sb("WO", [P, NPAIR, P])
        W1 = sb("W1", [P, 2 * DI])
        W2 = sb("W2", [P, 3, P])
        LNGB = sb("LNGB", [P, 2])
        B1 = sb("B1", [P, 3, 2])
        B2 = sb("B2", [P, 1])
        ROPE = sb("ROPE", [P, 4, NT, DH])
        QKS = sb("QKS", [P, 4, DH])
        BANDS = sb("BANDS", [P, 3, SPAN], BF16)
        BANDS32 = sb("BANDS32", [P, 3, SPAN])
        V_ALL = MOEW[:, :].rearrange("p (t h e) -> p t h e", t=NT, h=NH)
        l1_const, w_qkv, w_o, w_ff, w_qks = sem("l1_const"), sem("w_qkv"), sem("w_o"), sem("w_ff"), sem("w_qks")
        c = carver()
        L_SH = c(T)
        L_TAB = c(4 * NT * DH).rearrange("p (i t d) -> p i t d", i=4, t=NT)
        L_QT = c(NPAIR * (T + WIN)).rearrange("p (h n) -> p h n", h=NPAIR)
        L_KZ = c(NH * (WIN + T)).rearrange("p (h n) -> p h n", h=NH)
        L_CX = c(NPAIR * T).rearrange("p (h n) -> p h n", h=NPAIR)
        L_P = [c(NT * SPAN).rearrange("p (t n) -> p t n", t=NT) for _ in range(2)]
        L_DN = [c(T), c(T)]
        L_NM = c(NT * NH).rearrange("p (t h) -> p t h", t=NT)
        L_NMT = c(T + WIN)
        L_SS = [c(8), c(8)]
        L_SD = [c(8), c(8)]
        L_RAW = [c(T), c(T), c(T)]
        L_SQ = [c(T), c(T)]
        L_T1 = [c(T), c(T)]
        L_T2 = [c(T), c(T)]
        L_QK = [c(T), c(T)]
        L_XG = L_RAW[0]
        L_G = L_SQ + [L_RAW[1]]
        L_H = L_T1 + [L_RAW[2]]
        (p_sh, p_proj, p_raw, p_sq, p_t12, p_add, p_ss, p_sd, p_rn, p_qk, p_turn, p_tev, p_v, p_s, p_max, p_mturn, p_nmt,
         p_st, p_exp, p_pv, p_den, p_cx, p_wo, p_y, p_xg, p_ga, p_gelu, p_h, p_w2, p_ff, p_tab2, p_tab, p_pre) = [sem("p_" + n) for n in (
            "sh proj raw sq t12 add ss sd rn qk turn tev v s max mturn nmt st exp pv den cx wo y xg ga gelu h w2 ff tab2 tab pre").split()]
        NJ = NT * 4
        NV = NT * 2

        def score_tiles(g):
            return PS[:, 2 * g:2 * g + 2, :].rearrange("p g (u z) -> p (g u) z", u=2)[:, :, 0:SPAN]

        def l1f_tensor(pe):
            with pe.Fori(0, B) as b:
                ln_tensor(pe, b + 12, X[:, b, :])
            pe.wait_ge(p_pre, 5)
            with pe.Fori(0, DEPTH) as l:
                with pe.Fori(0, B) as b:
                    i = l * B + b
                    pe.wait_ge(w_qkv, 16 * l + 16)
                    pe.wait_ge(p_sh, 2 * i + 1)
                    for j in range(NJ):
                        if j >= 2:
                            pe.wait_ge(p_raw, i * NJ + j - 1)
                        t, q = j // 4, j % 4
                        pe.matmul(PS[:, j % 2, :], L_SH[:, t * P:(t + 1) * P], WQKV[:, q * T:(q + 1) * T],
                                  start=True, stop=True).then_inc(p_proj, 1)
                        if j >= 3:
                            l1f_turn(pe, i, j - 3)
                    for j in range(NV):
                        if j < 2:
                            pe.wait_ge(p_raw, i * NJ + NJ - 1 + j)
                        else:
                            pe.wait_ge(p_v, i * NV + j - 1)
                        t, q = j // 2, 4 + j % 2
                        mm = pe.matmul(PS[:, j % 2, :], L_SH[:, t * P:(t + 1) * P], WQKV[:, q * T:(q + 1) * T],
                                       start=True, stop=True)
                        mm.then_inc(p_proj, 1)
                        if j < 3:
                            l1f_turn(pe, i, NJ - 3 + j)
                    pe.wait_ge(p_tev, i * NJ + NJ)
                    pe.wait_ge(p_v, i * NV + NV)
                    for h in range(NH):
                        if h >= 2:
                            pe.wait_ge(p_max, i * NH + h - 1)
                        s = score_tiles(h % 2)
                        for t in range(NT):
                            pe.matmul(s[:, t, :], L_QT[:, h // 2, t * P:(t + 1) * P], L_KZ[:, h, t * P:t * P + SPAN],
                                      start=True, stop=False)
                            mm = pe.matmul(s[:, t, :], IDB[:, :], BANDS[:, 1 if t else 0, :], start=False, stop=True)
                        mm.then_inc(p_s, 1)
                    pe.wait_ge(p_max, i * NH + NH)
                    for t in range(NT):
                        mm = pe.transpose(PS[0:NH, 4, t * P:(t + 1) * P], L_NM[:, t, :], IDF[:, :])
                    mm.then_inc(p_mturn, 1)
                    pe.wait_ge(p_nmt, i + 1)
                    for h in range(NH):
                        if h >= 2:
                            pe.wait_ge(p_exp, i * NH + h - 1)
                        s = score_tiles(h % 2)
                        for t in range(NT):
                            pe.matmul(s[:, t, :], L_KZ[:, h, WIN + t * P:WIN + (t + 1) * P], L_QT[:, h // 2, t * P:t * P + SPAN],
                                      start=True, stop=False)
                            pe.matmul(s[:, t, :], IDB[:, :], BANDS[:, 2, :], start=False, stop=False)
                            mm = pe.matmul(s[:, t, :], IDF[0:NH, h:h + 1].to_broadcast([NH, P]), L_NMT[0:NH, t * P:t * P + SPAN],
                                           start=False, stop=True)
                        mm.then_inc(p_st, 1)
                        if h >= 1:
                            l1f_pv(pe, i, h - 1)
                    l1f_pv(pe, i, NH - 1)
                    pe.wait_ge(w_o, 16 * l + 16)
                    pe.wait_ge(p_cx, i * NH + NH)
                    for h in range(NPAIR):
                        mm = pe.matmul(PS[:, 0, :], WO[:, h, :], L_CX[:, h, :], start=h == 0, stop=h == NPAIR - 1)
                    mm.then_inc(p_wo, 1)
                    pe.wait_ge(p_sh, 2 * i + 2)
                    ln_tensor(pe, i + 16, L_SH)
                    pe.wait_ge(w_ff, 112 * l + 112)
                    pe.wait_ge(p_xg, i + 1)
                    for m, (m0, mw) in enumerate(FF):
                        pe.matmul(PS[0:mw, m, :], W1[:, DI + m0:DI + m0 + mw], L_XG, start=True, stop=True)
                        pe.matmul(PS[0:mw, 3 + m, :], W1[:, m0:m0 + mw], L_XG, start=True, stop=True).then_inc(p_ga, 1)
                    for m, (m0, mw) in enumerate(FF):
                        pe.wait_ge(p_h, 3 * i + m + 1)
                        mm = pe.matmul(PS[:, 7, :], W2[0:mw, m, :], L_H[m][0:mw, :], start=m == 0, stop=m == 2)
                    mm.then_inc(p_w2, 1)

        def l1f_turn(pe, i, j):
            pe.wait_ge(p_qk, i * NJ + j + 1)
            if j >= 2:
                pe.wait_ge(p_tev, i * NJ + j - 1)
            for h in range(4):
                mm = pe.transpose(PS[:, 2 + j % 2, h * P:(h + 1) * P], L_QK[j % 2][:, h * P:(h + 1) * P], IDF[:, :])
            mm.then_inc(p_turn, 1)

        def l1f_pv(pe, i, h):
            pe.wait_ge(p_exp, i * NH + h + 1)
            if h >= 4:
                pe.wait_ge(p_cx, i * NH + h - 3)
            for t in range(NT):
                w = min(SPAN, T - t * P)
                mm = pe.matmul(PS[:, 4 + h % 4, t * P:t * P + w], V_ALL[:, t, h, :], L_P[h % 2][:, t, 0:w],
                               start=t == 0, stop=t == NT - 1, skip_group_check=True)
            mm.then_inc(p_pv, 1)

        def l1f_scalar(act):
            with act.Fori(0, B) as b:
                ln_scalar(act, b + 12)
            with act.Fori(0, DEPTH) as l:
                with act.Fori(0, B) as b:
                    i = l * B + b
                    for j in range(NJ):
                        act.wait_ge(p_proj, i * (NJ + NV) + j + 1)
                        if j >= 3:
                            act.wait_ge(p_t12, i * NJ + j - 2)
                        act.activation(L_RAW[j % 3], PS[:, j % 2, :], ACT.Copy).then_inc(p_raw, 1)
                        act.wait_ge(p_raw, i * NJ + j + 1)
                        if j >= 2:
                            act.wait_ge(p_ss, i * NJ + j - 1)
                        act.activation(L_SQ[j % 2], L_RAW[j % 3], ACT.Square).then_inc(p_sq, 1)
                        if j >= 1:
                            l1f_sqrt(act, i, j - 1)
                        if j >= 3:
                            l1f_tev(act, i, j - 3)
                    l1f_sqrt(act, i, NJ - 1)
                    for j in range(NV):
                        act.wait_ge(p_proj, i * (NJ + NV) + NJ + j + 1)
                        t, h0 = j // 2, 8 * (j % 2)
                        src = PS[:, j % 2, :].rearrange("p (h u d) -> p h u d", u=2, d=DH)
                        dst = V_ALL[:, t, h0:h0 + 8, :].rearrange("p (h u) e -> p h u e", u=2)
                        act.activation(dst[:, :, 0, 0:DH], src[:, :, 0, :], ACT.Copy)
                        act.activation(dst[:, :, 1, DH:P], src[:, :, 1, :], ACT.Copy).then_inc(p_v, 1)
                        if j < 3:
                            l1f_tev(act, i, NJ - 3 + j)
                    for h in range(NH):
                        act.wait_ge(p_st, i * NH + h + 1)
                        if h >= 2:
                            act.wait_ge(p_pv, i * NH + h - 1)
                        act.activation(L_P[h % 2], score_tiles(h % 2), ACT.Exp).then_inc(p_exp, 1)
                        if h >= 1:
                            l1f_den(act, i, h - 1)
                    l1f_den(act, i, NH - 1)
                    ln_scalar(act, i + 16)
                    for m, (m0, mw) in enumerate(FF):
                        act.wait_ge(p_ga, 3 * i + m + 1)
                        act.activation(L_G[m][0:mw, :], PS[0:mw, m, :], ACT.Gelu, bias=B1[0:mw, m, 1:2]).then_inc(p_gelu, 1)

        def l1f_sqrt(act, i, j):
            act.wait_ge(p_ss, i * NJ + j + 1)
            act.activation(L_SD[j % 2], L_SS[j % 2], ACT.Sqrt).then_inc(p_sd, 1)

        def l1f_tev(act, i, j):
            act.wait_ge(p_turn, i * NJ + j + 1)
            t, q = j // 4, j % 4
            src = PS[:, 2 + j % 2, :].rearrange("p (h n) -> p h n", h=4)
            if q < 2:
                act.activation(L_QT[:, 4 * q:4 * q + 4, t * P:(t + 1) * P], src, ACT.Copy).then_inc(p_tev, 1)
            else:
                kz = L_KZ[:, 8 * (q - 2):8 * (q - 1), WIN + t * P:WIN + (t + 1) * P].rearrange("p (h u) n -> p h u n", u=2)
                act.activation(kz[0:DH, :, 0, :], src[0:DH, :, :], ACT.Copy)
                act.activation(kz[DH:P, :, 1, :], src[DH:P, :, :], ACT.Copy).then_inc(p_tev, 1)

        def l1f_den(act, i, h):
            act.wait_ge(p_pv, i * NH + h + 1)
            if h >= 4:
                act.wait_ge(p_cx, i * NH + h - 3)
            d = (h // 2) % 2
            if h % 2 == 0:
                act.activation(L_DN[d][0:DH, :], PS[DH:P, 4 + h % 4, :], ACT.Copy).then_inc(p_den, 1)
            else:
                act.activation(L_DN[d][DH:P, :], PS[0:DH, 4 + h % 4, :], ACT.Copy).then_inc(p_den, 1)

        def l1f_vector(dve):
            dve.wait_ge(l1_const, 16 * 2)
            dve.memset(Y[:, :, 0:1], 0.0).then_inc(p_y, 1)
            dve.memset(L_KZ, 0.0).then_inc(p_pre, 1)
            dve.memset(V_ALL, 1.0).then_inc(p_pre, 1)
            dve.memset(L_NMT, 0.0).then_inc(p_pre, 1)
            dve.memset(L_QT[:, :, T:T + WIN], 0.0).then_inc(p_pre, 1)
            dve.tensor_copy(BANDS[:, :, :], BANDS32[:, :, :]).then_inc(p_pre, 1)
            with dve.Fori(0, B) as b:
                ln_vector(dve, b + 12, X[:, b, :], Y[:, b, 1:T + 1])
            dve.wait_ge(ln_out, 17)
            dve.wait_ge(p_pre, 5)
            with dve.Fori(0, DEPTH) as l:
                dve.wait_ge(w_qks, 16 * l + 16)
                for k in range(4):
                    dve.tensor_tensor(L_TAB[:, k, :, :], ROPE[:, k, :, :], over(QKS[:, k, :], NT), ALU.mult).then_inc(p_tab, 1)
                with dve.Fori(0, B) as b:
                    i = l * B + b
                    dve.wait_ge(p_tab, 4 * l + 4)
                    dve.wait_ge(p_y, 2 * i + 1)
                    dve.tensor_scalar(L_SH[0:64, :], Y[0:64, b, 1:T + 1], 1.0, None, ALU.mult)
                    dve.tensor_scalar(L_SH[64:P, :], Y[64:P, b, 0:T], 1.0, None, ALU.mult).then_inc(p_sh, 1)
                    for j in range(NJ):
                        t, q = j // 4, j % 4
                        dve.wait_ge(p_raw, i * NJ + j + 1)
                        if j >= 2:
                            dve.wait_ge(p_qk, i * NJ + j - 1)
                        raw = L_RAW[j % 3].rearrange("p (h u d) -> p h u d", h=8, u=2)
                        t2 = L_T2[j % 2].rearrange("p (h u d) -> p h u d", h=8, u=2)
                        sin = L_TAB[:, 2 * (q // 2) + 1, t, :].rearrange("p (u d) -> p u d", u=2)
                        dve.tensor_tensor(L_T1[j % 2].rearrange("p (h d) -> p h d", h=8), L_RAW[j % 3].rearrange("p (h d) -> p h d", h=8),
                                          over(L_TAB[:, 2 * (q // 2), t, :], 8), ALU.mult)
                        for u in range(2):
                            ins = dve.tensor_tensor(t2[:, :, u, :], raw[:, :, 1 - u, :], over(sin[:, u, :], 8), ALU.mult)
                        ins.then_inc(p_t12, 1)
                        dve.wait_ge(p_sq, i * NJ + j + 1)
                        if j >= 2:
                            dve.wait_ge(p_sd, i * NJ + j - 1)
                        dve.tensor_reduce(L_SS[j % 2], L_SQ[j % 2].rearrange("p (h d) -> p h d", h=8), AX, ALU.add).then_inc(p_ss, 1)
                        if j >= 1:
                            l1f_norm(dve, i, j - 1)
                    l1f_norm(dve, i, NJ - 1)
                    for h in range(NH):
                        dve.wait_ge(p_s, i * NH + h + 1)
                        dve.tensor_reduce(L_NM[:, :, h], score_tiles(h % 2), AX, ALU.max, negate=True).then_inc(p_max, 1)
                    dve.wait_ge(p_mturn, i + 1)
                    dve.tensor_copy(L_NMT[0:NH, 0:T], PS[0:NH, 4, :]).then_inc(p_nmt, 1)
                    for h in range(NPAIR):
                        dve.wait_ge(p_den, i * NH + 2 * h + 2)
                        dn = L_DN[h % 2]
                        dve.reciprocal(dn, dn).then_inc(p_rn, 1)
                        dve.wait_ge(p_rn, i * (NJ + NPAIR) + NJ + h + 1)
                        for u in range(2):
                            r = slice(DH * u, DH * (u + 1))
                            dve.tensor_tensor(L_CX[r, h, :], PS[r, 4 + (2 * h + u) % 4, :], dn[r, :], ALU.mult).then_inc(p_cx, 1)
                    dve.wait_ge(p_wo, i + 1)
                    dve.tensor_tensor(Y[:, b, 1:T + 1], Y[:, b, 1:T + 1], PS[:, 0, :], ALU.add).then_inc(p_y, 1)
                    dve.wait_ge(p_y, 2 * i + 2)
                    dve.tensor_scalar(L_SH[0:64, :], Y[0:64, b, 1:T + 1], 1.0, None, ALU.mult)
                    dve.tensor_scalar(L_SH[64:P, :], Y[64:P, b, 0:T], 1.0, None, ALU.mult).then_inc(p_sh, 1)
                    dve.wait_ge(p_sh, 2 * i + 2)
                    ln_vector(dve, i + 16, L_SH, xn)
                    dve.wait_ge(w_ff, 112 * l + 112)
                    dve.wait_ge(ln_out, i + 18)
                    dve.tensor_scalar(L_XG, xn, LNGB[:, 0:1], LNGB[:, 1:2], ALU.mult, ALU.add).then_inc(p_xg, 1)
                    for m, (m0, mw) in enumerate(FF):
                        dve.wait_ge(p_gelu, 3 * i + m + 1)
                        dve.scalar_tensor_tensor(out=L_H[m][0:mw, :], in0=PS[0:mw, 3 + m, :], scalar=B1[0:mw, m, 0:1],
                                                 in1=L_G[m][0:mw, :], op0=ALU.add, op1=ALU.mult).then_inc(p_h, 1)
                    dve.wait_ge(p_w2, i + 1)
                    dve.scalar_tensor_tensor(out=Y[:, b, 1:T + 1], in0=PS[:, 7, :], scalar=B2[:, 0:1], in1=Y[:, b, 1:T + 1],
                                             op0=ALU.add, op1=ALU.add).then_inc(p_y, 1)
            dve.wait_ge(p_y, 2 * DEPTH * B + 1)
            with dve.Fori(0, B) as b:
                dve.tensor_tensor(X[:, b, :], X[:, b, :], Y[:, b, 1:T + 1], ALU.add).then_inc(x_done, 1)

        def l1f_norm(dve, i, j):
            dve.wait_ge(p_sd, i * NJ + j + 1)
            rn = L_SD[j % 2]
            dve.tensor_scalar(rn, rn, 1e-12, None, ALU.max).then_inc(p_tab2, 1)
            dve.wait_ge(p_tab2, i * NJ + j + 1)
            dve.reciprocal(rn, rn).then_inc(p_rn, 1)
            dve.wait_ge(p_rn, i * (NJ + NPAIR) + j + 1)
            dve.wait_ge(p_add, i * NJ + j + 1)
            if j >= 2:
                dve.wait_ge(p_turn, i * NJ + j - 1)
            dve.tensor_tensor(L_QK[j % 2].rearrange("p (h d) -> p h d", h=8), L_T1[j % 2].rearrange("p (h d) -> p h d", h=8),
                              along(rn, DH), ALU.mult).then_inc(p_qk, 1)

        def l1f_pool(pool):
            with pool.Fori(0, DEPTH) as l:
                with pool.Fori(0, B) as b:
                    i = l * B + b
                    for j in range(NJ):
                        pool.wait_ge(p_t12, i * NJ + j + 1)
                        pool.tensor_tensor(L_T1[j % 2], L_T1[j % 2], L_T2[j % 2], ALU.add).then_inc(p_add, 1)

        late_at = [0]

        def late(rows, cols):
            late_at[0] += cols
            assert late_at[0] <= 3 * NH * DH
            return WQKV[0:rows, late_at[0] - cols:late_at[0]]
        L2W = late(P, 4 * P).rearrange("p (i d) -> p i d", i=4)
        L2B = late(P, 2)
        L2BV = late(1, P)
        MASKF = late(P, NT * S2).rearrange("p (t k) -> p t k", t=NT)
        VCTX = late(S2, B * P).rearrange("p (b d) -> p b d", b=B)
        l2x_loaded = sem("l2x_loaded")
        c = carver()
        C_C = c(S2)
        C_Q = c(T)
        C_K = c(S2)
        C_V = c(P)
        C_S = c(NT * S2).rearrange("p (t k) -> p t k", t=NT)
        C_M = c(NT)
        C_SUM = c(NT)
        C_R = c(NT)
        C_PT = c(T)
        C_CX = c(T)
        C_MASK = c(NT * S2).rearrange("p (t k) -> p t k", t=NT)
        (c_ctx, c_proj, c_q, c_kv, c_score, c_max, c_sub, c_exp, c_vec, c_p, c_turn, c_pt, c_cx, c_cxs, c_out) = [sem("c_" + n) for n in (
            "ctx proj q kv score max sub exp vec p turn pt cx cxs out").split()]
        CS = PS[:, 0, :].rearrange("p (t z) -> p t z", t=NT)[:, :, 0:S2]

        def cross_tensor(pe, b, k, ln, project):
            ln_tensor(pe, b + ln, X[:, b, :])
            pe.wait_ge(c_ctx, k + 1)
            if project:
                pe.matmul(PS[:, 4, 0:S2], L2W[:, 1, :], C_C, start=True, stop=True)
                pe.matmul(PS[0:S2, 5, 0:P], C_C, L2W[:, 2, :], start=True, stop=False)
                pe.matmul(PS[0:S2, 5, 0:P], ONEROW[0:1, 0:S2], L2BV, start=False, stop=True).then_inc(c_proj, 1)
                pe.wait_ge(ln_out, b + ln + 2)
                pe.matmul(PS[:, 2, :], L2W[:, 0, :], xn, start=True, stop=True).then_inc(c_proj, 1)
                pe.wait_ge(c_q, k + 1)
                pe.wait_ge(c_kv, k + 1)
            else:
                pe.wait_ge(ln_out, b + ln + 2)
            q, keys = (C_Q, C_K) if project else (xn, C_C)
            for t in range(NT):
                mm = pe.matmul(CS[:, t, :], q[:, t * P:(t + 1) * P], keys, start=True, stop=True)
            mm.then_inc(c_score, 1)
            pe.wait_ge(c_p, k + 1)
            for t in range(NT):
                mm = pe.transpose(PS[0:S2, 3, t * P:(t + 1) * P], C_S[:, t, :], IDF[:, :])
            mm.then_inc(c_turn, 1)
            pe.wait_ge(c_pt, k + 1)
            pe.matmul(PS[:, 4, :], C_V[0:S2, :], C_PT[0:S2, :], start=True, stop=True).then_inc(c_cx, 1)
            if project:
                pe.wait_ge(c_cxs, k + 1)
                pe.matmul(PS[:, 5, :], L2W[:, 3, :], C_CX, start=True, stop=True).then_inc(c_out, 1)

        def cross_scalar(act, b, k, ln, project):
            ln_scalar(act, b + ln)
            act.wait_ge(c_sub, k + 1)
            act.activation(C_S, C_S, ACT.Exp).then_inc(c_exp, 1)
            act.wait_ge(c_turn, k + 1)
            act.activation(C_PT[0:S2, :], PS[0:S2, 3, :], ACT.Copy).then_inc(c_pt, 1)
            if project:
                act.wait_ge(c_cx, k + 1)
                act.activation(C_CX, PS[:, 4, :], ACT.Copy).then_inc(c_cxs, 1)

        def cross_vector(dve, b, k, ln, project):
            ln_vector(dve, b + ln, X[:, b, :], xn)
            if project:
                dve.wait_ge(c_proj, 2 * k + 1)
                dve.tensor_copy(C_K, PS[:, 4, 0:S2])
                dve.tensor_copy(C_V[0:S2, :], PS[0:S2, 5, 0:P]).then_inc(c_kv, 1)
                dve.wait_ge(c_proj, 2 * k + 2)
                dve.tensor_scalar(C_Q, PS[:, 2, :], L2B[:, 0:1], P ** -0.5, ALU.add, ALU.mult).then_inc(c_q, 1)
            dve.wait_ge(c_score, k + 1)
            scores = CS
            if not project:
                for t in range(NT):
                    ins = dve.scalar_tensor_tensor(out=C_S[:, t, :], in0=CS[:, t, :], scalar=P ** 0.5, in1=C_MASK[:, t, :], op0=ALU.mult, op1=ALU.add)
                ins.then_inc(c_q, 1)
                dve.wait_ge(c_q, k + 1)
                scores = C_S
            dve.tensor_reduce(C_M, scores, AX, ALU.max, negate=True).then_inc(c_max, 1)
            dve.wait_ge(c_max, k + 1)
            dve.tensor_tensor(C_S, scores, along(C_M, S2), ALU.add).then_inc(c_sub, 1)
            dve.wait_ge(c_exp, k + 1)
            dve.tensor_reduce(C_SUM, C_S, AX, ALU.add).then_inc(c_vec, 1)
            dve.wait_ge(c_vec, 2 * k + 1)
            dve.reciprocal(C_R, C_SUM).then_inc(c_vec, 1)
            dve.wait_ge(c_vec, 2 * k + 2)
            dve.tensor_tensor(C_S, C_S, along(C_R, S2), ALU.mult).then_inc(c_p, 1)
            if project:
                dve.wait_ge(c_out, k + 1)
                dve.scalar_tensor_tensor(out=X[:, b, :], in0=PS[:, 5, :], scalar=L2B[:, 1:2], in1=X[:, b, :],
                                         op0=ALU.add, op1=ALU.add).then_inc(x_done, 1)
            else:
                dve.wait_ge(c_cx, k + 1)
                dve.tensor_tensor(X[:, b, :], X[:, b, :], PS[:, 4, :], ALU.add).then_inc(x_done, 1)

        def l2x_tensor(pe):
            pe.wait_ge(l2x_loaded, 16 * 5)
            with pe.Fori(0, B) as b:
                cross_tensor(pe, b, b, 40, True)

        def l2x_scalar(act):
            with act.Fori(0, B) as b:
                cross_scalar(act, b, b, 40, True)

        def l2x_vector(dve):
            dve.wait_ge(l2x_loaded, 16 * 5)
            with dve.Fori(0, B) as b:
                cross_vector(dve, b, b, 40, True)

        def l2x_pool(pool):
            with pool.Fori(0, B) as b:
                pool.wait_ge(x_done, b + 16)
                pool.tensor_copy(C_C, CT[:, b, :]).then_inc(c_ctx, 1)

        DF, NC = 512, 4
        M_W1 = MOEW[:, 0:4096].rearrange("p (e c m) -> p e c m", e=NE, c=NC)
        M_W2 = MOEW[:, 4096:8192].rearrange("p (e c m) -> p e c m", e=NE, c=NC)
        M_B1 = sb("M_B1", [P, 2, NE, NC])
        M_B2 = sb("M_B2", [NE, 2, P])
        M_GW = sb("M_GW", [P, 2, NE])
        M_GB = sb("M_GB", [1, 2, NE])
        RANK = sb("RANK", [P, NE])
        moe_loaded, moe_w = sem("moe_loaded"), sem("moe_w")

        def carve_moe(c):
            d = {}
            for n in "E S1 S2 T1 T2".split():
                d[n] = c(NT * NE).rearrange("p (t e) -> p t e", t=NT)
            for n in "M SUM R M1 M2 MX".split():
                d[n] = c(NT)
            d["GT"] = c(T)
            d["SG"], d["H"] = [c(T), c(T)], [c(T), c(T)]
            return d
        (m_logit, m_max, m_sub, m_exp, m_vec, m_w, m_turn, m_gt, m_bc, m_z, m_act, m_h, m_down) = [sem("m_" + n) for n in (
            "logit max sub exp vec w turn gt bc z act h down").split()]
        NM = NE * NC

        def moe_tensor(pe, k, s, d, src):
            for t in range(NT):
                o = PS[:, 0, t * NE:(t + 1) * NE]
                pe.matmul(o, src[:, t * P:(t + 1) * P], M_GW[:, s, :], start=True, stop=False)
                mm = pe.matmul(o, ONEROW[:, :], M_GB[:, s, :], start=False, stop=True)
            mm.then_inc(m_logit, 1)
            pe.wait_ge(m_w, k + 1)
            for t in range(NT):
                mm = pe.transpose(PS[0:NE, 4, t * P:(t + 1) * P], d["E"][:, t, :], IDF[:, :])
            mm.then_inc(m_turn, 1)
            pe.wait_ge(m_gt, k + 1)
            pe.matmul(PS[:, 1, :], M_B2[:, s, :], d["GT"][0:NE, :], start=True, stop=False)
            for i in range(NM):
                e, c = i // NC, i % NC
                if c == 0:
                    if e >= 2:
                        pe.wait_ge(m_h, k * NM + NC * (e - 1))
                    pe.matmul(PS[:, 5 * (e % 2), :], IDF[0:NE, e:e + 1].to_broadcast([NE, P]), d["GT"][0:NE, :],
                              start=True, stop=True).then_inc(m_bc, 1)
                if i >= 2:
                    pe.wait_ge(m_act, k * NM + i - 1)
                pe.matmul(PS[:, 2 + i % 2, :], M_W1[:, e, c, :], src, start=True, stop=True).then_inc(m_z, 1)
                if i >= 1:
                    moe_down(pe, k, d, i - 1)
            moe_down(pe, k, d, NM - 1)

        def moe_down(pe, k, d, i):
            pe.wait_ge(m_h, k * NM + i + 1)
            pe.matmul(PS[:, 1, :], M_W2[:, i // NC, i % NC, :], d["H"][i % 2], start=False, stop=i == NM - 1).then_inc(m_down, 1)

        def moe_scalar(act, k, s, d, func):
            act.wait_ge(m_sub, k + 1)
            act.activation(d["E"], d["E"], ACT.Exp).then_inc(m_exp, 1)
            for i in range(NM):
                e, c = i // NC, i % NC
                act.wait_ge(m_z, k * NM + i + 1)
                if i >= 2:
                    act.wait_ge(m_h, k * NM + i - 1)
                act.activation(d["SG"][i % 2], PS[:, 2 + i % 2, :], func, bias=M_B1[:, s, e, c:c + 1]).then_inc(m_act, 1)

        def moe_vector(dve, k, s, d, vec0, top2):
            n = [0]

            def step(ins):
                n[0] += 1
                ins.then_inc(m_vec, 1)
                dve.wait_ge(m_vec, vec0 + n[0])
            E, S1, S2_, T1, T2 = d["E"], d["S1"], d["S2"], d["T1"], d["T2"]
            dve.wait_ge(m_logit, k + 1)
            lg = PS[:, 0, 0:NT * NE].rearrange("p (t e) -> p t e", t=NT)
            dve.tensor_reduce(d["M"], lg, AX, ALU.max, negate=True).then_inc(m_max, 1)
            dve.wait_ge(m_max, k + 1)
            dve.tensor_tensor(E, lg, along(d["M"], NE), ALU.add).then_inc(m_sub, 1)
            dve.wait_ge(m_exp, k + 1)
            step(dve.tensor_reduce(d["SUM"], E, AX, ALU.add))
            step(dve.reciprocal(d["R"], d["SUM"]))
            ins = dve.tensor_tensor(E, E, along(d["R"], NE), ALU.mult)
            if top2:
                step(ins)
                rank = over(RANK[:, :], NT)
                for sel, m, src in ((S1, d["M1"], E), (S2_, d["M2"], T2)):
                    step(dve.tensor_reduce(m, src, AX, ALU.max))
                    step(dve.tensor_tensor(T1, src, along(m, NE), ALU.is_equal))
                    step(dve.tensor_tensor(T1, T1, rank, ALU.mult))
                    step(dve.tensor_reduce(d["MX"], T1, AX, ALU.max))
                    step(dve.tensor_tensor(sel, T1, along(d["MX"], NE), ALU.is_equal))
                    if sel is S1:
                        step(dve.tensor_scalar(T2, S1, -2.0, None, ALU.mult))
                        step(dve.tensor_tensor(T2, T2, E, ALU.add))
                step(dve.tensor_tensor(d["SUM"], d["M1"], d["M2"], ALU.add))
                step(dve.reciprocal(d["R"], d["SUM"]))
                step(dve.tensor_tensor(S1, S1, S2_, ALU.add))
                step(dve.tensor_tensor(S1, S1, E, ALU.mult))
                ins = dve.tensor_tensor(E, S1, along(d["R"], NE), ALU.mult)
            ins.then_inc(m_w, 1)
            assert n[0] == (19 if top2 else 2), n[0]
            dve.wait_ge(m_turn, k + 1)
            dve.tensor_copy(d["GT"][0:NE, :], PS[0:NE, 4, :]).then_inc(m_gt, 1)
            for i in range(NM):
                dve.wait_ge(m_act, k * NM + i + 1)
                if i % NC == 0:
                    dve.wait_ge(m_bc, k * NE + i // NC + 1)
                if i >= 2:
                    dve.wait_ge(m_down, k * NM + i - 1)
                dve.tensor_tensor(d["H"][i % 2], d["SG"][i % 2], PS[:, 5 * (i // NC % 2), :], ALU.mult).then_inc(m_h, 1)
            dve.wait_ge(m_down, k * NM + NM)

        c = carver()
        G2 = carve_moe(c)

        def l2f_tensor(pe):
            pe.wait_ge(moe_loaded, 16 * 9)
            pe.wait_ge(moe_w, 16 * 2)
            with pe.Fori(0, B) as b:
                ln_tensor(pe, b + 44, X[:, b, :])
                pe.wait_ge(ln_out, b + 46)
                moe_tensor(pe, b, 0, G2, xn)

        def l2f_scalar(act):
            act.wait_ge(moe_loaded, 16 * 9)
            with act.Fori(0, B) as b:
                ln_scalar(act, b + 44)
                moe_scalar(act, b, 0, G2, ACT.Gelu)

        def l2f_vector(dve):
            dve.wait_ge(moe_loaded, 16 * 9)
            with dve.Fori(0, B) as b:
                ln_vector(dve, b + 44, X[:, b, :], xn)
                moe_vector(dve, b, 0, G2, 19 * b, True)
                dve.tensor_tensor(X[:, b, :], X[:, b, :], PS[:, 1, :], ALU.add).then_inc(x_done, 1)

        def l3x_tensor(pe):
            with pe.Fori(0, B) as b:
                cross_tensor(pe, b, b + 4, 48, False)

        def l3x_scalar(act):
            with act.Fori(0, B) as b:
                cross_scalar(act, b, b + 4, 48, False)

        def l3x_vector(dve):
            dve.tensor_scalar(C_MASK, MASKF[:, :, :], -1.0e9, None, ALU.mult).then_inc(c_kv, 1)
            dve.wait_ge(c_kv, 5)
            with dve.Fori(0, B) as b:
                cross_vector(dve, b, b + 4, 48, False)

        def l3x_pool(pool):
            with pool.Fori(0, B) as b:
                pool.wait_ge(x_done, b + 24)
                pool.tensor_copy(C_V[0:S2, :], VCTX[:, b, :])
                pool.tensor_copy(C_C, CT[:, b, :]).then_inc(c_ctx, 1)

        CONVW = late(P, 3 * P).rearrange("p (k d) -> p k d", k=3)
        WQKV3 = late(P, 3 * P).rearrange("p (i d) -> p i d", i=3)
        WO3 = late(P, P)
        B3 = late(P, 8)
        BV3 = late(1, P)
        l3_loaded = sem("l3_loaded")
        c = carver()
        H_KM = c(H0 * T).rearrange("p (h n) -> p h n", h=H0)
        VROW3 = H0 * VSTEP
        H_VB = c(NT * VROW3).rearrange("p (t z) -> p t z", t=NT)
        H_P = [c(T) for _ in range(4)]
        H_C1, H_Q, H_K, H_CX = c(T), c(T), c(T), c(T)
        H_N1, H_XR = c(T), c(T)
        H_RC = H_K
        H_NM = c(NT * H0).rearrange("p (t h) -> p t h", t=NT)
        H_NMT = c(T)
        G3 = carve_moe(c)
        (h_conv, h_c1, h_proj, h_ev, h_km, h_s, h_max, h_mturn, h_nmt, h_st, h_exp, h_pv, h_rc, h_cx, h_wo, h_r, h_n1, h_ev2) = [
            sem("h_" + n) for n in "conv c1 proj ev km s max mturn nmt st exp pv rc cx wo r n1 ev2".split()]
        NU = H0 * NT

        def l3f_tensor(pe):
            nc.disable_value_cache = True
            pe.wait_ge(l3_loaded, 16 * 5)
            pe.wait_ge(moe_w, 16 * 4)
            with pe.Fori(0, B) as b:
                k0 = 3 * b + 52
                ln_tensor(pe, k0, X[:, b, :])
                pe.wait_ge(ln_out, k0 + 2)
                for k in range(3):
                    mm = pe.matmul(PS[:, 0, :], CONVW[:, k, :], XN[:, k:k + T], start=k == 0, stop=k == 2)
                mm.then_inc(h_conv, 1)
                pe.wait_ge(h_c1, b + 1)
                for j in range(2):
                    pe.matmul(PS[:, 1 + j, :], WQKV3[:, j, :], H_C1, start=True, stop=True)
                for t in range(NT):
                    o = PS[:, 3, t * P:(t + 1) * P]
                    pe.matmul(o, H_C1[:, t * P:(t + 1) * P], WQKV3[:, 2, :], start=True, stop=False)
                    mm = pe.matmul(o, ONEROW[:, :], BV3, start=False, stop=True)
                mm.then_inc(h_proj, 1)
                pe.wait_ge(h_ev, b + 1)
                for n in range(NU):
                    h, t = n // NT, n % NT
                    if t == 0:
                        pe.wait_ge(h_km, b * H0 + h + 1)
                    if n >= 4:
                        pe.wait_ge(h_max, b * NU + n - 3)
                    pe.matmul(PS[:, n % 4, :], H_Q[:, t * P:(t + 1) * P], H_KM[:, h, :], start=True, stop=True).then_inc(h_s, 1)
                pe.wait_ge(h_max, b * NU + NU)
                for t in range(NT):
                    mm = pe.transpose(PS[0:H0, 4, t * P:(t + 1) * P], H_NM[:, t, :], IDF[:, :])
                mm.then_inc(h_mturn, 1)
                pe.wait_ge(h_nmt, b + 1)
                for n in range(NU):
                    h, t = n // NT, n % NT
                    if n >= 4:
                        pe.wait_ge(h_exp, b * NU + n - 3)
                    pe.matmul(PS[:, n % 4, :], H_KM[:, h, t * P:(t + 1) * P], H_Q, start=True, stop=False)
                    pe.matmul(PS[:, n % 4, :], IDF[0:H0, h:h + 1].to_broadcast([H0, P]), H_NMT[0:H0, :],
                              start=False, stop=True).then_inc(h_st, 1)
                    if n >= 2:
                        l3f_pv(pe, b, n - 2)
                l3f_pv(pe, b, NU - 2)
                l3f_pv(pe, b, NU - 1)
                pe.wait_ge(h_cx, 2 * b + 2)
                pe.matmul(PS[:, 0, :], WO3, H_CX, start=True, stop=True).then_inc(h_wo, 1)
                pe.wait_ge(h_r, 2 * b + 1)
                ln_tensor(pe, k0 + 1, H_XR)
                pe.wait_ge(h_n1, b + 1)
                moe_tensor(pe, b + 4, 1, G3, H_N1)
                pe.wait_ge(h_r, 2 * b + 2)
                ln_tensor(pe, k0 + 2, H_XR)
            nc.disable_value_cache = False

        def l3f_pv(pe, b, n):
            h, t = n // NT, n % NT
            pe.wait_ge(h_exp, b * NU + n + 1)
            pe.matmul(PS[:, 4 + h // 8, :], H_VB[:, t, h * P:(h + 1) * P], H_P[n % 4],
                      start=n % (8 * NT) == 0, stop=n % (8 * NT) == 8 * NT - 1).then_inc(h_pv, 1)

        def l3f_scalar(act):
            nc.disable_value_cache = True
            with act.Fori(0, B) as b:
                k0 = 3 * b + 52
                ln_scalar(act, k0)
                for n in range(NU):
                    act.wait_ge(h_st, b * NU + n + 1)
                    if n >= 4:
                        act.wait_ge(h_pv, b * NU + n - 3)
                    act.activation(H_P[n % 4], PS[:, n % 4, :], ACT.Exp).then_inc(h_exp, 1)
                ln_scalar(act, k0 + 1)
                moe_scalar(act, b + 4, 1, G3, ACT.Relu)
                ln_scalar(act, k0 + 2)
            nc.disable_value_cache = False

        def l3f_vector(dve):
            nc.disable_value_cache = True
            dve.wait_ge(l3_loaded, 16 * 5)
            dve.memset(H_VB, 0.0).then_inc(h_rc, 1)
            dve.wait_ge(h_rc, 1)
            for h in range(H0):
                at = h * P + 64 + DK0 * (h % 8)
                dve.memset(H_VB[:, :, at:at + DK0], 1.0)
            with dve.Fori(0, B) as b:
                k0 = 3 * b + 52
                ln_vector(dve, k0, X[:, b, :], xn)
                dve.wait_ge(h_conv, b + 1)
                dve.tensor_scalar(H_C1, PS[:, 0, :], B3[:, 0:1], None, ALU.add).then_inc(h_c1, 1)
                dve.wait_ge(h_proj, b + 1)
                dve.tensor_scalar(H_K, PS[:, 2, :], B3[:, 2:3], None, ALU.add).then_inc(h_rc, 1)
                for t in range(NT):
                    for g in range(2):
                        vg = H_VB[:, t, g * 8 * P:g * 8 * P + 8 * VSTEP].rearrange("p (h e) -> p h e", e=VSTEP)[:, :, 0:DK0]
                        dve.tensor_copy(vg, PS[:, 3, t * P + g * 64:t * P + (g + 1) * 64].rearrange("p (h e) -> p h e", e=DK0))
                dve.tensor_scalar(H_Q, PS[:, 1, :], B3[:, 1:2], DK0 ** -0.5, ALU.add, ALU.mult).then_inc(h_ev, 1)
                dve.wait_ge(h_rc, 3 * b + 2)
                for h in range(H0):
                    dve.tensor_scalar(H_KM[:, h, :], H_K, HMASK[:, h:h + 1], None, ALU.mult).then_inc(h_km, 1)
                for n in range(NU):
                    h, t = n // NT, n % NT
                    dve.wait_ge(h_s, b * NU + n + 1)
                    dve.tensor_reduce(H_NM[:, t, h:h + 1], PS[:, n % 4, :], AX, ALU.max, negate=True).then_inc(h_max, 1)
                dve.wait_ge(h_mturn, b + 1)
                dve.tensor_copy(H_NMT[0:H0, :], PS[0:H0, 4, :]).then_inc(h_nmt, 1)
                dve.wait_ge(h_km, b * H0 + H0)
                for g in range(2):
                    dve.wait_ge(h_pv, b * NU + (g + 1) * 8 * NT)
                    if g:
                        dve.wait_ge(h_cx, 2 * b + g)
                    dve.reciprocal(H_RC[0:64, :], PS[64:P, 4 + g, :]).then_inc(h_rc, 1)
                    dve.wait_ge(h_rc, 3 * b + g + 3)
                    dve.tensor_tensor(H_CX[64 * g:64 * g + 64, :], PS[0:64, 4 + g, :], H_RC[0:64, :], ALU.mult).then_inc(h_cx, 1)
                dve.wait_ge(h_wo, b + 1)
                dve.scalar_tensor_tensor(out=H_XR, in0=PS[:, 0, :], scalar=B3[:, 3:4], in1=H_C1,
                                         op0=ALU.add, op1=ALU.add).then_inc(h_r, 1)
                dve.wait_ge(h_r, 2 * b + 1)
                ln_vector(dve, k0 + 1, H_XR, H_N1)
                dve.wait_ge(ln_out, k0 + 3)
                dve.tensor_scalar(H_N1, H_N1, B3[:, 4:5], B3[:, 5:6], ALU.mult, ALU.add).then_inc(h_n1, 1)
                dve.wait_ge(h_n1, b + 1)
                moe_vector(dve, b + 4, 1, G3, 2 * b + 76, False)
                dve.tensor_tensor(H_XR, H_N1, PS[:, 1, :], ALU.add).then_inc(h_r, 1)
                dve.wait_ge(h_r, 2 * b + 2)
                ln_vector(dve, k0 + 2, H_XR, H_CX)
                dve.wait_ge(ln_out, k0 + 4)
                dve.tensor_scalar(H_Q, H_CX, B3[:, 6:7], B3[:, 7:8], ALU.mult, ALU.add).then_inc(h_ev2, 1)
                dve.wait_ge(h_ev2, b + 1)
                dve.tensor_tensor(X[:, b, :], X[:, b, :], H_Q, ALU.add).then_inc(x_done, 1)
                dve.wait_ge(x_done, b + 29)
            nc.disable_value_cache = False

        block = ctx.enter_context(nc.Block())

        @block.sync
        def _(sp):
            sp.dma_start(X[:, :, :], a["xT"]).then_inc(x_loaded, 16)
            for dst, name in ((CT[:, :, :], "ctxT"), (AVG[:, :], "c_avg"), (IDF[:, :], "c_ident"),
                              (HMASK[:, :], "c_hmask"), (EPSC[:, :], "c_eps")):
                sp.dma_start(dst, a[name]).then_inc(const_loaded, 16)
            for dst, name in ((L0W[:, :, :], "L0_W"), (L0B[:, :], "L0_b"), (BVROW[:, :], "L0_bv"), (ONEROW[:, :], "c_onerow"),
                              (MSK_Q[:, :, :], "mask_q"), (MSK_T[:, :], "mask_t"), (PAD_Q[:, :, :], "pad_q"),
                              (PAD_T[:, :], "pad_t")):
                src = a[name]
                if name == "pad_q":
                    src = bass.AP(tensor=src.tensor, offset=0, ap=[[0, P], [S2, B], [1, S2]])
                sp.dma_start(dst, src).then_inc(l0_loaded, 16)
            for dst, name in ((GW0[:, :], "L0F_gate"), (E_G, "L0F_g"), (E_U, "L0F_u"), (E_D, "L0F_d")):
                sp.dma_start(dst, a[name]).then_inc(l0f_loaded, 16)
            sp.wait_ge(f_gate, 1)
            for b in range(B):
                sp.dma_start(F_GB[0:NE, b, :], F_G[b * NE:(b + 1) * NE, :]).then_inc(f_gb, 16)
            for dst, name, part in ((L1W[:, :, :], "L1X_W", 0), (L1CW[:, :], "L1X_cw", 2), (L1G[:, :], "L1X_gain", 1),
                                    (PTR_I[:, :], "ptr", 0), (IDS_I[:, :, :], "ids", -1), (IOTA[:, :], "c_iota", S2)):
                src = a[name]
                if part > 0:
                    src = bass.AP(tensor=src.tensor, offset=0, ap=[[0, P], [1, part]])
                elif part < 0:
                    src = bass.AP(tensor=src.tensor, offset=0, ap=[[0, P], [T, B], [1, S2]])
                sp.dma_start(dst, src).then_inc(l1x_loaded, 16)
            sp.dma_start(ROPE[:, :, :, :], a["c_rope"]).then_inc(l1_const, 16)
            sp.dma_start(BANDS32[:, :, :], a["c_bands"]).then_inc(l1_const, 16)

            def load_qkv(l):
                sp.dma_start(WQKV[:, :], a["L1F_qkv"][l, :, :]).then_inc(w_qkv, 16)
                sp.dma_start(QKS[:, :, :], bass.AP(tensor=a["L1F_qks"].tensor, offset=l * 4 * DH, ap=[[0, P], [DH, 4], [1, DH]])).then_inc(w_qks, 16)

            def load_wo(l):
                sp.dma_start(WO[:, :, :], a["L1F_wo"][l, :, :, :]).then_inc(w_o, 16)

            def load_ff(l):
                sp.dma_start(W1[:, :], a["L1F_w1"][l, :, :]).then_inc(w_ff, 16)
                sp.dma_start(W2[:, 0:2, :], a["L1F_w2a"][l, :, :, :]).then_inc(w_ff, 16)
                sp.dma_start(W2[0:DI - 256, 2, :], a["L1F_w2b"][l, :, :]).then_inc(w_ff, 16)
                sp.dma_start(LNGB[:, :], a["L1F_lngb"][l, :, :]).then_inc(w_ff, 16)
                sp.dma_start(B1[:, 0:2, :], a["L1F_b1a"][l, :, :, :]).then_inc(w_ff, 16)
                sp.dma_start(B1[0:DI - 256, 2, :], a["L1F_b1b"][l, :, :]).then_inc(w_ff, 16)
                sp.dma_start(B2[:, :], a["L1F_b2"][l, :, :]).then_inc(w_ff, 16)

            load_qkv(0)
            load_wo(0)
            load_ff(0)
            with sp.Fori(1, DEPTH) as l:
                sp.wait_ge(p_proj, l * B * (NJ + NV))
                sp.wait_ge(p_tab, 4 * l)
                load_qkv(l)
                sp.wait_ge(p_wo, l * B)
                load_wo(l)
                sp.wait_ge(p_y, 2 * B * l + 1)
                load_ff(l)
            sp.wait_ge(p_proj, DEPTH * B * (NJ + NV))
            for dst, name in ((L2W, "L2X_W"), (L2B, "L2X_b"), (L2BV, "L2X_bv"), (MASKF, "maskf"), (VCTX, "vctx")):
                sp.dma_start(dst, a[name]).then_inc(l2x_loaded, 16)
            for dst, name in ((M_B1[:, 0, :, :], "L2F_b1"), (M_B1[:, 1, :, :], "L3F_b1"), (M_B2[:, 0, :], "L2F_b2"), (M_B2[:, 1, :], "L3F_b2"),
                              (M_GW[:, 0, :], "L2F_gw"), (M_GW[:, 1, :], "L3F_gw"), (M_GB[:, 0, :], "L2F_gb"), (M_GB[:, 1, :], "L3F_gb"),
                              (RANK[:, :], "c_rank")):
                sp.dma_start(dst, a[name]).then_inc(moe_loaded, 16)
            sp.wait_ge(x_done, 16)
            sp.dma_start(M_W1, a["L2F_w1"]).then_inc(moe_w, 16)
            sp.dma_start(M_W2, a["L2F_w2"]).then_inc(moe_w, 16)
            for dst, name in ((CONVW, "L3F_conv"), (WQKV3, "L3F_wqkv"), (WO3, "L3F_wo"), (B3, "L3F_b"), (BV3, "L3F_bv")):
                sp.dma_start(dst, a[name]).then_inc(l3_loaded, 16)
            sp.wait_ge(x_done, 24)
            sp.dma_start(M_W1, a["L3F_w1"]).then_inc(moe_w, 16)
            sp.dma_start(M_W2, a["L3F_w2"]).then_inc(moe_w, 16)
            sp.wait_ge(x_done, 4 * 8)
            sp.dma_start(out, X[:, :, :]).then_inc(out_stored, 16)
            sp.wait_ge(out_stored, 16)

        @block.gpsimd
        def _(pool):
            pool.wait_ge(const_loaded, 16 * 5)
            pool.memset(XN[:, :], 0.0).then_inc(pool_const, 1)
            pool.tensor_copy(IDB[:, :], IDF[:, :]).then_inc(pool_const, 1)
            l0x_pool(pool)
            pool.wait_ge(x_done, 4 * 1)
            l0f_pool(pool)
            pool.wait_ge(x_done, 4 * 2)
            l1x_pool(pool)
            pool.wait_ge(x_done, 4 * 3)
            l1f_pool(pool)
            pool.wait_ge(x_done, 4 * 4)
            l2x_pool(pool)
            pool.wait_ge(x_done, 4 * 6)
            l3x_pool(pool)
        @block.scalar
        def _(act):
            act.wait_ge(const_loaded, 16 * 5)
            l0x_scalar(act)
            act.wait_ge(x_done, 4 * 1)
            l0f_scalar(act)
            act.wait_ge(x_done, 4 * 2)
            l1x_scalar(act)
            act.wait_ge(x_done, 4 * 3)
            l1f_scalar(act)
            act.wait_ge(x_done, 4 * 4)
            l2x_scalar(act)
            act.wait_ge(x_done, 4 * 5)
            l2f_scalar(act)
            act.wait_ge(x_done, 4 * 6)
            l3x_scalar(act)
            act.wait_ge(x_done, 4 * 7)
            l3f_scalar(act)
        @block.tensor
        def _(pe):
            pe.wait_ge(const_loaded, 16 * 5)
            pe.wait_ge(x_loaded, 16)
            pe.wait_ge(pool_const, 2)
            l0x_tensor(pe)
            pe.wait_ge(x_done, 4 * 1)
            l0f_tensor(pe)
            pe.wait_ge(x_done, 4 * 2)
            l1x_tensor(pe)
            pe.wait_ge(x_done, 4 * 3)
            l1f_tensor(pe)
            pe.wait_ge(x_done, 4 * 4)
            l2x_tensor(pe)
            pe.wait_ge(x_done, 4 * 5)
            l2f_tensor(pe)
            pe.wait_ge(x_done, 4 * 6)
            l3x_tensor(pe)
            pe.wait_ge(x_done, 4 * 7)
            l3f_tensor(pe)
        @block.vector
        def _(dve):
            dve.wait_ge(const_loaded, 16 * 5)
            dve.wait_ge(x_loaded, 16)
            dve.wait_ge(pool_const, 2)
            dve.memset(LN_C[:, :], 0.0).then_inc(ln_out, 1)
            dve.wait_ge(ln_out, 1)
            l0x_vector(dve)
            dve.wait_ge(x_done, 4 * 1)
            l0f_vector(dve)
            dve.wait_ge(x_done, 4 * 2)
            l1x_vector(dve)
            dve.wait_ge(x_done, 4 * 3)
            l1f_vector(dve)
            dve.wait_ge(x_done, 4 * 4)
            l2x_vector(dve)
            dve.wait_ge(x_done, 4 * 5)
            l2f_vector(dve)
            dve.wait_ge(x_done, 4 * 6)
            l3x_vector(dve)
            dve.wait_ge(x_done, 4 * 7)
            l3f_vector(dve)


def kernel(**inputs):
    import numpy as np
    import concourse.bacc as bacc
    from concourse.bass_utils import run_bass_kernel_spmd

    v = {k: np.asarray(w) for k, w in inputs.items()}
    f = np.float32
    eye = np.eye(P, dtype=f)
    half = np.arange(0, 64, 2, dtype=f)
    pos = np.arange(T, dtype=f)
    freqs = pos[:, None] * (f(1.0) / f(10000.0) ** (half / f(64)))[None, :]
    base = (half + f(0.4 * 64)) / f(1.4 * 64)
    decay = base[None, :] ** ((pos - T // 2) / f(16))[:, None]
    cos, sin = np.cos(freqs), np.sin(freqs)
    qk = []
    for s, by in ((decay, f(8.0)), (f(1.0) / decay, f(1.0))):
        qk += [np.concatenate([cos * s, cos * s], 1) * by, np.concatenate([-sin * s, sin * s], 1) * by]
    rope = np.stack([x.reshape(NT, P, 64).transpose(1, 0, 2) for x in qk], 1).astype(f)
    r, s = np.arange(P)[:, None], np.arange(P + 32)[None, :]
    q_sees = (r + 32 - s >= 0) & (r + 32 - s <= 32)
    k_seen = (s - r >= 0) & (s - r <= 32)
    bands = np.stack([np.where(m, 0.0, NEG) for m in (q_sees & (s >= 32), q_sees, k_seen)], 1).astype(f)
    arrays = {
        "c_avg": np.full((P, P), 1 / P, f), "c_ident": eye, 
        "c_hmask": np.repeat(np.eye(H0, dtype=f), DK0, axis=0), "c_eps": np.full((P, 1), EPS, f),
        "c_onerow": np.ones((1, P), f),
        "xT": v["x"].transpose(2, 0, 1), "ctxT": v["ctx_1024"].transpose(2, 0, 1),
        "mask_q": v["mask_SxS2_bk1"].reshape(NT, P, S2).transpose(1, 0, 2),
        "mask_t": v["mask_SxS2_bk1"].T,
        "pad_q": v["mask_BxS2_bf0"], "pad_t": v["mask_BxS2_bf0"].T,
        "L0_W": np.stack([v["L0_xattn_" + n].T for n in ("Wq", "Wk", "Wv", "Wo")], 1),
        "L0_b": np.stack([v["L0_xattn_" + n] for n in ("bq", "bk", "bo")], 1),
        "L0_bv": v["L0_xattn_bv"][None, :],
        "L0F_gate": v["L0_ffn_gate_w"],
        "L0F_g": v["L0_ffn_Wg"].transpose(1, 0, 2).reshape(P, 8, 2, P),
        "L0F_u": v["L0_ffn_Wu"].transpose(1, 0, 2).reshape(P, 8, 2, P),
        "L0F_d": v["L0_ffn_Wd"].reshape(8, 2, P, P).transpose(2, 0, 1, 3),
        "L1X_W": np.stack([v["L1_xattn_" + n].T for n in ("Wqj", "Wqi", "Wkj", "Wki", "Wvj", "Wvi", "Wout")], 1),
        "L1X_cw": v["L1_xattn_council_weights"][None, :], "L1X_gain": v["L1_xattn_gain"].reshape(1, 1),
        "ptr": v["itok_BxS_0_4092"].reshape(B, NT, P).transpose(2, 0, 1).reshape(P, B * NT), "ids": v["itok_BxS_0_7"],
        "c_iota": np.arange(S2, dtype=f)[None, :],
        "c_rope": rope, "c_bands": bands,
        "L1F_qkv": v["L1_ffn_Wqkv"],
        "L1F_qks": np.stack([v["L1_ffn_q_scale"], np.roll(v["L1_ffn_q_scale"], 32, -1),
                             v["L1_ffn_k_scale"], np.roll(v["L1_ffn_k_scale"], 32, -1)], 1),
        "L1F_wo": v["L1_ffn_Wo"].reshape(6, 8, P, P).transpose(0, 2, 1, 3),
        "L1F_w1": v["L1_ffn_W1"], "L1F_w2a": v["L1_ffn_W2"][:, :256].reshape(6, 2, P, P).transpose(0, 2, 1, 3),
        "L1F_w2b": v["L1_ffn_W2"][:, 256:],
        "L1F_lngb": np.stack([v["L1_ffn_ln_g"], v["L1_ffn_ln_b"]], 2),
        "L1F_b1a": v["L1_ffn_b1"].reshape(6, 2, 341)[:, :, :256].reshape(6, 2, 2, P).transpose(0, 3, 2, 1),
        "L1F_b1b": v["L1_ffn_b1"].reshape(6, 2, 341)[:, :, 256:].transpose(0, 2, 1),
        "L1F_b2": v["L1_ffn_b2"][:, :, None],
        "L2X_W": np.stack([v["L2_xattn_" + n].T for n in ("Wq", "Wk", "Wv", "Wo")], 1),
        "L2X_b": np.stack([v["L2_xattn_bq"], v["L2_xattn_bo"]], 1), "L2X_bv": v["L2_xattn_bv"][None, :],
        "maskf": v["mask_SxS2_fk1"].reshape(NT, P, S2).transpose(1, 0, 2), "vctx": v["ctx_1024"].transpose(1, 0, 2),
        "c_rank": np.repeat(8 - np.arange(8, dtype=f)[None, :], P, 0),
        **{n + k: w for n, g, gb, w1, b1, w2, b2 in (
            ("L2F", "L2_ffn_Wg", "L2_ffn_bg", "L2_ffn_W1", "L2_ffn_b1", "L2_ffn_W2", "L2_ffn_b2"),
            ("L3F", "L3_ffn_gate_w", "L3_ffn_gate_b", "L3_ffn_w1", "L3_ffn_b1", "L3_ffn_w2", "L3_ffn_b2")) for k, w in (
            ("_gw", v[g]), ("_gb", v[gb][None, :]), ("_w1", v[w1].transpose(1, 0, 2).reshape(P, 8, 4, P)),
            ("_b1", v[b1].reshape(8, 4, P).transpose(2, 0, 1)), ("_w2", v[w2].reshape(8, 4, P, P).transpose(2, 0, 1, 3)),
            ("_b2", v[b2]))},
        "L3F_conv": v["L3_ffn_conv_w"].transpose(1, 2, 0),
        "L3F_wqkv": v["L3_ffn_wqkv"].reshape(3, P, P).transpose(2, 0, 1), "L3F_wo": v["L3_ffn_wo"].T,
        "L3F_b": np.stack([v["L3_ffn_conv_b"], v["L3_ffn_bqkv"][0:P], v["L3_ffn_bqkv"][P:2 * P], v["L3_ffn_bo"],
                           v["L3_ffn_ln1_g"], v["L3_ffn_ln1_b"], v["L3_ffn_ln2_g"], v["L3_ffn_ln2_b"]], 1),
        "L3F_bv": v["L3_ffn_bqkv"][None, 2 * P:],
    }
    nc = bacc.Bacc("TRN2", target_bir_lowering=False, num_devices=1)
    arrays = {k: np.ascontiguousarray(w) for k, w in arrays.items()}
    aps = {k: nc.dram_tensor(k, w.shape, mybir.dt.from_np(w.dtype), kind="ExternalInput").ap() for k, w in arrays.items()}
    out = nc.dram_tensor("out", (P, B, T), F32, kind="ExternalOutput").ap()
    build(nc, aps, out)
    r = run_bass_kernel_spmd(nc, [arrays], core_ids=[0])
    return np.ascontiguousarray(r.results[0]["out"].transpose(1, 2, 0))
```

```python
from contextlib import ExitStack

import concourse.bass as bass
from concourse import mybir

F32 = mybir.dt.float32
BF16 = mybir.dt.bfloat16
I32 = mybir.dt.int32
U8 = mybir.dt.uint8
ALU = mybir.AluOpType
ACT = mybir.ActivationFunctionType
AX = mybir.AxisListType.X


P = 128
B, T, S2 = 4, 512, 77
NT = T // P
H0, DK0 = 16, 8
NEG = -1.0e30
EPS = 1e-5


class Steps:

    def __init__(self, eng, sem):
        self.eng, self.sem, self.base, self.n = eng, sem, 0, 0

    def body(self, turn, per):
        self.base, self.n, self.per = turn * per, 0, per

    def done(self, ins):
        self.n += 1
        return ins.then_inc(self.sem, 1)

    def settle(self):
        self.eng.wait_ge(self.sem, self.base + self.n)

    def end(self):
        assert self.n == self.per, (self.sem, self.n, self.per)


def over(ap, n):
    return ap.rearrange("p (o k) -> p o k", o=1).to_broadcast([ap.shape[0], n, ap.shape[1]])


def along(ap, n):
    return ap.rearrange("p (h o) -> p h o", o=1).to_broadcast([ap.shape[0], ap.shape[1], n])


def build(nc, a, out):
    with ExitStack() as ctx:
        def sb(name, shape, dt=F32):
            return ctx.enter_context(nc.sbuf_tensor(name, shape, dt))

        def sem(name):
            return ctx.enter_context(nc.semaphore(name))

        PS = ctx.enter_context(nc.psum_tensor("PS", [P, 8, 512], F32))
        X = sb("X", [P, B, T])
        XN = sb("XN", [P, T + 2])
        xn = XN[:, 1:T + 1]
        LN_C = sb("LN_C", [P, T])
        LN_Q = sb("LN_Q", [P, T])
        LN_S = sb("LN_S", [P, NT])
        LN_R = sb("LN_R", [P, NT])
        EPSC = sb("EPSC", [P, 1])
        AVG = sb("AVG", [P, P])
        IDF = sb("IDF", [P, P])
        IDB = sb("IDB", [P, P], BF16)
        CT = sb("CT", [P, B, S2])
        HMASK = sb("HMASK", [P, H0])
        ARENA_COLS = 27 * 1024
        ARENA = sb("ARENA", [P, ARENA_COLS])

        def carver():
            at = [0]

            def carve(cols, dt=F32):
                n = cols if dt == F32 else (cols + 1) // 2
                v = ARENA[:, at[0]:at[0] + n]
                at[0] += n
                assert at[0] <= ARENA_COLS, at[0]
                return v if dt == F32 else v.bitcast(dt)
            return carve

        x_loaded, const_loaded, out_stored = sem("x_loaded"), sem("const_loaded"), sem("out_stored")
        x_done = sem("x_done")
        pool_const = sem("pool_const")
        ln_mean, ln_cen, ln_sq, ln_var, ln_sd, ln_rs, ln_bc, ln_out = [sem(n) for n in (
            "ln_mean", "ln_cen", "ln_sq", "ln_var", "ln_sd", "ln_rs", "ln_bc", "ln_out")]

        def ln_tensor_mean(pe, k, src):
            pe.wait_ge(ln_out, k + 1)
            pe.matmul(PS[:, 6, :], AVG[:, :], src, start=True, stop=True).then_inc(ln_mean, 1)

        def ln_tensor_var(pe, k):
            pe.wait_ge(ln_sq, k + 1)
            for t in range(NT):
                mm = pe.matmul(PS[:, 7, t:t + 1], LN_Q[:, t * P:(t + 1) * P], AVG[:, 0:1], start=True, stop=True)
            mm.then_inc(ln_var, 1)

        def ln_tensor_out(pe, k):
            pe.wait_ge(ln_rs, k + 1)
            for t in range(NT):
                mm = pe.matmul(PS[:, 6, t * P:(t + 1) * P], LN_R[:, t:t + 1].to_broadcast([P, P]), IDF[:, :],
                               start=True, stop=True)
            mm.then_inc(ln_bc, 1)

        def ln_tensor(pe, k, src):
            ln_tensor_mean(pe, k, src)
            ln_tensor_var(pe, k)
            ln_tensor_out(pe, k)

        def ln_scalar_square(act, k):
            act.wait_ge(ln_cen, k + 1)
            act.activation(LN_Q[:, :], LN_C[:, :], ACT.Square).then_inc(ln_sq, 1)

        def ln_scalar_sd(act, k):
            act.wait_ge(ln_var, k + 1)
            act.activation(LN_S[:, :], PS[:, 7, 0:NT], ACT.Sqrt, bias=EPSC[:, 0:1]).then_inc(ln_sd, 1)

        def ln_scalar(act, k):
            ln_scalar_square(act, k)
            ln_scalar_sd(act, k)

        def ln_vector_center(dve, k, src):
            dve.wait_ge(ln_mean, k + 1)
            dve.tensor_tensor(LN_C[:, :], src, PS[:, 6, :], ALU.subtract).then_inc(ln_cen, 1)

        def ln_vector_rs(dve, k):
            dve.wait_ge(ln_sd, k + 1)
            dve.reciprocal(LN_R[:, :], LN_S[:, :]).then_inc(ln_rs, 1)

        def ln_vector_out(dve, k, dst):
            dve.wait_ge(ln_bc, k + 1)
            dve.tensor_tensor(dst, LN_C[:, :], PS[:, 6, :], ALU.mult).then_inc(ln_out, 1)

        def ln_vector(dve, k, src, dst):
            ln_vector_center(dve, k, src)
            ln_vector_rs(dve, k)
            ln_vector_out(dve, k, dst)

        L0W = sb("L0W", [P, 4, P])
        L0B = sb("L0B", [P, 3])
        BVROW = sb("BVROW", [1, P])
        ONEROW = sb("ONEROW", [1, P])
        MSK_Q = sb("MSK_Q", [P, NT, S2], U8)
        MSK_T = sb("MSK_T", [S2, T], U8)
        PAD_Q = sb("PAD_Q", [P, B, S2], U8)
        PAD_T = sb("PAD_T", [S2, B], U8)
        l0_loaded = sem("l0_loaded")
        c = carver()
        XM_Q = c(T)
        XM_K = c(S2)
        XM_C = c(S2)
        XM_KB = c(H0 * S2).rearrange("p (h k) -> p h k", h=H0)
        VSTEP = P + DK0
        XM_VB = c(H0 * VSTEP)
        XM_MQ32 = c(NT * S2).rearrange("p (t k) -> p t k", t=NT)
        XM_MQ = c(NT * S2, BF16).rearrange("p (t k) -> p t k", t=NT)
        XM_MT32 = c(T)
        XM_MT = c(T, BF16)
        XM_PADQ = c(B * S2).rearrange("p (b k) -> p b k", b=B)
        XM_PADT = c(B)
        XM_NM = c(NT * H0).rearrange("p (t h) -> p t h", t=NT)
        XM_NMT = c(T)
        XM_P = [c(T), c(T)]
        XM_RC = c(T)
        XM_CX = c(T)
        HG = [(0, 6), (6, 12), (12, 16)]
        l0_ctx, l0_proj, l0_q, l0_k, l0_v, l0_mask, l0_kb = [sem(n) for n in (
            "l0_ctx", "l0_proj", "l0_q", "l0_k", "l0_v", "l0_mask", "l0_kb")]
        l0_score, l0_max, l0_turn, l0_nmt, l0_st, l0_exp, l0_pv, l0_cx, l0_wo = [sem(n) for n in (
            "l0_score", "l0_max", "l0_turn", "l0_nmt", "l0_st", "l0_exp", "l0_pv", "l0_cx", "l0_wo")]
        l0_vec, l0_masks_vec = sem("l0_vec"), sem("l0_masks_vec")

        def l0x_tensor(pe):
            pe.wait_ge(l0_loaded, 16 * 8)
            with pe.Fori(0, B) as b:
                ln_tensor(pe, b, X[:, b, :])
                pe.wait_ge(l0_ctx, b + 1)
                pe.matmul(PS[:, 3, 0:S2], L0W[:, 1, :], XM_C, start=True, stop=True).then_inc(l0_proj, 1)
                pe.matmul(PS[0:S2, 4, 0:P], XM_C, L0W[:, 2, :], start=True, stop=False)
                pe.matmul(PS[0:S2, 4, 0:P], ONEROW[0:1, 0:S2], BVROW[:, :], start=False, stop=True).then_inc(l0_proj, 1)
                pe.wait_ge(ln_out, b + 2)
                pe.matmul(PS[:, 5, :], L0W[:, 0, :], xn, start=True, stop=True).then_inc(l0_proj, 1)
                pe.wait_ge(l0_q, b + 1)
                pe.wait_ge(l0_kb, b + 1)
                pe.wait_ge(l0_mask, 2 * b + 2)
                for t in range(NT):
                    if t:
                        pe.wait_ge(l0_max, b * NT + t)
                    for g, (h0, h1) in enumerate(HG):
                        o = PS[:, g, 0:(h1 - h0) * S2]
                        pe.matmul(o, XM_Q[:, t * P:(t + 1) * P], XM_KB[:, h0:h1, :], start=True, stop=False)
                        mm = pe.matmul(o, IDB[:, :], over(XM_MQ[:, t, :], h1 - h0),
                                       start=False, stop=True)
                    mm.then_inc(l0_score, 1)
                pe.wait_ge(l0_max, b * NT + NT)
                for t in range(NT):
                    mm = pe.transpose(PS[0:H0, 5, t * P:(t + 1) * P], XM_NM[:, t, :], IDF[:, :])
                mm.then_inc(l0_turn, 1)
                pe.wait_ge(l0_nmt, b + 1)
                pe.wait_ge(l0_v, 2 * b + 2)
                for h in range(H0):
                    o = PS[0:S2, 3 + h % 2, :]
                    if h >= 2:
                        pe.wait_ge(l0_exp, b * H0 + h - 1)
                    pe.matmul(o, XM_KB[:, h, :], XM_Q, start=True, stop=False)
                    pe.matmul(o, IDB[0:S2, 0:S2], XM_MT[0:S2, :], start=False, stop=False)
                    pe.matmul(o, IDF[0:H0, h:h + 1].to_broadcast([H0, S2]), XM_NMT[0:H0, :], start=False, stop=True).then_inc(l0_st, 1)
                    if h >= 1:
                        l0x_pv(pe, b, h - 1)
                l0x_pv(pe, b, H0 - 1)
                pe.wait_ge(l0_cx, 2 * b + 2)
                pe.matmul(PS[:, 0, :], L0W[:, 3, :], XM_CX, start=True, stop=True).then_inc(l0_wo, 1)

        def l0x_pv(pe, b, h):
            pe.wait_ge(l0_exp, b * H0 + h + 1)
            pe.matmul(PS[:, 1 + h // 8, :], XM_VB[0:S2, h * P:(h + 1) * P], XM_P[h % 2][0:S2, :],
                      start=h % 8 == 0, stop=h % 8 == 7).then_inc(l0_pv, 1)

        def l0x_scalar(act):
            with act.Fori(0, B) as b:
                ln_scalar(act, b)
                for h in range(H0):
                    act.wait_ge(l0_st, b * H0 + h + 1)
                    if h >= 2:
                        act.wait_ge(l0_pv, b * H0 + h - 1)
                    act.activation(XM_P[h % 2][0:S2, :], PS[0:S2, 3 + h % 2, :], ACT.Exp).then_inc(l0_exp, 1)

        def l0x_vector(dve):
            st = Steps(dve, l0_masks_vec)
            dve.wait_ge(l0_loaded, 16 * 8)
            st.body(0, 5)
            st.done(dve.tensor_scalar(XM_MQ32, MSK_Q[:, :, :], NEG, None, ALU.mult))
            st.done(dve.tensor_scalar(XM_MT32[0:S2, :], MSK_T[:, :], NEG, None, ALU.mult))
            st.done(dve.tensor_scalar(XM_PADQ, PAD_Q[:, :, :], NEG, None, ALU.mult))
            st.done(dve.tensor_scalar(XM_PADT[0:S2, :], PAD_T[:, :], NEG, None, ALU.mult))
            st.done(dve.memset(XM_VB, 0.0))
            st.settle()
            for h in range(H0):
                at = h * P + 64 + DK0 * (h % 8)
                dve.memset(XM_VB[:, at:at + DK0], 1.0)
            with dve.Fori(0, B) as b:
                st = Steps(dve, l0_vec)
                st.body(b, 2)
                ln_vector(dve, b, X[:, b, :], xn)
                dve.tensor_tensor(XM_MQ, XM_MQ32, over(XM_PADQ[:, b, :], NT), ALU.min).then_inc(l0_mask, 1)
                dve.tensor_scalar(XM_MT[0:S2, :], XM_MT32[0:S2, :], XM_PADT[0:S2, bass.ts(b, 1)], None, ALU.min).then_inc(l0_mask, 1)
                dve.wait_ge(l0_proj, 3 * b + 2)
                dve.tensor_scalar(XM_K, PS[:, 3, 0:S2], L0B[:, 1:2], None, ALU.add).then_inc(l0_k, 1)
                dve.wait_ge(l0_k, b + 1)
                dve.tensor_tensor(XM_KB, over(XM_K, H0),
                                  along(HMASK[:, :], S2),
                                  ALU.mult).then_inc(l0_kb, 1)
                for g in range(2):
                    vg = XM_VB[0:S2, g * 8 * P:g * 8 * P + 8 * VSTEP].rearrange("p (h e) -> p h e", e=VSTEP)[:, :, 0:DK0]
                    dve.tensor_copy(vg, PS[0:S2, 4, g * 64:(g + 1) * 64].rearrange("p (h e) -> p h e", e=DK0)).then_inc(l0_v, 1)
                dve.wait_ge(l0_proj, 3 * b + 3)
                dve.tensor_scalar(XM_Q, PS[:, 5, :], L0B[:, 0:1], DK0 ** -0.5, ALU.add, ALU.mult).then_inc(l0_q, 1)
                for t in range(NT):
                    dve.wait_ge(l0_score, b * NT + t + 1)
                    for g, (h0, h1) in enumerate(HG):
                        ins = dve.tensor_reduce(XM_NM[:, t, h0:h1],
                                                PS[:, g, 0:(h1 - h0) * S2].rearrange("p (h k) -> p h k", k=S2),
                                                AX, ALU.max, negate=True)
                    ins.then_inc(l0_max, 1)
                dve.wait_ge(l0_turn, b + 1)
                dve.tensor_copy(XM_NMT[0:H0, :], PS[0:H0, 5, :]).then_inc(l0_nmt, 1)
                for g in range(2):
                    dve.wait_ge(l0_pv, b * H0 + 8 * g + 8)
                    if g:
                        dve.wait_ge(l0_cx, 2 * b + g)
                    st.done(dve.reciprocal(XM_RC[0:64, :], PS[64:P, 1 + g, :]))
                    st.settle()
                    dve.tensor_tensor(XM_CX[64 * g:64 * g + 64, :], PS[0:64, 1 + g, :], XM_RC[0:64, :],
                                      ALU.mult).then_inc(l0_cx, 1)
                dve.wait_ge(l0_wo, b + 2)
                dve.scalar_tensor_tensor(out=X[:, b, :], in0=PS[:, 0, :], scalar=L0B[:, 2:3], in1=X[:, b, :],
                                         op0=ALU.add, op1=ALU.add).then_inc(x_done, 1)
                st.end()

        def l0x_pool(pool):
            pool.wait_ge(x_loaded, 16)
            pool.memset(XM_C, 0.0).then_inc(l0_wo, 1)
            with pool.Fori(0, B) as b:
                pool.wait_ge(l0_wo, b + 1)
                pool.tensor_copy(XM_C, CT[:, b, :]).then_inc(l0_ctx, 1)

        NE, CAP = 8, 128
        MOEW = sb("MOEW", [P, 8192])
        GW0 = sb("GW0", [P, NE])
        E_G = MOEW[:, 0:2048].rearrange("p (e c m) -> p e c m", e=NE, c=2)
        E_U = MOEW[:, 2048:4096].rearrange("p (e c m) -> p e c m", e=NE, c=2)
        E_D = MOEW[:, 4096:6144].rearrange("p (e c m) -> p e c m", e=NE, c=2)
        l0f_loaded = sem("l0f_loaded")
        c = carver()
        F_XA = c(B * T).rearrange("p (b n) -> p b n", b=B)
        F_E = c(NT * NE).rearrange("p (t e) -> p t e", t=NT)
        F_M = c(NT)
        F_S = c(NT)
        F_R = c(NT)
        F_AFF = c(NT * B * NE).rearrange("p (t j) -> p t j", t=NT)
        F_A = c(T)
        F_W = c(T)
        F_M8 = c(8)
        F_G = c(T)
        F_GB = c(B * T).rearrange("p (b n) -> p b n", b=B)
        F_GS = c(T)
        F_SG = [c(T), c(T)]
        F_T = [c(T), c(T)]
        F_H = [c(T), c(T)]
        f_logit, f_neg, f_sub, f_exp, f_sum, f_aff, f_xa, f_turn, f_gate, f_gb = [sem(n) for n in (
            "f_logit", "f_neg", "f_sub", "f_exp", "f_sum", "f_aff", "f_xa", "f_turn", "f_gate", "f_gb")]
        f_gs = sem("f_gs")
        f_bc, f_gu, f_silu, f_h, f_down, f_vec, f_topk = [sem(n) for n in (
            "f_bc", "f_gu", "f_silu", "f_h", "f_down", "f_vec", "f_topk")]
        N0 = NE * 2

        def l0f_tensor(pe):
            pe.wait_ge(l0f_loaded, 16 * 4)
            with pe.Fori(0, B) as b:
                ln_tensor(pe, b + 4, X[:, b, :])
                pe.wait_ge(ln_out, b + 6)
                for t in range(NT):
                    mm = pe.matmul(PS[:, 0, t * NE:(t + 1) * NE], xn[:, t * P:(t + 1) * P], GW0[:, :], start=True, stop=True)
                mm.then_inc(f_logit, 1)
            pe.wait_ge(f_aff, B)
            for t in range(NT):
                mm = pe.transpose(PS[0:B * NE, 1, t * P:(t + 1) * P], F_AFF[:, t, :], IDF[:, :])
            mm.then_inc(f_turn, 1)
            pe.wait_ge(f_xa, B)
            with pe.Fori(0, B) as b:
                pe.wait_ge(f_gs, b + 1)
                for i in range(N0):
                    e, h = i // 2, i % 2
                    if h == 0:
                        if e >= 2:
                            pe.wait_ge(f_h, b * N0 + 2 * (e - 1))
                        pe.matmul(PS[:, 5 * (e % 2), :], IDF[0:NE, e:e + 1].to_broadcast([NE, P]), F_GS[0:NE, :], start=True, stop=True).then_inc(f_bc, 1)
                    if i >= 2:
                        pe.wait_ge(f_h, b * N0 + i - 1)
                    pe.matmul(PS[:, 2 + i % 2, :], E_G[:, e, h, :], F_XA[:, b, :], start=True, stop=True)
                    pe.matmul(PS[:, [4, 6][i % 2], :], E_U[:, e, h, :], F_XA[:, b, :], start=True, stop=True).then_inc(f_gu, 1)
                    if i >= 1:
                        l0f_down(pe, b, i - 1)
                l0f_down(pe, b, N0 - 1)

        def l0f_down(pe, b, i):
            pe.wait_ge(f_h, b * N0 + i + 1)
            pe.matmul(PS[:, 1, :], E_D[:, i // 2, i % 2, :], F_H[i % 2], start=i == 0, stop=i == N0 - 1).then_inc(f_down, 1)

        def l0f_scalar(act):
            with act.Fori(0, B) as b:
                ln_scalar(act, b + 4)
                act.wait_ge(f_sub, b + 1)
                act.activation(F_E, F_E, ACT.Exp).then_inc(f_exp, 1)
            with act.Fori(0, B) as b:
                for i in range(N0):
                    act.wait_ge(f_gu, b * N0 + i + 1)
                    if i >= 2:
                        act.wait_ge(f_h, b * N0 + i - 1)
                    act.activation(F_SG[i % 2], PS[:, 2 + i % 2, :], ACT.Silu).then_inc(f_silu, 1)

        def l0f_vector(dve):
            st = Steps(dve, f_vec)
            with dve.Fori(0, B) as b:
                st.body(b, 2)
                ln_vector(dve, b + 4, X[:, b, :], xn)
                dve.wait_ge(f_logit, b + 1)
                lg = PS[:, 0, 0:NT * NE].rearrange("p (t e) -> p t e", t=NT)
                dve.tensor_reduce(F_M, lg, AX, ALU.max, negate=True).then_inc(f_neg, 1)
                dve.wait_ge(f_neg, b + 1)
                dve.tensor_tensor(F_E, lg, along(F_M, NE), ALU.add).then_inc(f_sub, 1)
                dve.wait_ge(f_exp, b + 1)
                st.done(dve.tensor_reduce(F_S, F_E, AX, ALU.add))
                st.settle()
                st.done(dve.reciprocal(F_R, F_S))
                st.settle()
                dve.tensor_tensor(F_AFF[:, :, bass.ts(b, NE)], F_E, along(F_R, NE), ALU.mult).then_inc(f_aff, 1)
                dve.wait_ge(f_aff, b + 1)
                dve.wait_ge(f_xa, b + 1)
                st.end()
            dve.wait_ge(f_turn, 1)
            tk = Steps(dve, f_topk)
            tk.done(dve.tensor_copy(F_A[0:B * NE, :], PS[0:B * NE, 1, :]))
            tk.done(dve.tensor_copy(F_W[0:B * NE, :], PS[0:B * NE, 1, :]))
            tk.settle()
            for r in range(CAP // 8):
                tk.done(dve.max(F_M8[0:B * NE, :], F_W[0:B * NE, :]))
                tk.settle()
                tk.done(dve.match_replace(out=F_W[0:B * NE, :], in_to_replace=F_M8[0:B * NE, :], in_values=F_W[0:B * NE, :], imm_value=-1.0))
                tk.settle()
            dve.scalar_tensor_tensor(out=F_G[0:B * NE, :], in0=F_W[0:B * NE, :], scalar=0.0, in1=F_A[0:B * NE, :],
                                     op0=ALU.is_lt, op1=ALU.mult).then_inc(f_gate, 1)
            with dve.Fori(0, B) as b:
                for i in range(N0):
                    dve.wait_ge(f_silu, b * N0 + i + 1)
                    st2 = F_T[i % 2]
                    dve.tensor_tensor(st2, F_SG[i % 2], PS[:, [4, 6][i % 2], :], ALU.mult).then_inc(f_neg, 1)
                    dve.wait_ge(f_neg, b * N0 + i + 1 + B)
                    dve.wait_ge(f_bc, b * NE + i // 2 + 1)
                    if i >= 2:
                        dve.wait_ge(f_down, b * N0 + i - 1)
                    dve.tensor_tensor(F_H[i % 2], st2, PS[:, 5 * (i // 2 % 2), :], ALU.mult).then_inc(f_h, 1)
                dve.wait_ge(f_down, (b + 1) * N0)
                dve.tensor_tensor(X[:, b, :], X[:, b, :], PS[:, 1, :], ALU.add).then_inc(x_done, 1)

        def l0f_pool(pool):
            with pool.Fori(0, B) as b:
                pool.wait_ge(ln_out, b + 6)
                pool.tensor_copy(F_XA[:, b, :], xn).then_inc(f_xa, 1)
            pool.wait_ge(f_gb, 16 * B)
            with pool.Fori(0, B) as b:
                pool.wait_ge(x_done, b + 4)
                pool.tensor_copy(F_GS[0:NE, :], F_GB[0:NE, b, :]).then_inc(f_gs, 1)

        L1W = sb("L1W", [P, 7, P])
        L1CW = sb("L1CW", [P, 2])
        L1G = sb("L1G", [P, 1])
        PTR_I = sb("PTR_I", [P, B * NT], I32)
        IDS_I = sb("IDS_I", [P, B, S2], I32)
        IOTA = sb("IOTA", [P, S2])
        l1x_loaded = sem("l1x_loaded")
        c = carver()
        A_C = c(S2)
        A_Q = c(2 * T).rearrange("p (j n) -> p j n", j=2)
        A_K = c(2 * S2).rearrange("p (j k) -> p j k", j=2)
        A_V = c(2 * P).rearrange("p (j d) -> p j d", j=2)
        A_PTR = c(B * NT)
        A_IX = c(3 * B * NT).rearrange("p (w b t) -> p w b t", w=3, b=B)
        A_IDS = c(B * S2).rearrange("p (b k) -> p b k", b=B)
        A_OH = c(3 * NT * S2).rearrange("p (w k) -> p w k", w=3 * NT)
        A_T = c(3 * NT * S2).rearrange("p (w k) -> p w k", w=3 * NT)
        A_L = c(2 * 3 * NT).rearrange("p (j w) -> p j w", j=2)
        A_N = c(16 * NT).rearrange("p (i t) -> p i t", t=NT)
        A_M = c(2 * NT).rearrange("p (j t) -> p j t", j=2)
        A_P = c(2 * NT * S2).rearrange("p (j t k) -> p j t k", j=2, t=NT)
        A_PT = c(2 * T).rearrange("p (j n) -> p j n", j=2)
        A_CX = c(T)
        A_W = c(2)
        A_WM = c(4)
        a_ctx, a_proj, a_q, a_kv, a_score, a_sub, a_exp, a_p, a_turn, a_pt, a_cx, a_cxs, a_out, a_vec, a_pre, a_we = [
            sem(n) for n in ("a_ctx", "a_proj", "a_q", "a_kv", "a_score", "a_sub", "a_exp", "a_p", "a_turn", "a_pt",
                             "a_cx", "a_cxs", "a_out", "a_vec", "a_pre", "a_we")]
        PSC = PS[:, 0:2, :].rearrange("p g (u j z) -> p (g u) j z", u=2, j=2)[:, :, :, 0:S2]

        def l1x_tensor(pe):
            pe.wait_ge(l1x_loaded, 16 * 6)
            with pe.Fori(0, B) as b:
                ln_tensor(pe, b + 8, X[:, b, :])
                pe.wait_ge(a_ctx, b + 1)
                for j in range(2):
                    pe.matmul(PS[:, 4, j * P:j * P + S2], L1W[:, 2 + j, :], A_C, start=True, stop=True)
                for j in range(2):
                    mm = pe.matmul(PS[0:S2, 5, j * P:(j + 1) * P], A_C, L1W[:, 4 + j, :], start=True, stop=True)
                mm.then_inc(a_proj, 1)
                pe.wait_ge(ln_out, b + 10)
                for j in range(2):
                    mm = pe.matmul(PS[:, 2 + j, :], L1W[:, j, :], xn, start=True, stop=True)
                mm.then_inc(a_proj, 1)
                pe.wait_ge(a_q, 2 * b + 2)
                pe.wait_ge(a_kv, b + 1)
                for t in range(NT):
                    for j in range(2):
                        mm = pe.matmul(PSC[:, t, j, :], A_Q[:, j, t * P:(t + 1) * P], A_K[:, j, :], start=True, stop=True)
                mm.then_inc(a_score, 1)
                pe.wait_ge(a_p, b + 1)
                for j in range(2):
                    for t in range(NT):
                        mm = pe.transpose(PS[0:S2, 2 + j, t * P:(t + 1) * P], A_P[:, j, t, :], IDF[:, :])
                mm.then_inc(a_turn, 1)
                pe.wait_ge(a_pt, 2 * b + 2)
                for j in range(2):
                    mm = pe.matmul(PS[:, 4, :], A_V[0:S2, j, :], A_PT[0:S2, j, :], start=j == 0, stop=j == 1)
                mm.then_inc(a_cx, 1)
                pe.wait_ge(a_cxs, b + 1)
                pe.matmul(PS[:, 5, :], L1W[:, 6, :], A_CX, start=True, stop=True).then_inc(a_out, 1)

        def l1x_scalar(act):
            act.wait_ge(a_sub, 1)
            act.activation(A_W, A_W, ACT.Exp).then_inc(a_we, 1)
            with act.Fori(0, B) as b:
                ln_scalar(act, b + 8)
                act.wait_ge(a_proj, 2 * b + 2)
                for j in range(2):
                    act.activation(A_Q[:, j, :], PS[:, 2 + j, :], ACT.Copy, scale=P ** -0.5).then_inc(a_q, 1)
                act.wait_ge(a_sub, b + 2)
                act.activation(A_L, A_L, ACT.Exp).then_inc(a_exp, 1)
                act.wait_ge(a_turn, b + 1)
                for j in range(2):
                    act.activation(A_PT[0:S2, j, :], PS[0:S2, 2 + j, :], ACT.Copy).then_inc(a_pt, 1)
                act.wait_ge(a_cx, b + 1)
                act.activation(A_CX, PS[:, 4, :], ACT.Copy).then_inc(a_cxs, 1)

        def l1x_vector(dve):
            dve.wait_ge(l1x_loaded, 16 * 6)
            pre = Steps(dve, a_pre)

            def once(ins):
                pre.done(ins)
                pre.settle()
            once(dve.tensor_reduce(A_WM[:, 0:1], L1CW[:, :], AX, ALU.max, negate=True))
            dve.tensor_scalar(A_W, L1CW[:, :], A_WM[:, 0:1], None, ALU.add).then_inc(a_sub, 1)
            dve.wait_ge(a_we, 1)
            once(dve.tensor_reduce(A_WM[:, 1:2], A_W, AX, ALU.add))
            once(dve.reciprocal(A_WM[:, 2:3], A_WM[:, 1:2]))
            once(dve.tensor_scalar(A_W, A_W, A_WM[:, 2:3], None, ALU.mult))
            once(dve.tensor_copy(A_PTR, PTR_I[:, :]))
            once(dve.tensor_copy(A_IDS, IDS_I[:, :, :]))
            for w in range(3):
                ix = A_IX[:, w, :, :]
                once(dve.tensor_scalar(ix, A_PTR.rearrange("p (b t) -> p b t", b=B), float(w), float(S2 - 1), ALU.add, ALU.min))
                once(dve.tensor_scalar(ix, ix, 0.0, None, ALU.max))
            st = Steps(dve, a_vec)
            with dve.Fori(0, B) as b:
                st.body(b, 45)

                def step(ins):
                    st.done(ins)
                    st.settle()
                ln_vector(dve, b + 8, X[:, b, :], xn)
                dve.wait_ge(a_proj, 2 * b + 1)
                step(dve.tensor_copy(A_K, PS[:, 4, 0:2 * P].rearrange("p (j z) -> p j z", j=2)[:, :, 0:S2]))
                for j in range(2):
                    ins = dve.tensor_scalar(A_V[0:S2, j, :], PS[0:S2, 5, j * P:(j + 1) * P], A_W[0:S2, j:j + 1], None, ALU.mult)
                    if j == 0:
                        step(ins)
                ins.then_inc(a_kv, 1)
                for w in range(3):
                    step(dve.tensor_tensor(A_OH[:, w * NT:(w + 1) * NT, :], over(IOTA[:, :], NT), along(A_IX[:, w, b, :], S2), ALU.is_equal))
                step(dve.tensor_tensor(A_T[:, 0:NT, :], A_OH[:, 0:NT, :], over(A_IDS[:, b, :], NT), ALU.mult))
                rel, acc = A_N[:, 0, :], A_N[:, 1, :]
                step(dve.tensor_reduce(rel, A_T[:, 0:NT, :], AX, ALU.add))
                dve.wait_ge(a_score, b + 1)
                for j in range(2):
                    s = PSC[:, :, j, :].rearrange("p t (o k) -> p o t k", o=1).to_broadcast([P, 3, NT, S2])
                    step(dve.tensor_tensor(A_T.rearrange("p (w t) k -> p w t k", w=3), A_OH.rearrange("p (w t) k -> p w t k", w=3), s, ALU.mult))
                    step(dve.tensor_reduce(A_L[:, j, :], A_T, AX, ALU.add))
                l_rel, v1, v2 = [A_L[:, 0, w * NT:(w + 1) * NT] for w in range(3)]
                plus, most, less, imply, diff, xor = [A_N[:, i, :] for i in range(2, 8)]
                none, tmp = A_N[:, 8, :], A_N[:, 9, :]
                step(dve.tensor_tensor(plus, v1, v2, ALU.add))
                step(dve.tensor_tensor(most, v1, v2, ALU.max))
                step(dve.tensor_scalar(less, v1, -1.0, None, ALU.mult))
                step(dve.tensor_tensor(imply, less, v2, ALU.max))
                step(dve.tensor_tensor(diff, v1, v2, ALU.subtract))
                step(dve.scalar_tensor_tensor(out=xor, in0=diff, scalar=-1.0, in1=diff, op0=ALU.mult, op1=ALU.max))
                step(dve.tensor_scalar(tmp, rel, 4.0, None, ALU.is_gt))
                step(dve.scalar_tensor_tensor(out=none, in0=rel, scalar=0.0, in1=tmp, op0=ALU.is_lt, op1=ALU.max))
                step(dve.tensor_tensor(acc, none, l_rel, ALU.mult))
                for rule, term in enumerate((plus, most, less, imply, xor)):
                    step(dve.scalar_tensor_tensor(out=tmp, in0=rel, scalar=float(rule), in1=term, op0=ALU.is_equal, op1=ALU.mult))
                    step(dve.tensor_tensor(l_rel if rule == 4 else acc, acc, tmp, ALU.add))
                L = A_L.rearrange("p j (w t) -> p j w t", w=3)
                step(dve.tensor_tensor(A_M, L[:, :, 0, :], L[:, :, 1, :], ALU.max))
                step(dve.tensor_tensor(A_M, A_M, L[:, :, 2, :], ALU.max))
                for w in range(3):
                    ins = dve.tensor_tensor(L[:, :, w, :], L[:, :, w, :], A_M, ALU.subtract)
                    if w < 2:
                        step(ins)
                ins.then_inc(a_sub, 1)
                dve.wait_ge(a_exp, b + 1)
                step(dve.tensor_tensor(A_M, L[:, :, 0, :], L[:, :, 1, :], ALU.add))
                step(dve.tensor_tensor(A_M, A_M, L[:, :, 2, :], ALU.add))
                step(dve.reciprocal(A_M, A_M))
                for w in range(3):
                    step(dve.tensor_tensor(L[:, :, w, :], L[:, :, w, :], A_M, ALU.mult))
                for j in range(2):
                    step(dve.tensor_tensor(A_T, A_OH, along(A_L[:, j, :], S2), ALU.mult))
                    step(dve.tensor_tensor(A_P[:, j, :, :], A_T[:, 0:NT, :], A_T[:, NT:2 * NT, :], ALU.add))
                    ins = dve.tensor_tensor(A_P[:, j, :, :], A_P[:, j, :, :], A_T[:, 2 * NT:3 * NT, :], ALU.add)
                    if j == 0:
                        step(ins)
                ins.then_inc(a_p, 1)
                dve.wait_ge(a_out, b + 1)
                dve.scalar_tensor_tensor(out=X[:, b, :], in0=PS[:, 5, :], scalar=L1G[:, 0:1], in1=X[:, b, :],
                                         op0=ALU.mult, op1=ALU.add).then_inc(x_done, 1)
                st.end()

        def l1x_pool(pool):
            with pool.Fori(0, B) as b:
                pool.wait_ge(x_done, b + 8)
                pool.tensor_copy(A_C, CT[:, b, :]).then_inc(a_ctx, 1)

        DEPTH, NH, DH, WIN = 6, 16, 64, 32
        NPAIR = NH // 2
        DI = 341
        FF = [(0, 128), (128, 128), (256, DI - 256)]
        SPAN = P + WIN
        Y = sb("Y", [P, B, T + 1])
        WQKV = sb("WQKV", [P, 2 * 3 * T])
        W_QKV = WQKV[:, :].rearrange("p (g s n) -> p g s n", g=2, s=3)
        WO = sb("WO", [P, NPAIR, P])
        W1 = sb("W1", [P, 2 * DI])
        W2 = sb("W2", [P, 3, P])
        LNGB = sb("LNGB", [P, 2])
        B1 = sb("B1", [P, 3, 2])
        B2 = sb("B2", [P, 1])
        ROPE = sb("ROPE", [P, 4, NT, DH])
        QKS = sb("QKS", [P, 4, DH])
        BANDS = sb("BANDS", [P, 3, SPAN], BF16)
        BANDS32 = sb("BANDS32", [P, 3, SPAN])
        V_ALL = MOEW[:, :].rearrange("p (t h e) -> p t h e", t=NT, h=NH)
        NMSEL = sb("NMSEL", [P, 8], BF16)
        l1_const, w_qkv, w_o, w_ff, w_qks = sem("l1_const"), [sem("w_qkv0"), sem("w_qkv1")], sem("w_o"), sem("w_ff"), sem("w_qks")
        c = carver()
        L_SH = c(T)
        L_TAB = c(4 * NT * DH).rearrange("p (i t d) -> p i t d", i=4, t=NT)
        L_QT = c(NPAIR * (T + WIN)).rearrange("p (h n) -> p h n", h=NPAIR)
        L_KT = c(NPAIR * (WIN + T)).rearrange("p (h n) -> p h n", h=NPAIR)
        L_QB = c(4 * T, BF16).rearrange("p (h n) -> p h n", h=4)
        L_KB = c(4 * (WIN + T), BF16).rearrange("p (h n) -> p h n", h=4)
        L_CX = c(NPAIR * T).rearrange("p (h n) -> p h n", h=NPAIR)
        L_P = [c(NT * SPAN).rearrange("p (t n) -> p t n", t=NT) for _ in range(4)]
        L_DN = [c(T), c(T)]
        L_NM = c(NT * 8).rearrange("p (t h) -> p t h", t=NT)
        L_NMB = c(T + WIN, BF16)
        L_ONE = c(1)
        L_ONE4 = L_ONE.rearrange("p (o u) -> p o u", o=1)
        L_SS, L_SD = c(64), c(64)
        L_RAW, L_SQ, L_T2 = [[c(T), c(T)] for _ in range(3)]
        L_QK = [c(T) for _ in range(8)]
        L_SF = L_CX[:, 0, :]
        L_XG = L_CX[:, 1, :]
        L_G = [L_CX[:, 2 + m, :] for m in range(3)]
        L_H = [L_CX[:, 5 + m, :] for m in range(3)]
        (p_sh, p_proj, p_raw, p_sq, p_t1, p_t12, p_add, p_ss, p_sd, p_rn, p_qk, p_turn, p_tev, p_cast, p_v, p_s, p_max,
         p_st, p_exp, p_pv, p_den, p_rd, p_cx, p_out, p_y, p_sf, p_xg, p_ga, p_gelu, p_h, p_tab, p_pre) = [
            sem("p_" + n) for n in (
                "sh proj raw sq t1 t12 add ss sd rn qk turn tev cast v s max "
                "st exp pv den rd cx out y sf xg ga gelu h tab pre").split()]
        PROJ, TURN, PV0 = 4, 5, 6
        FFB = [(0, 1), (2, 3), (6, 7)]
        NJ, NV = 8, NT
        NP = NJ + NV
        NPT = 20

        ORDER = [
            "P0 S0 P1 S1 P2 S2 P3 S3 P4 M P5 P6 T0 P7 D0 C0 P8 T1 P9 C1 P10 T2 P11 C2 P12 D1 P13 T3 P14 P15 C3 D2 P16 P17 P18 P19 D3",
            "S0 N S1 P0 S2 P1 S3 P2 M P3 P4 D0 T0 P5 T1 D1 D2 C0 T2 C1 C2 D3 T3 P6 C3 P7 P8 P9 F0 P10 P11 F1 P12 P13 F2 P14 P15 F3 P16 P17 F4 P18 F5 P19",
        ]

        def order(g, projecting):
            return [(w[0], int(w[1:] or 0)) for w in ORDER[g].split() if projecting or w[0] not in "PN"]

        def through_units(eng, body):
            nc.disable_value_cache = True
            with eng.Fori(0, DEPTH - 1) as l:
                with eng.Fori(0, B - 1) as b:
                    body(l * B + b, b, l, b + 1, l, False)
                body(l * B + B - 1, B - 1, l, 0, l + 1, True)
            with eng.Fori(0, B - 1) as b:
                body((DEPTH - 1) * B + b, b, DEPTH - 1, b + 1, DEPTH - 1, False)
            body(DEPTH * B - 1, B - 1, DEPTH - 1, None, DEPTH, False)
            nc.disable_value_cache = False

        def score_tiles(g):
            return PS[:, 2 * g:2 * g + 2, :].rearrange("p g (u z) -> p (g u) z", u=2)[:, :, 0:SPAN]

        def is_first(u):
            return isinstance(u, int) and u == 0

        def turn_bank(j):
            return PROJ if j >= 3 and j % 2 else TURN

        def half(h):
            return slice(DH * (h % 2), DH * (h % 2) + DH)

        def l1f_tensor(pe):
            with pe.Fori(0, B) as b:
                ln_tensor(pe, b + 12, X[:, b, :])
            pe.wait_ge(p_pre, 8)
            pe.wait_ge(ln_out, 17)
            for p in range(NPT):
                l1f_project(pe, 0, 0, 0, 0, p)

            def body(i, b, l, nb, nl, new_layer):
                for g in range(2):
                    u = 2 * i + g
                    for what, n in order(g, g == 0 or nb is not None):
                        if what == "P":
                            l1f_project(pe, u + 1, 1 - g, i + g, nl if g else l, n)
                        elif what == "S":
                            if n == 0:
                                pe.wait_ge(p_cast, 8 * u + 8)
                                pe.wait_ge(p_v, NV * u + NV)
                                if g == 0:
                                    pe.wait_ge(p_y, 2 * i + 1)
                            else:
                                pe.wait_ge(p_max, 10 * u + 2 * n)
                            for t in range(NT):
                                for v in range(2):
                                    r = half(v)
                                    pe.matmul(score_tiles(v)[:, t, :], L_QB[r, n, t * P:(t + 1) * P], L_KB[r, n, t * P:t * P + SPAN],
                                              start=t % 2 == 0, stop=False, skip_group_check=True)
                            for v in range(2):
                                for t in range(NT):
                                    mm = pe.matmul(score_tiles(v)[:, t, :], IDB[:, :], BANDS[:, 1 if t else 0, :],
                                                   start=False, stop=t % 2 == 1, skip_group_check=True)
                                mm.then_inc(p_s, 1)
                        elif what == "M":
                            pe.wait_ge(p_max, 10 * u + 8)
                            if g == 1:
                                pe.wait_ge(p_den, 8 * u)
                            for t in range(NT):
                                mm = pe.transpose(PS[0:8, PV0, t * P:(t + 1) * P], L_NM[:, t, :], IDF[:, :])
                            mm.then_inc(p_s, 1)
                        elif what == "T":
                            if n == 0:
                                pe.wait_ge(p_max, 10 * u + 10)
                            else:
                                pe.wait_ge(p_exp, 8 * u + 2 * n)
                            pair = 4 * g + n
                            for t in range(NT):
                                for v in range(2):
                                    r = half(v)
                                    pe.matmul(score_tiles(v)[:, t, :], L_KT[r, pair, WIN + t * P:WIN + (t + 1) * P],
                                              L_QT[r, pair, t * P:t * P + SPAN], start=t % 2 == 0, stop=False,
                                              skip_group_check=True)
                            for v in range(2):
                                s, h = score_tiles(v), 2 * n + v
                                for t in range(NT):
                                    pe.matmul(s[:, t, :], IDB[:, :], BANDS[:, 2, :], start=False, stop=False, skip_group_check=True)
                                    mm = pe.matmul(s[:, t, :], NMSEL[:, h:h + 1].to_broadcast([P, P]), L_NMB[:, t * P:t * P + SPAN],
                                                   start=False, stop=t % 2 == 1, skip_group_check=True)
                                mm.then_inc(p_st, 1)
                        elif what == "C":
                            l1f_pv(pe, u, g, 2 * n)
                            l1f_pv(pe, u, g, 2 * n + 1)
                        elif what == "F":
                            l1f_ff_tensor(pe, i, l, n)
            through_units(pe, body)

        def l1f_project(pe, u, g, i, l, p):
            if p < NP:
                if p == 0:
                    pe.wait_ge(w_qkv[g], 16 * l + 16)
                    pe.wait_ge(p_sh, i + 1)
                    if not is_first(u):
                        pe.wait_ge(p_tev, NJ * u)
                elif p <= NJ:
                    pe.wait_ge(p_raw, NJ * u + p)
                else:
                    pe.wait_ge(p_v, NV * u + p - NJ)
                t, q = (p // 2, p % 2) if p < NJ else (p - NJ, 2)
                pe.matmul(PS[:, PROJ, :], L_SH[:, t * P:(t + 1) * P], W_QKV[:, g, q, :], start=True, stop=True).then_inc(p_proj, 1)
            j = p - 10
            if 0 <= j < NJ:
                pe.wait_ge(p_qk, NJ * u + j + 1)
                if j in (1, 2) or (j == 0 and not is_first(u)):
                    pe.wait_ge(p_tev, NJ * u + j)
                elif j == 3:
                    pe.wait_ge(p_v, NV * u + NV)
                elif j >= 4:
                    pe.wait_ge(p_tev, NJ * u + j - 1)
                for h in range(4):
                    mm = pe.transpose(PS[:, turn_bank(j), h * P:(h + 1) * P], L_QK[j][:, h * P:(h + 1) * P], IDF[:, :])
                mm.then_inc(p_turn, 1)

        def l1f_pv(pe, u, g, h):
            pe.wait_ge(p_exp, 8 * u + h + 1)
            if h >= 2:
                pe.wait_ge(p_den, 8 * u + h - 1)
            for t in range(NT):
                w = min(SPAN, T - t * P)
                mm = pe.matmul(PS[:, PV0 + h % 2, t * P:t * P + w], V_ALL[:, t, 8 * g + h, :], L_P[h % 4][:, t, 0:w],
                               start=t == 0, stop=t == NT - 1, skip_group_check=True)
            mm.then_inc(p_pv, 1)

        def l1f_ff_tensor(pe, i, l, s):
            if s == 0:
                pe.wait_ge(w_o, 16 * l + 16)
                pe.wait_ge(p_cx, 8 * i + 8)
                for h in range(NPAIR):
                    mm = pe.matmul(PS[:, 0, :], WO[:, h, :], L_CX[:, h, :], start=h == 0, stop=h == NPAIR - 1)
                mm.then_inc(p_out, 1)
            elif s == 1:
                pe.wait_ge(p_sf, i + 1)
                ln_tensor_mean(pe, i + 16, L_SF)
            elif s == 2:
                ln_tensor_var(pe, i + 16)
            elif s == 3:
                ln_tensor_out(pe, i + 16)
            elif s == 4:
                pe.wait_ge(w_ff, 112 * l + 112)
                pe.wait_ge(p_xg, i + 1)
                for m, (m0, mw) in enumerate(FF):
                    pe.matmul(PS[0:mw, FFB[m][0], :], W1[:, DI + m0:DI + m0 + mw], L_XG, start=True, stop=True)
                    pe.matmul(PS[0:mw, FFB[m][1], :], W1[:, m0:m0 + mw], L_XG, start=True, stop=True).then_inc(p_ga, 1)
            else:
                for m, (m0, mw) in enumerate(FF):
                    pe.wait_ge(p_h, 3 * i + m + 1)
                    mm = pe.matmul(PS[:, 0, :], W2[0:mw, m, :], L_H[m][0:mw, :], start=m == 0, stop=m == 2)
                mm.then_inc(p_out, 1)

        def l1f_scalar(act):
            with act.Fori(0, B) as b:
                ln_scalar(act, b + 12)
            for p in range(NPT):
                l1f_project_scalar(act, 0, 0, p)

            def body(i, b, l, nb, nl, new_layer):
                for g in range(2):
                    u = 2 * i + g
                    for what, n in order(g, g == 0 or nb is not None):
                        if what == "P":
                            l1f_project_scalar(act, u + 1, 1 - g, n)
                        elif what == "T":
                            for h in (2 * n, 2 * n + 1):
                                act.wait_ge(p_st, 8 * u + h + 1)
                                if h >= 4:
                                    act.wait_ge(p_pv, 8 * u + h - 3)
                                act.activation(L_P[h % 4], score_tiles(h % 2), ACT.Exp).then_inc(p_exp, 1)
                        elif what == "C":
                            l1f_leave(act, u, g, 2 * n)
                            l1f_leave(act, u, g, 2 * n + 1)
                        elif what == "F" and n == 1:
                            ln_scalar_square(act, i + 16)
                        elif what == "F" and n == 2:
                            ln_scalar_sd(act, i + 16)
                        elif what == "F" and n == 4:
                            for m, (m0, mw) in enumerate(FF):
                                act.wait_ge(p_ga, 3 * i + m + 1)
                                act.activation(L_G[m][0:mw, :], PS[0:mw, FFB[m][0], :], ACT.Gelu, bias=B1[0:mw, m, 1:2]).then_inc(p_gelu, 1)
            through_units(act, body)

        def l1f_project_scalar(act, u, g, p):
            if p < NP:
                act.wait_ge(p_proj, NP * u + p + 1)
            if p < NJ:
                if p >= 2 or not is_first(u):
                    act.wait_ge(p_ss, NJ * u + p - 1)
                act.activation(L_SQ[p % 2], PS[:, PROJ, :], ACT.Square).then_inc(p_sq, 1)
                if p >= 2 or not is_first(u):
                    act.wait_ge(p_add, NJ * u + p - 1)
                act.activation(L_RAW[p % 2], PS[:, PROJ, :], ACT.Copy).then_inc(p_raw, 1)
            elif p < NP:
                src = PS[:, PROJ, :].rearrange("p (h u d) -> p h u d", u=2, d=DH)
                dst = V_ALL[:, p - NJ, 8 * g:8 * g + 8, :].rearrange("p (h u) e -> p h u e", u=2)
                act.activation(dst[:, :, 0, 0:DH], src[:, :, 0, :], ACT.Copy)
                act.activation(dst[:, :, 1, DH:P], src[:, :, 1, :], ACT.Copy).then_inc(p_v, 1)
            if p == NJ:
                act.wait_ge(p_ss, NJ * u + NJ)
                act.activation(L_SD, L_SS, ACT.Sqrt).then_inc(p_sd, 1)
            j = p - 10
            if 0 <= j < NJ:
                t, dst = j // 2, (L_QT, L_KT)[j % 2]
                t0 = t * P + (WIN if j % 2 else 0)
                act.wait_ge(p_turn, NJ * u + j + 1)
                act.activation(dst[:, 4 * g:4 * g + 4, t0:t0 + P], PS[:, turn_bank(j), :].rearrange("p (h n) -> p h n", h=4),
                               ACT.Copy).then_inc(p_tev, 1)

        def l1f_leave(act, u, g, h):
            act.wait_ge(p_pv, 8 * u + h + 1)
            k = h // 2
            if h % 2 == 0 and (g == 1 or k >= 2):
                act.wait_ge(p_cx, 4 * u + k - 1)
            r, other = half(h), half(h + 1)
            act.activation(L_DN[k % 2][r, :], PS[other, PV0 + h % 2, :], ACT.Copy)
            act.activation(L_CX[r, 4 * g + k, :], PS[r, PV0 + h % 2, :], ACT.Copy).then_inc(p_den, 1)

        def l1f_vector(dve):
            dve.wait_ge(l1_const, 16 * 2)
            dve.memset(Y[:, :, 0:1], 0.0).then_inc(p_y, 1)
            dve.memset(L_KT[:, :, 0:WIN], 0.0).then_inc(p_pre, 1)
            dve.memset(L_KB[:, :, 0:WIN], 0.0).then_inc(p_pre, 1)
            dve.memset(V_ALL, 1.0).then_inc(p_pre, 1)
            dve.memset(L_NMB, 0.0).then_inc(p_pre, 1)
            dve.memset(L_ONE, 1.0).then_inc(p_pre, 1)
            dve.memset(L_QT[:, :, T:T + WIN], 0.0).then_inc(p_pre, 1)
            dve.tensor_copy(BANDS[:, :, :], BANDS32[:, :, :]).then_inc(p_pre, 1)
            dve.tensor_tensor(NMSEL[:, :], IDB[:, 0:8], IDB[:, 32:40], ALU.add).then_inc(p_pre, 1)
            with dve.Fori(0, B) as b:
                ln_vector(dve, b + 12, X[:, b, :], Y[:, b, 1:T + 1])
            dve.wait_ge(ln_out, 17)
            dve.wait_ge(p_pre, 8)
            dve.wait_ge(p_y, 1)
            l1f_tables(dve, 0)
            l1f_shift(dve, 0, L_SH, p_sh)
            for p in range(NPT):
                l1f_project_vector(dve, 0, p)

            def body(i, b, l, nb, nl, new_layer):
                for g in range(2):
                    u = 2 * i + g
                    for what, n in order(g, g == 0 or nb is not None):
                        if what == "P":
                            l1f_project_vector(dve, u + 1, n)
                        elif what == "N":
                            dve.wait_ge(p_proj, NP * (2 * i + 2))
                            dve.wait_ge(p_y, 2 * i + 1)
                            l1f_shift(dve, nb, L_SH, p_sh)
                            if new_layer:
                                dve.wait_ge(p_add, NJ * (2 * i + 2))
                                l1f_tables(dve, nl)
                        elif what == "S":
                            for h in (2 * n, 2 * n + 1):
                                dve.wait_ge(p_s, 9 * u + h + 1)
                                dve.tensor_reduce(L_NM[:, :, h], score_tiles(h % 2), AX, ALU.max, negate=True).then_inc(p_max, 1)
                        elif what == "M":
                            dve.wait_ge(p_s, 9 * u + 9)
                            dve.tensor_scalar(L_NMB[0:8, 0:T], PS[0:8, PV0, :], 1.0, None, ALU.mult).then_inc(p_max, 1)
                            dve.wait_ge(p_max, 10 * u + 9)
                            dve.tensor_tensor(L_NMB[32:40, 0:T], PS[0:8, PV0, :], L_NMB[0:8, 0:T], ALU.subtract).then_inc(p_max, 1)
                        elif what == "D":
                            l1f_divide(dve, u, g, n)
                        elif what == "F":
                            l1f_ff_vector(dve, i, b, l, n)
            through_units(dve, body)
            dve.wait_ge(p_y, 2 * DEPTH * B + 1)
            with dve.Fori(0, B) as b:
                dve.tensor_tensor(X[:, b, :], X[:, b, :], Y[:, b, 1:T + 1], ALU.add).then_inc(x_done, 1)

        def l1f_tables(dve, l):
            dve.wait_ge(w_qks, 16 * l + 16)
            for k in range(4):
                dve.tensor_tensor(L_TAB[:, k, :, :], ROPE[:, k, :, :], over(QKS[:, k, :], NT), ALU.mult).then_inc(p_tab, 1)
            dve.wait_ge(p_tab, 4 * l + 4)

        def l1f_shift(dve, b, dst, done):
            dve.tensor_scalar(dst[0:64, :], Y[0:64, b, 1:T + 1], 1.0, None, ALU.mult)
            dve.tensor_scalar(dst[64:P, :], Y[64:P, b, 0:T], 1.0, None, ALU.mult).then_inc(done, 1)

        def l1f_project_vector(dve, u, p):
            if p < NJ:
                t, q = p // 2, p % 2
                dve.wait_ge(p_raw, NJ * u + p + 1)
                if p >= 2 or not is_first(u):
                    dve.wait_ge(p_add, NJ * u + p - 1)
                raw = L_RAW[p % 2].rearrange("p (h u d) -> p h u d", h=8, u=2)
                t2 = L_T2[p % 2].rearrange("p (h u d) -> p h u d", h=8, u=2)
                sin = L_TAB[:, 2 * q + 1, t, :].rearrange("p (u d) -> p u d", u=2)
                for v in range(2):
                    ins = dve.tensor_tensor(t2[:, :, v, :], raw[:, :, 1 - v, :], over(sin[:, v, :], 8), ALU.mult)
                ins.then_inc(p_t12, 1)
                dve.wait_ge(p_sq, NJ * u + p + 1)
                if p == 0 and not is_first(u):
                    dve.wait_ge(p_sd, u)
                dve.tensor_reduce(L_SS[:, 8 * p:8 * p + 8], L_SQ[p % 2].rearrange("p (h d) -> p h d", h=8), AX, ALU.add).then_inc(p_ss, 1)
            if p == NJ + 1:
                dve.wait_ge(p_sd, u + 1)
                dve.tensor_scalar(L_SD, L_SD, 1e-12, None, ALU.max).then_inc(p_rn, 1)
                dve.wait_ge(p_rn, 2 * u + 1)
                dve.reciprocal(L_SD, L_SD).then_inc(p_rn, 1)
                dve.wait_ge(p_rn, 2 * u + 2)
            if NJ < p <= NJ + 4:
                for j in (2 * (p - NJ - 1), 2 * (p - NJ - 1) + 1):
                    dve.wait_ge(p_add, NJ * u + j + 1)
                    qk = L_QK[j].rearrange("p (h d) -> p h d", h=8)
                    dve.tensor_tensor(qk, qk, along(L_SD[:, 8 * j:8 * j + 8], DH), ALU.mult).then_inc(p_qk, 1)

        def l1f_divide(dve, u, g, k):
            dve.wait_ge(p_den, 8 * u + 2 * k + 2)
            dn, cx = L_DN[k % 2], L_CX[:, 4 * g + k, :]
            dve.reciprocal(dn, dn).then_inc(p_rd, 1)
            dve.wait_ge(p_rd, 4 * u + k + 1)
            dve.tensor_tensor(cx, cx, dn, ALU.mult).then_inc(p_cx, 1)

        def l1f_ff_vector(dve, i, b, l, s):
            if s == 0:
                dve.wait_ge(p_out, 2 * i + 1)
                dve.tensor_tensor(Y[:, b, 1:T + 1], Y[:, b, 1:T + 1], PS[:, 0, :], ALU.add).then_inc(p_y, 1)
                dve.wait_ge(p_y, 2 * i + 2)
                l1f_shift(dve, b, L_SF, p_sf)
            elif s == 1:
                dve.wait_ge(p_sf, i + 1)
                ln_vector_center(dve, i + 16, L_SF)
            elif s == 2:
                ln_vector_rs(dve, i + 16)
            elif s == 3:
                ln_vector_out(dve, i + 16, xn)
                dve.wait_ge(w_ff, 112 * l + 112)
                dve.wait_ge(ln_out, i + 18)
                dve.tensor_scalar(L_XG, xn, LNGB[:, 0:1], LNGB[:, 1:2], ALU.mult, ALU.add).then_inc(p_xg, 1)
            elif s == 4:
                for m, (m0, mw) in enumerate(FF):
                    dve.wait_ge(p_gelu, 3 * i + m + 1)
                    dve.scalar_tensor_tensor(out=L_H[m][0:mw, :], in0=PS[0:mw, FFB[m][1], :], scalar=B1[0:mw, m, 0:1],
                                             in1=L_G[m][0:mw, :], op0=ALU.add, op1=ALU.mult).then_inc(p_h, 1)
            else:
                dve.wait_ge(p_out, 2 * i + 2)
                dve.scalar_tensor_tensor(out=Y[:, b, 1:T + 1], in0=PS[:, 0, :], scalar=B2[:, 0:1], in1=Y[:, b, 1:T + 1],
                                         op0=ALU.add, op1=ALU.add).then_inc(p_y, 1)

        def l1f_pool(pool):
            for p in range(NPT):
                l1f_project_pool(pool, 0, 0, 0, p)

            def body(i, b, l, nb, nl, new_layer):
                for g in range(2):
                    for what, n in order(g, g == 0 or nb is not None):
                        if what == "P":
                            l1f_project_pool(pool, 2 * i + g + 1, 1 - g, nl if g else l, n)
            through_units(pool, body)

        def l1f_project_pool(pool, u, g, l, p):
            if p < NJ:
                t, q = p // 2, p % 2
                if p == 0:
                    pool.wait_ge(p_tab, 4 * l + 4)
                pool.wait_ge(p_raw, NJ * u + p + 1)
                if not is_first(u):
                    pool.wait_ge(p_turn, NJ * u + p - 7)
                pool.tensor_tensor(L_QK[p].rearrange("p (h d) -> p h d", h=8), L_RAW[p % 2].rearrange("p (h d) -> p h d", h=8),
                                   over(L_TAB[:, 2 * q, t, :], 8), ALU.mult).then_inc(p_t1, 1)
                pool.wait_ge(p_t1, NJ * u + p + 1)
                pool.wait_ge(p_t12, NJ * u + p + 1)
                pool.tensor_tensor(L_QK[p], L_QK[p], L_T2[p % 2], ALU.add).then_inc(p_add, 1)
            j = p - 11
            if 0 <= j < NJ:
                src, dst = ((L_QT, L_QB), (L_KT, L_KB))[j % 2]
                t0 = (j // 2) * P + (WIN if j % 2 else 0)
                pool.wait_ge(p_tev, NJ * u + j + 1)
                if j == 0 and not is_first(u):
                    pool.wait_ge(p_s, 9 * u)
                if j == 0 and is_first(u):
                    pool.wait_ge(p_pre, 8)
                pool.tensor_tensor(dst[:, :, t0:t0 + P], src[:, 4 * g:4 * g + 4, t0:t0 + P],
                                   L_ONE4.to_broadcast([P, 4, P]), ALU.mult).then_inc(p_cast, 1)

        late_at = [0]

        def late(rows, cols):
            late_at[0] += cols
            assert late_at[0] <= 3 * NH * DH
            return WQKV[0:rows, late_at[0] - cols:late_at[0]]
        L2W = late(P, 4 * P).rearrange("p (i d) -> p i d", i=4)
        L2B = late(P, 2)
        L2BV = late(1, P)
        MASKF = late(P, NT * S2).rearrange("p (t k) -> p t k", t=NT)
        VCTX = late(S2, B * P).rearrange("p (b d) -> p b d", b=B)
        l2x_loaded = sem("l2x_loaded")
        c = carver()
        C_C = c(S2)
        C_Q = c(T)
        C_K = c(S2)
        C_V = c(P)
        C_S = c(NT * S2).rearrange("p (t k) -> p t k", t=NT)
        C_M = c(NT)
        C_SUM = c(NT)
        C_R = c(NT)
        C_PT = c(T)
        C_CX = c(T)
        C_MASK = c(NT * S2).rearrange("p (t k) -> p t k", t=NT)
        (c_ctx, c_proj, c_q, c_kv, c_score, c_max, c_sub, c_exp, c_vec, c_p, c_turn, c_pt, c_cx, c_cxs, c_out) = [sem("c_" + n) for n in (
            "ctx proj q kv score max sub exp vec p turn pt cx cxs out").split()]
        CS = PS[:, 0, :].rearrange("p (t z) -> p t z", t=NT)[:, :, 0:S2]

        def cross_tensor(pe, b, k, ln, project):
            ln_tensor(pe, b + ln, X[:, b, :])
            pe.wait_ge(c_ctx, k + 1)
            if project:
                pe.matmul(PS[:, 4, 0:S2], L2W[:, 1, :], C_C, start=True, stop=True)
                pe.matmul(PS[0:S2, 5, 0:P], C_C, L2W[:, 2, :], start=True, stop=False)
                pe.matmul(PS[0:S2, 5, 0:P], ONEROW[0:1, 0:S2], L2BV, start=False, stop=True).then_inc(c_proj, 1)
                pe.wait_ge(ln_out, b + ln + 2)
                pe.matmul(PS[:, 2, :], L2W[:, 0, :], xn, start=True, stop=True).then_inc(c_proj, 1)
                pe.wait_ge(c_q, k + 1)
                pe.wait_ge(c_kv, k + 1)
            else:
                pe.wait_ge(ln_out, b + ln + 2)
            q, keys = (C_Q, C_K) if project else (xn, C_C)
            for t in range(NT):
                mm = pe.matmul(CS[:, t, :], q[:, t * P:(t + 1) * P], keys, start=True, stop=True)
            mm.then_inc(c_score, 1)
            pe.wait_ge(c_p, k + 1)
            for t in range(NT):
                mm = pe.transpose(PS[0:S2, 3, t * P:(t + 1) * P], C_S[:, t, :], IDF[:, :])
            mm.then_inc(c_turn, 1)
            pe.wait_ge(c_pt, k + 1)
            pe.matmul(PS[:, 4, :], C_V[0:S2, :], C_PT[0:S2, :], start=True, stop=True).then_inc(c_cx, 1)
            if project:
                pe.wait_ge(c_cxs, k + 1)
                pe.matmul(PS[:, 5, :], L2W[:, 3, :], C_CX, start=True, stop=True).then_inc(c_out, 1)

        def cross_scalar(act, b, k, ln, project):
            ln_scalar(act, b + ln)
            act.wait_ge(c_sub, k + 1)
            act.activation(C_S, C_S, ACT.Exp).then_inc(c_exp, 1)
            act.wait_ge(c_turn, k + 1)
            act.activation(C_PT[0:S2, :], PS[0:S2, 3, :], ACT.Copy).then_inc(c_pt, 1)
            if project:
                act.wait_ge(c_cx, k + 1)
                act.activation(C_CX, PS[:, 4, :], ACT.Copy).then_inc(c_cxs, 1)

        def cross_vector(dve, b, k, ln, project):
            ln_vector(dve, b + ln, X[:, b, :], xn)
            if project:
                dve.wait_ge(c_proj, 2 * k + 1)
                dve.tensor_copy(C_K, PS[:, 4, 0:S2])
                dve.tensor_copy(C_V[0:S2, :], PS[0:S2, 5, 0:P]).then_inc(c_kv, 1)
                dve.wait_ge(c_proj, 2 * k + 2)
                dve.tensor_scalar(C_Q, PS[:, 2, :], L2B[:, 0:1], P ** -0.5, ALU.add, ALU.mult).then_inc(c_q, 1)
            dve.wait_ge(c_score, k + 1)
            scores = CS
            if not project:
                for t in range(NT):
                    ins = dve.scalar_tensor_tensor(out=C_S[:, t, :], in0=CS[:, t, :], scalar=P ** 0.5, in1=C_MASK[:, t, :], op0=ALU.mult, op1=ALU.add)
                ins.then_inc(c_q, 1)
                dve.wait_ge(c_q, k + 1)
                scores = C_S
            dve.tensor_reduce(C_M, scores, AX, ALU.max, negate=True).then_inc(c_max, 1)
            dve.wait_ge(c_max, k + 1)
            dve.tensor_tensor(C_S, scores, along(C_M, S2), ALU.add).then_inc(c_sub, 1)
            dve.wait_ge(c_exp, k + 1)
            dve.tensor_reduce(C_SUM, C_S, AX, ALU.add).then_inc(c_vec, 1)
            dve.wait_ge(c_vec, 2 * k + 1)
            dve.reciprocal(C_R, C_SUM).then_inc(c_vec, 1)
            dve.wait_ge(c_vec, 2 * k + 2)
            dve.tensor_tensor(C_S, C_S, along(C_R, S2), ALU.mult).then_inc(c_p, 1)
            if project:
                dve.wait_ge(c_out, k + 1)
                dve.scalar_tensor_tensor(out=X[:, b, :], in0=PS[:, 5, :], scalar=L2B[:, 1:2], in1=X[:, b, :],
                                         op0=ALU.add, op1=ALU.add).then_inc(x_done, 1)
            else:
                dve.wait_ge(c_cx, k + 1)
                dve.tensor_tensor(X[:, b, :], X[:, b, :], PS[:, 4, :], ALU.add).then_inc(x_done, 1)

        def l2x_tensor(pe):
            pe.wait_ge(l2x_loaded, 16 * 5)
            with pe.Fori(0, B) as b:
                cross_tensor(pe, b, b, 40, True)

        def l2x_scalar(act):
            with act.Fori(0, B) as b:
                cross_scalar(act, b, b, 40, True)

        def l2x_vector(dve):
            dve.wait_ge(l2x_loaded, 16 * 5)
            with dve.Fori(0, B) as b:
                cross_vector(dve, b, b, 40, True)

        def l2x_pool(pool):
            with pool.Fori(0, B) as b:
                pool.wait_ge(x_done, b + 16)
                pool.tensor_copy(C_C, CT[:, b, :]).then_inc(c_ctx, 1)

        DF, NC = 512, 4
        M_W1 = MOEW[:, 0:4096].rearrange("p (e c m) -> p e c m", e=NE, c=NC)
        M_W2 = MOEW[:, 4096:8192].rearrange("p (e c m) -> p e c m", e=NE, c=NC)
        M_B1 = sb("M_B1", [P, 2, NE, NC])
        M_B2 = sb("M_B2", [NE, 2, P])
        M_GW = sb("M_GW", [P, 2, NE])
        M_GB = sb("M_GB", [1, 2, NE])
        RANK = sb("RANK", [P, NE])
        moe_loaded, moe_w = sem("moe_loaded"), sem("moe_w")

        def carve_moe(c):
            d = {}
            for n in "E S1 S2 T1 T2".split():
                d[n] = c(NT * NE).rearrange("p (t e) -> p t e", t=NT)
            for n in "M SUM R M1 M2 MX".split():
                d[n] = c(NT)
            d["GT"] = c(T)
            d["SG"], d["H"] = [c(T), c(T)], [c(T), c(T)]
            return d
        (m_logit, m_max, m_sub, m_exp, m_vec, m_w, m_turn, m_gt, m_bc, m_z, m_act, m_h, m_down) = [sem("m_" + n) for n in (
            "logit max sub exp vec w turn gt bc z act h down").split()]
        NM = NE * NC

        def moe_tensor(pe, k, s, d, src):
            for t in range(NT):
                o = PS[:, 0, t * NE:(t + 1) * NE]
                pe.matmul(o, src[:, t * P:(t + 1) * P], M_GW[:, s, :], start=True, stop=False)
                mm = pe.matmul(o, ONEROW[:, :], M_GB[:, s, :], start=False, stop=True)
            mm.then_inc(m_logit, 1)
            pe.wait_ge(m_w, k + 1)
            for t in range(NT):
                mm = pe.transpose(PS[0:NE, 4, t * P:(t + 1) * P], d["E"][:, t, :], IDF[:, :])
            mm.then_inc(m_turn, 1)
            pe.wait_ge(m_gt, k + 1)
            pe.matmul(PS[:, 1, :], M_B2[:, s, :], d["GT"][0:NE, :], start=True, stop=False)
            for i in range(NM):
                e, c = i // NC, i % NC
                if c == 0:
                    if e >= 2:
                        pe.wait_ge(m_h, k * NM + NC * (e - 1))
                    pe.matmul(PS[:, 5 * (e % 2), :], IDF[0:NE, e:e + 1].to_broadcast([NE, P]), d["GT"][0:NE, :],
                              start=True, stop=True).then_inc(m_bc, 1)
                if i >= 2:
                    pe.wait_ge(m_act, k * NM + i - 1)
                pe.matmul(PS[:, 2 + i % 2, :], M_W1[:, e, c, :], src, start=True, stop=True).then_inc(m_z, 1)
                if i >= 1:
                    moe_down(pe, k, d, i - 1)
            moe_down(pe, k, d, NM - 1)

        def moe_down(pe, k, d, i):
            pe.wait_ge(m_h, k * NM + i + 1)
            pe.matmul(PS[:, 1, :], M_W2[:, i // NC, i % NC, :], d["H"][i % 2], start=False, stop=i == NM - 1).then_inc(m_down, 1)

        def moe_scalar(act, k, s, d, func):
            act.wait_ge(m_sub, k + 1)
            act.activation(d["E"], d["E"], ACT.Exp).then_inc(m_exp, 1)
            for i in range(NM):
                e, c = i // NC, i % NC
                act.wait_ge(m_z, k * NM + i + 1)
                if i >= 2:
                    act.wait_ge(m_h, k * NM + i - 1)
                act.activation(d["SG"][i % 2], PS[:, 2 + i % 2, :], func, bias=M_B1[:, s, e, c:c + 1]).then_inc(m_act, 1)

        def moe_vector(dve, k, s, d, vec0, top2):
            n = [0]

            def step(ins):
                n[0] += 1
                ins.then_inc(m_vec, 1)
                dve.wait_ge(m_vec, vec0 + n[0])
            E, S1, S2_, T1, T2 = d["E"], d["S1"], d["S2"], d["T1"], d["T2"]
            dve.wait_ge(m_logit, k + 1)
            lg = PS[:, 0, 0:NT * NE].rearrange("p (t e) -> p t e", t=NT)
            dve.tensor_reduce(d["M"], lg, AX, ALU.max, negate=True).then_inc(m_max, 1)
            dve.wait_ge(m_max, k + 1)
            dve.tensor_tensor(E, lg, along(d["M"], NE), ALU.add).then_inc(m_sub, 1)
            dve.wait_ge(m_exp, k + 1)
            step(dve.tensor_reduce(d["SUM"], E, AX, ALU.add))
            step(dve.reciprocal(d["R"], d["SUM"]))
            ins = dve.tensor_tensor(E, E, along(d["R"], NE), ALU.mult)
            if top2:
                step(ins)
                rank = over(RANK[:, :], NT)
                for sel, m, src in ((S1, d["M1"], E), (S2_, d["M2"], T2)):
                    step(dve.tensor_reduce(m, src, AX, ALU.max))
                    step(dve.tensor_tensor(T1, src, along(m, NE), ALU.is_equal))
                    step(dve.tensor_tensor(T1, T1, rank, ALU.mult))
                    step(dve.tensor_reduce(d["MX"], T1, AX, ALU.max))
                    step(dve.tensor_tensor(sel, T1, along(d["MX"], NE), ALU.is_equal))
                    if sel is S1:
                        step(dve.tensor_scalar(T2, S1, -2.0, None, ALU.mult))
                        step(dve.tensor_tensor(T2, T2, E, ALU.add))
                step(dve.tensor_tensor(d["SUM"], d["M1"], d["M2"], ALU.add))
                step(dve.reciprocal(d["R"], d["SUM"]))
                step(dve.tensor_tensor(S1, S1, S2_, ALU.add))
                step(dve.tensor_tensor(S1, S1, E, ALU.mult))
                ins = dve.tensor_tensor(E, S1, along(d["R"], NE), ALU.mult)
            ins.then_inc(m_w, 1)
            assert n[0] == (19 if top2 else 2), n[0]
            dve.wait_ge(m_turn, k + 1)
            dve.tensor_copy(d["GT"][0:NE, :], PS[0:NE, 4, :]).then_inc(m_gt, 1)
            for i in range(NM):
                dve.wait_ge(m_act, k * NM + i + 1)
                if i % NC == 0:
                    dve.wait_ge(m_bc, k * NE + i // NC + 1)
                if i >= 2:
                    dve.wait_ge(m_down, k * NM + i - 1)
                dve.tensor_tensor(d["H"][i % 2], d["SG"][i % 2], PS[:, 5 * (i // NC % 2), :], ALU.mult).then_inc(m_h, 1)
            dve.wait_ge(m_down, k * NM + NM)

        c = carver()
        G2 = carve_moe(c)

        def l2f_tensor(pe):
            pe.wait_ge(moe_loaded, 16 * 9)
            pe.wait_ge(moe_w, 16 * 2)
            with pe.Fori(0, B) as b:
                ln_tensor(pe, b + 44, X[:, b, :])
                pe.wait_ge(ln_out, b + 46)
                moe_tensor(pe, b, 0, G2, xn)

        def l2f_scalar(act):
            act.wait_ge(moe_loaded, 16 * 9)
            with act.Fori(0, B) as b:
                ln_scalar(act, b + 44)
                moe_scalar(act, b, 0, G2, ACT.Gelu)

        def l2f_vector(dve):
            dve.wait_ge(moe_loaded, 16 * 9)
            with dve.Fori(0, B) as b:
                ln_vector(dve, b + 44, X[:, b, :], xn)
                moe_vector(dve, b, 0, G2, 19 * b, True)
                dve.tensor_tensor(X[:, b, :], X[:, b, :], PS[:, 1, :], ALU.add).then_inc(x_done, 1)

        def l3x_tensor(pe):
            with pe.Fori(0, B) as b:
                cross_tensor(pe, b, b + 4, 48, False)

        def l3x_scalar(act):
            with act.Fori(0, B) as b:
                cross_scalar(act, b, b + 4, 48, False)

        def l3x_vector(dve):
            dve.tensor_scalar(C_MASK, MASKF[:, :, :], -1.0e9, None, ALU.mult).then_inc(c_kv, 1)
            dve.wait_ge(c_kv, 5)
            with dve.Fori(0, B) as b:
                cross_vector(dve, b, b + 4, 48, False)

        def l3x_pool(pool):
            with pool.Fori(0, B) as b:
                pool.wait_ge(x_done, b + 24)
                pool.tensor_copy(C_V[0:S2, :], VCTX[:, b, :])
                pool.tensor_copy(C_C, CT[:, b, :]).then_inc(c_ctx, 1)

        CONVW = late(P, 3 * P).rearrange("p (k d) -> p k d", k=3)
        WQKV3 = late(P, 3 * P).rearrange("p (i d) -> p i d", i=3)
        WO3 = late(P, P)
        B3 = late(P, 8)
        BV3 = late(1, P)
        l3_loaded = sem("l3_loaded")
        c = carver()
        H_KM = c(H0 * T).rearrange("p (h n) -> p h n", h=H0)
        VROW3 = H0 * VSTEP
        H_VB = c(NT * VROW3).rearrange("p (t z) -> p t z", t=NT)
        H_P = [c(T) for _ in range(4)]
        H_C1, H_Q, H_K, H_CX = c(T), c(T), c(T), c(T)
        H_N1, H_XR = c(T), c(T)
        H_RC = H_K
        H_NM = c(NT * H0).rearrange("p (t h) -> p t h", t=NT)
        H_NMT = c(T)
        G3 = carve_moe(c)
        (h_conv, h_c1, h_proj, h_ev, h_km, h_s, h_max, h_mturn, h_nmt, h_st, h_exp, h_pv, h_rc, h_cx, h_wo, h_r, h_n1, h_ev2) = [
            sem("h_" + n) for n in "conv c1 proj ev km s max mturn nmt st exp pv rc cx wo r n1 ev2".split()]
        NU = H0 * NT

        def l3f_tensor(pe):
            nc.disable_value_cache = True
            pe.wait_ge(l3_loaded, 16 * 5)
            pe.wait_ge(moe_w, 16 * 4)
            with pe.Fori(0, B) as b:
                k0 = 3 * b + 52
                ln_tensor(pe, k0, X[:, b, :])
                pe.wait_ge(ln_out, k0 + 2)
                for k in range(3):
                    mm = pe.matmul(PS[:, 0, :], CONVW[:, k, :], XN[:, k:k + T], start=k == 0, stop=k == 2)
                mm.then_inc(h_conv, 1)
                pe.wait_ge(h_c1, b + 1)
                for j in range(2):
                    pe.matmul(PS[:, 1 + j, :], WQKV3[:, j, :], H_C1, start=True, stop=True)
                for t in range(NT):
                    o = PS[:, 3, t * P:(t + 1) * P]
                    pe.matmul(o, H_C1[:, t * P:(t + 1) * P], WQKV3[:, 2, :], start=True, stop=False)
                    mm = pe.matmul(o, ONEROW[:, :], BV3, start=False, stop=True)
                mm.then_inc(h_proj, 1)
                pe.wait_ge(h_ev, b + 1)
                for n in range(NU):
                    h, t = n // NT, n % NT
                    if t == 0:
                        pe.wait_ge(h_km, b * H0 + h + 1)
                    if n >= 4:
                        pe.wait_ge(h_max, b * NU + n - 3)
                    pe.matmul(PS[:, n % 4, :], H_Q[:, t * P:(t + 1) * P], H_KM[:, h, :], start=True, stop=True).then_inc(h_s, 1)
                pe.wait_ge(h_max, b * NU + NU)
                for t in range(NT):
                    mm = pe.transpose(PS[0:H0, 4, t * P:(t + 1) * P], H_NM[:, t, :], IDF[:, :])
                mm.then_inc(h_mturn, 1)
                pe.wait_ge(h_nmt, b + 1)
                for n in range(NU):
                    h, t = n // NT, n % NT
                    if n >= 4:
                        pe.wait_ge(h_exp, b * NU + n - 3)
                    pe.matmul(PS[:, n % 4, :], H_KM[:, h, t * P:(t + 1) * P], H_Q, start=True, stop=False)
                    pe.matmul(PS[:, n % 4, :], IDF[0:H0, h:h + 1].to_broadcast([H0, P]), H_NMT[0:H0, :],
                              start=False, stop=True).then_inc(h_st, 1)
                    if n >= 2:
                        l3f_pv(pe, b, n - 2)
                l3f_pv(pe, b, NU - 2)
                l3f_pv(pe, b, NU - 1)
                pe.wait_ge(h_cx, 2 * b + 2)
                pe.matmul(PS[:, 0, :], WO3, H_CX, start=True, stop=True).then_inc(h_wo, 1)
                pe.wait_ge(h_r, 2 * b + 1)
                ln_tensor(pe, k0 + 1, H_XR)
                pe.wait_ge(h_n1, b + 1)
                moe_tensor(pe, b + 4, 1, G3, H_N1)
                pe.wait_ge(h_r, 2 * b + 2)
                ln_tensor(pe, k0 + 2, H_XR)
            nc.disable_value_cache = False

        def l3f_pv(pe, b, n):
            h, t = n // NT, n % NT
            pe.wait_ge(h_exp, b * NU + n + 1)
            pe.matmul(PS[:, 4 + h // 8, :], H_VB[:, t, h * P:(h + 1) * P], H_P[n % 4],
                      start=n % (8 * NT) == 0, stop=n % (8 * NT) == 8 * NT - 1).then_inc(h_pv, 1)

        def l3f_scalar(act):
            nc.disable_value_cache = True
            with act.Fori(0, B) as b:
                k0 = 3 * b + 52
                ln_scalar(act, k0)
                for n in range(NU):
                    act.wait_ge(h_st, b * NU + n + 1)
                    if n >= 4:
                        act.wait_ge(h_pv, b * NU + n - 3)
                    act.activation(H_P[n % 4], PS[:, n % 4, :], ACT.Exp).then_inc(h_exp, 1)
                ln_scalar(act, k0 + 1)
                moe_scalar(act, b + 4, 1, G3, ACT.Relu)
                ln_scalar(act, k0 + 2)
            nc.disable_value_cache = False

        def l3f_vector(dve):
            nc.disable_value_cache = True
            dve.wait_ge(l3_loaded, 16 * 5)
            dve.memset(H_VB, 0.0).then_inc(h_rc, 1)
            dve.wait_ge(h_rc, 1)
            for h in range(H0):
                at = h * P + 64 + DK0 * (h % 8)
                dve.memset(H_VB[:, :, at:at + DK0], 1.0)
            with dve.Fori(0, B) as b:
                k0 = 3 * b + 52
                ln_vector(dve, k0, X[:, b, :], xn)
                dve.wait_ge(h_conv, b + 1)
                dve.tensor_scalar(H_C1, PS[:, 0, :], B3[:, 0:1], None, ALU.add).then_inc(h_c1, 1)
                dve.wait_ge(h_proj, b + 1)
                dve.tensor_scalar(H_K, PS[:, 2, :], B3[:, 2:3], None, ALU.add).then_inc(h_rc, 1)
                for t in range(NT):
                    for g in range(2):
                        vg = H_VB[:, t, g * 8 * P:g * 8 * P + 8 * VSTEP].rearrange("p (h e) -> p h e", e=VSTEP)[:, :, 0:DK0]
                        dve.tensor_copy(vg, PS[:, 3, t * P + g * 64:t * P + (g + 1) * 64].rearrange("p (h e) -> p h e", e=DK0))
                dve.tensor_scalar(H_Q, PS[:, 1, :], B3[:, 1:2], DK0 ** -0.5, ALU.add, ALU.mult).then_inc(h_ev, 1)
                dve.wait_ge(h_rc, 3 * b + 2)
                for h in range(H0):
                    dve.tensor_scalar(H_KM[:, h, :], H_K, HMASK[:, h:h + 1], None, ALU.mult).then_inc(h_km, 1)
                for n in range(NU):
                    h, t = n // NT, n % NT
                    dve.wait_ge(h_s, b * NU + n + 1)
                    dve.tensor_reduce(H_NM[:, t, h:h + 1], PS[:, n % 4, :], AX, ALU.max, negate=True).then_inc(h_max, 1)
                dve.wait_ge(h_mturn, b + 1)
                dve.tensor_copy(H_NMT[0:H0, :], PS[0:H0, 4, :]).then_inc(h_nmt, 1)
                dve.wait_ge(h_km, b * H0 + H0)
                for g in range(2):
                    dve.wait_ge(h_pv, b * NU + (g + 1) * 8 * NT)
                    if g:
                        dve.wait_ge(h_cx, 2 * b + g)
                    dve.reciprocal(H_RC[0:64, :], PS[64:P, 4 + g, :]).then_inc(h_rc, 1)
                    dve.wait_ge(h_rc, 3 * b + g + 3)
                    dve.tensor_tensor(H_CX[64 * g:64 * g + 64, :], PS[0:64, 4 + g, :], H_RC[0:64, :], ALU.mult).then_inc(h_cx, 1)
                dve.wait_ge(h_wo, b + 1)
                dve.scalar_tensor_tensor(out=H_XR, in0=PS[:, 0, :], scalar=B3[:, 3:4], in1=H_C1,
                                         op0=ALU.add, op1=ALU.add).then_inc(h_r, 1)
                dve.wait_ge(h_r, 2 * b + 1)
                ln_vector(dve, k0 + 1, H_XR, H_N1)
                dve.wait_ge(ln_out, k0 + 3)
                dve.tensor_scalar(H_N1, H_N1, B3[:, 4:5], B3[:, 5:6], ALU.mult, ALU.add).then_inc(h_n1, 1)
                dve.wait_ge(h_n1, b + 1)
                moe_vector(dve, b + 4, 1, G3, 2 * b + 76, False)
                dve.tensor_tensor(H_XR, H_N1, PS[:, 1, :], ALU.add).then_inc(h_r, 1)
                dve.wait_ge(h_r, 2 * b + 2)
                ln_vector(dve, k0 + 2, H_XR, H_CX)
                dve.wait_ge(ln_out, k0 + 4)
                dve.tensor_scalar(H_Q, H_CX, B3[:, 6:7], B3[:, 7:8], ALU.mult, ALU.add).then_inc(h_ev2, 1)
                dve.wait_ge(h_ev2, b + 1)
                dve.tensor_tensor(X[:, b, :], X[:, b, :], H_Q, ALU.add).then_inc(x_done, 1)
                dve.wait_ge(x_done, b + 29)
            nc.disable_value_cache = False

        block = ctx.enter_context(nc.Block())

        @block.sync
        def _(sp):
            sp.dma_start(X[:, :, :], a["xT"]).then_inc(x_loaded, 16)
            for dst, name in ((CT[:, :, :], "ctxT"), (AVG[:, :], "c_avg"), (IDF[:, :], "c_ident"),
                              (HMASK[:, :], "c_hmask"), (EPSC[:, :], "c_eps")):
                sp.dma_start(dst, a[name]).then_inc(const_loaded, 16)
            for dst, name in ((L0W[:, :, :], "L0_W"), (L0B[:, :], "L0_b"), (BVROW[:, :], "L0_bv"), (ONEROW[:, :], "c_onerow"),
                              (MSK_Q[:, :, :], "mask_q"), (MSK_T[:, :], "mask_t"), (PAD_Q[:, :, :], "pad_q"),
                              (PAD_T[:, :], "pad_t")):
                src = a[name]
                if name == "pad_q":
                    src = bass.AP(tensor=src.tensor, offset=0, ap=[[0, P], [S2, B], [1, S2]])
                sp.dma_start(dst, src).then_inc(l0_loaded, 16)
            for dst, name in ((GW0[:, :], "L0F_gate"), (E_G, "L0F_g"), (E_U, "L0F_u"), (E_D, "L0F_d")):
                sp.dma_start(dst, a[name]).then_inc(l0f_loaded, 16)
            sp.wait_ge(f_gate, 1)
            for b in range(B):
                sp.dma_start(F_GB[0:NE, b, :], F_G[b * NE:(b + 1) * NE, :]).then_inc(f_gb, 16)
            for dst, name, part in ((L1W[:, :, :], "L1X_W", 0), (L1CW[:, :], "L1X_cw", 2), (L1G[:, :], "L1X_gain", 1),
                                    (PTR_I[:, :], "ptr", 0), (IDS_I[:, :, :], "ids", -1), (IOTA[:, :], "c_iota", S2)):
                src = a[name]
                if part > 0:
                    src = bass.AP(tensor=src.tensor, offset=0, ap=[[0, P], [1, part]])
                elif part < 0:
                    src = bass.AP(tensor=src.tensor, offset=0, ap=[[0, P], [T, B], [1, S2]])
                sp.dma_start(dst, src).then_inc(l1x_loaded, 16)
            sp.dma_start(ROPE[:, :, :, :], a["c_rope"]).then_inc(l1_const, 16)
            sp.dma_start(BANDS32[:, :, :], a["c_bands"]).then_inc(l1_const, 16)

            def load_qkv(l, g):
                sp.dma_start(W_QKV[:, g, :, :], a["L1F_qkv"][l, :, g, :, :]).then_inc(w_qkv[g], 16)

            def load_qks(l):
                sp.dma_start(QKS[:, :, :], bass.AP(tensor=a["L1F_qks"].tensor, offset=l * 4 * DH, ap=[[0, P], [DH, 4], [1, DH]])).then_inc(w_qks, 16)

            def load_wo(l):
                sp.dma_start(WO[:, :, :], a["L1F_wo"][l, :, :, :]).then_inc(w_o, 16)

            def load_ff(l):
                sp.dma_start(W1[:, :], a["L1F_w1"][l, :, :]).then_inc(w_ff, 16)
                sp.dma_start(W2[:, 0:2, :], a["L1F_w2a"][l, :, :, :]).then_inc(w_ff, 16)
                sp.dma_start(W2[0:DI - 256, 2, :], a["L1F_w2b"][l, :, :]).then_inc(w_ff, 16)
                sp.dma_start(LNGB[:, :], a["L1F_lngb"][l, :, :]).then_inc(w_ff, 16)
                sp.dma_start(B1[:, 0:2, :], a["L1F_b1a"][l, :, :, :]).then_inc(w_ff, 16)
                sp.dma_start(B1[0:DI - 256, 2, :], a["L1F_b1b"][l, :, :]).then_inc(w_ff, 16)
                sp.dma_start(B2[:, :], a["L1F_b2"][l, :, :]).then_inc(w_ff, 16)

            load_qks(0)
            load_qkv(0, 0)
            load_qkv(0, 1)
            load_wo(0)
            load_ff(0)
            with sp.Fori(1, DEPTH) as l:
                sp.wait_ge(p_tab, 4 * l)
                load_qks(l)
                sp.wait_ge(p_proj, NP * (2 * B * l - 1))
                load_qkv(l, 0)
                sp.wait_ge(p_proj, NP * 2 * B * l)
                load_qkv(l, 1)
                sp.wait_ge(p_out, 2 * l * B)
                load_wo(l)
                sp.wait_ge(p_y, 2 * B * l + 1)
                load_ff(l)
            sp.wait_ge(p_proj, DEPTH * B * 2 * NP)
            for dst, name in ((L2W, "L2X_W"), (L2B, "L2X_b"), (L2BV, "L2X_bv"), (MASKF, "maskf"), (VCTX, "vctx")):
                sp.dma_start(dst, a[name]).then_inc(l2x_loaded, 16)
            for dst, name in ((M_B1[:, 0, :, :], "L2F_b1"), (M_B1[:, 1, :, :], "L3F_b1"), (M_B2[:, 0, :], "L2F_b2"), (M_B2[:, 1, :], "L3F_b2"),
                              (M_GW[:, 0, :], "L2F_gw"), (M_GW[:, 1, :], "L3F_gw"), (M_GB[:, 0, :], "L2F_gb"), (M_GB[:, 1, :], "L3F_gb"),
                              (RANK[:, :], "c_rank")):
                sp.dma_start(dst, a[name]).then_inc(moe_loaded, 16)
            sp.wait_ge(x_done, 16)
            sp.dma_start(M_W1, a["L2F_w1"]).then_inc(moe_w, 16)
            sp.dma_start(M_W2, a["L2F_w2"]).then_inc(moe_w, 16)
            for dst, name in ((CONVW, "L3F_conv"), (WQKV3, "L3F_wqkv"), (WO3, "L3F_wo"), (B3, "L3F_b"), (BV3, "L3F_bv")):
                sp.dma_start(dst, a[name]).then_inc(l3_loaded, 16)
            sp.wait_ge(x_done, 24)
            sp.dma_start(M_W1, a["L3F_w1"]).then_inc(moe_w, 16)
            sp.dma_start(M_W2, a["L3F_w2"]).then_inc(moe_w, 16)
            sp.wait_ge(x_done, 4 * 8)
            sp.dma_start(out, X[:, :, :]).then_inc(out_stored, 16)
            sp.wait_ge(out_stored, 16)

        @block.gpsimd
        def _(pool):
            pool.wait_ge(const_loaded, 16 * 5)
            pool.memset(XN[:, :], 0.0).then_inc(pool_const, 1)
            pool.tensor_copy(IDB[:, :], IDF[:, :]).then_inc(pool_const, 1)
            l0x_pool(pool)
            pool.wait_ge(x_done, 4 * 1)
            l0f_pool(pool)
            pool.wait_ge(x_done, 4 * 2)
            l1x_pool(pool)
            pool.wait_ge(x_done, 4 * 3)
            l1f_pool(pool)
            pool.wait_ge(x_done, 4 * 4)
            l2x_pool(pool)
            pool.wait_ge(x_done, 4 * 6)
            l3x_pool(pool)
        @block.scalar
        def _(act):
            act.wait_ge(const_loaded, 16 * 5)
            l0x_scalar(act)
            act.wait_ge(x_done, 4 * 1)
            l0f_scalar(act)
            act.wait_ge(x_done, 4 * 2)
            l1x_scalar(act)
            act.wait_ge(x_done, 4 * 3)
            l1f_scalar(act)
            act.wait_ge(x_done, 4 * 4)
            l2x_scalar(act)
            act.wait_ge(x_done, 4 * 5)
            l2f_scalar(act)
            act.wait_ge(x_done, 4 * 6)
            l3x_scalar(act)
            act.wait_ge(x_done, 4 * 7)
            l3f_scalar(act)
        @block.tensor
        def _(pe):
            pe.wait_ge(const_loaded, 16 * 5)
            pe.wait_ge(x_loaded, 16)
            pe.wait_ge(pool_const, 2)
            l0x_tensor(pe)
            pe.wait_ge(x_done, 4 * 1)
            l0f_tensor(pe)
            pe.wait_ge(x_done, 4 * 2)
            l1x_tensor(pe)
            pe.wait_ge(x_done, 4 * 3)
            l1f_tensor(pe)
            pe.wait_ge(x_done, 4 * 4)
            l2x_tensor(pe)
            pe.wait_ge(x_done, 4 * 5)
            l2f_tensor(pe)
            pe.wait_ge(x_done, 4 * 6)
            l3x_tensor(pe)
            pe.wait_ge(x_done, 4 * 7)
            l3f_tensor(pe)
        @block.vector
        def _(dve):
            dve.wait_ge(const_loaded, 16 * 5)
            dve.wait_ge(x_loaded, 16)
            dve.wait_ge(pool_const, 2)
            dve.memset(LN_C[:, :], 0.0).then_inc(ln_out, 1)
            dve.wait_ge(ln_out, 1)
            l0x_vector(dve)
            dve.wait_ge(x_done, 4 * 1)
            l0f_vector(dve)
            dve.wait_ge(x_done, 4 * 2)
            l1x_vector(dve)
            dve.wait_ge(x_done, 4 * 3)
            l1f_vector(dve)
            dve.wait_ge(x_done, 4 * 4)
            l2x_vector(dve)
            dve.wait_ge(x_done, 4 * 5)
            l2f_vector(dve)
            dve.wait_ge(x_done, 4 * 6)
            l3x_vector(dve)
            dve.wait_ge(x_done, 4 * 7)
            l3f_vector(dve)


def kernel(**inputs):
    import numpy as np
    import concourse.bacc as bacc
    from concourse.bass_utils import run_bass_kernel_spmd

    v = {k: np.asarray(w) for k, w in inputs.items()}
    f = np.float32
    eye = np.eye(P, dtype=f)
    half = np.arange(0, 64, 2, dtype=f)
    pos = np.arange(T, dtype=f)
    freqs = pos[:, None] * (f(1.0) / f(10000.0) ** (half / f(64)))[None, :]
    base = (half + f(0.4 * 64)) / f(1.4 * 64)
    decay = base[None, :] ** ((pos - T // 2) / f(16))[:, None]
    cos, sin = np.cos(freqs), np.sin(freqs)
    qk = []
    for s, by in ((decay, f(8.0)), (f(1.0) / decay, f(1.0))):
        qk += [np.concatenate([cos * s, cos * s], 1) * by, np.concatenate([-sin * s, sin * s], 1) * by]
    rope = np.stack([x.reshape(NT, P, 64).transpose(1, 0, 2) for x in qk], 1).astype(f)
    r, s = np.arange(P)[:, None], np.arange(P + 32)[None, :]
    q_sees = (r + 32 - s >= 0) & (r + 32 - s <= 32)
    k_seen = (s - r >= 0) & (s - r <= 32)
    bands = np.stack([np.where(m, 0.0, NEG) for m in (q_sees & (s >= 32), q_sees, k_seen)], 1).astype(f)
    arrays = {
        "c_avg": np.full((P, P), 1 / P, f), "c_ident": eye, 
        "c_hmask": np.repeat(np.eye(H0, dtype=f), DK0, axis=0), "c_eps": np.full((P, 1), EPS, f),
        "c_onerow": np.ones((1, P), f),
        "xT": v["x"].transpose(2, 0, 1), "ctxT": v["ctx_1024"].transpose(2, 0, 1),
        "mask_q": v["mask_SxS2_bk1"].reshape(NT, P, S2).transpose(1, 0, 2),
        "mask_t": v["mask_SxS2_bk1"].T,
        "pad_q": v["mask_BxS2_bf0"], "pad_t": v["mask_BxS2_bf0"].T,
        "L0_W": np.stack([v["L0_xattn_" + n].T for n in ("Wq", "Wk", "Wv", "Wo")], 1),
        "L0_b": np.stack([v["L0_xattn_" + n] for n in ("bq", "bk", "bo")], 1),
        "L0_bv": v["L0_xattn_bv"][None, :],
        "L0F_gate": v["L0_ffn_gate_w"],
        "L0F_g": v["L0_ffn_Wg"].transpose(1, 0, 2).reshape(P, 8, 2, P),
        "L0F_u": v["L0_ffn_Wu"].transpose(1, 0, 2).reshape(P, 8, 2, P),
        "L0F_d": v["L0_ffn_Wd"].reshape(8, 2, P, P).transpose(2, 0, 1, 3),
        "L1X_W": np.stack([v["L1_xattn_" + n].T for n in ("Wqj", "Wqi", "Wkj", "Wki", "Wvj", "Wvi", "Wout")], 1),
        "L1X_cw": v["L1_xattn_council_weights"][None, :], "L1X_gain": v["L1_xattn_gain"].reshape(1, 1),
        "ptr": v["itok_BxS_0_4092"].reshape(B, NT, P).transpose(2, 0, 1).reshape(P, B * NT), "ids": v["itok_BxS_0_7"],
        "c_iota": np.arange(S2, dtype=f)[None, :],
        "c_rope": rope, "c_bands": bands,
        "L1F_qkv": v["L1_ffn_Wqkv"].reshape(6, P, 3, 2, T).transpose(0, 1, 3, 2, 4),
        "L1F_qks": np.stack([v["L1_ffn_q_scale"], np.roll(v["L1_ffn_q_scale"], 32, -1),
                             v["L1_ffn_k_scale"], np.roll(v["L1_ffn_k_scale"], 32, -1)], 1),
        "L1F_wo": v["L1_ffn_Wo"].reshape(6, 8, P, P).transpose(0, 2, 1, 3),
        "L1F_w1": v["L1_ffn_W1"], "L1F_w2a": v["L1_ffn_W2"][:, :256].reshape(6, 2, P, P).transpose(0, 2, 1, 3),
        "L1F_w2b": v["L1_ffn_W2"][:, 256:],
        "L1F_lngb": np.stack([v["L1_ffn_ln_g"], v["L1_ffn_ln_b"]], 2),
        "L1F_b1a": v["L1_ffn_b1"].reshape(6, 2, 341)[:, :, :256].reshape(6, 2, 2, P).transpose(0, 3, 2, 1),
        "L1F_b1b": v["L1_ffn_b1"].reshape(6, 2, 341)[:, :, 256:].transpose(0, 2, 1),
        "L1F_b2": v["L1_ffn_b2"][:, :, None],
        "L2X_W": np.stack([v["L2_xattn_" + n].T for n in ("Wq", "Wk", "Wv", "Wo")], 1),
        "L2X_b": np.stack([v["L2_xattn_bq"], v["L2_xattn_bo"]], 1), "L2X_bv": v["L2_xattn_bv"][None, :],
        "maskf": v["mask_SxS2_fk1"].reshape(NT, P, S2).transpose(1, 0, 2), "vctx": v["ctx_1024"].transpose(1, 0, 2),
        "c_rank": np.repeat(8 - np.arange(8, dtype=f)[None, :], P, 0),
        **{n + k: w for n, g, gb, w1, b1, w2, b2 in (
            ("L2F", "L2_ffn_Wg", "L2_ffn_bg", "L2_ffn_W1", "L2_ffn_b1", "L2_ffn_W2", "L2_ffn_b2"),
            ("L3F", "L3_ffn_gate_w", "L3_ffn_gate_b", "L3_ffn_w1", "L3_ffn_b1", "L3_ffn_w2", "L3_ffn_b2")) for k, w in (
            ("_gw", v[g]), ("_gb", v[gb][None, :]), ("_w1", v[w1].transpose(1, 0, 2).reshape(P, 8, 4, P)),
            ("_b1", v[b1].reshape(8, 4, P).transpose(2, 0, 1)), ("_w2", v[w2].reshape(8, 4, P, P).transpose(2, 0, 1, 3)),
            ("_b2", v[b2]))},
        "L3F_conv": v["L3_ffn_conv_w"].transpose(1, 2, 0),
        "L3F_wqkv": v["L3_ffn_wqkv"].reshape(3, P, P).transpose(2, 0, 1), "L3F_wo": v["L3_ffn_wo"].T,
        "L3F_b": np.stack([v["L3_ffn_conv_b"], v["L3_ffn_bqkv"][0:P], v["L3_ffn_bqkv"][P:2 * P], v["L3_ffn_bo"],
                           v["L3_ffn_ln1_g"], v["L3_ffn_ln1_b"], v["L3_ffn_ln2_g"], v["L3_ffn_ln2_b"]], 1),
        "L3F_bv": v["L3_ffn_bqkv"][None, 2 * P:],
    }
    nc = bacc.Bacc("TRN2", target_bir_lowering=False, num_devices=1)
    arrays = {k: np.ascontiguousarray(w) for k, w in arrays.items()}
    aps = {k: nc.dram_tensor(k, w.shape, mybir.dt.from_np(w.dtype), kind="ExternalInput").ap() for k, w in arrays.items()}
    out = nc.dram_tensor("out", (P, B, T), F32, kind="ExternalOutput").ap()
    build(nc, aps, out)
    r = run_bass_kernel_spmd(nc, [arrays], core_ids=[0])
    return np.ascontiguousarray(r.results[0]["out"].transpose(1, 2, 0))
```

```python
from contextlib import ExitStack

import concourse.bass as bass
from concourse import mybir

F32 = mybir.dt.float32
BF16 = mybir.dt.bfloat16
I32 = mybir.dt.int32
U8 = mybir.dt.uint8
ALU = mybir.AluOpType
ACT = mybir.ActivationFunctionType
AX = mybir.AxisListType.X


P = 128
B, T, S2 = 4, 512, 77
NT = T // P
H0, DK0 = 16, 8
NEG = -1.0e30
EPS = 1e-5


class Steps:

    def __init__(self, eng, sem):
        self.eng, self.sem, self.base, self.n = eng, sem, 0, 0

    def body(self, turn, per):
        self.base, self.n, self.per = turn * per, 0, per

    def done(self, ins):
        self.n += 1
        return ins.then_inc(self.sem, 1)

    def settle(self):
        self.eng.wait_ge(self.sem, self.base + self.n)

    def end(self):
        assert self.n == self.per, (self.sem, self.n, self.per)


def over(ap, n):
    return ap.rearrange("p (o k) -> p o k", o=1).to_broadcast([ap.shape[0], n, ap.shape[1]])


def along(ap, n):
    return ap.rearrange("p (h o) -> p h o", o=1).to_broadcast([ap.shape[0], ap.shape[1], n])


def build(nc, a, out):
    with ExitStack() as ctx:
        def sb(name, shape, dt=F32):
            return ctx.enter_context(nc.sbuf_tensor(name, shape, dt))

        def sem(name):
            return ctx.enter_context(nc.semaphore(name))

        PS = ctx.enter_context(nc.psum_tensor("PS", [P, 8, 512], F32))
        X = sb("X", [P, B, T])
        XN = sb("XN", [P, T + 2])
        xn = XN[:, 1:T + 1]
        LN_C = sb("LN_C", [P, T])
        LN_Q = sb("LN_Q", [P, T])
        LN_S = sb("LN_S", [P, NT])
        LN_R = sb("LN_R", [P, NT])
        LN4_S = sb("LN4_S", [P, B * NT])
        LN4_R = sb("LN4_R", [P, B * NT])
        EPSC = sb("EPSC", [P, 1])
        AVG = sb("AVG", [P, P])
        IDF = sb("IDF", [P, P])
        IDB = sb("IDB", [P, P], BF16)
        CT = sb("CT", [P, B, S2])
        HMASK = sb("HMASK", [P, H0])
        ARENA_COLS = 27 * 1024
        ARENA = sb("ARENA", [P, ARENA_COLS])

        XN4 = ARENA[:, ARENA_COLS - B * T:].rearrange("p (b n) -> p b n", b=B)
        SQ4 = ARENA[:, ARENA_COLS - 2 * B * T:ARENA_COLS - B * T].rearrange("p (b n) -> p b n", b=B)

        def carver():
            at = [0]

            def carve(cols, dt=F32):
                n = cols if dt == F32 else (cols + 1) // 2
                v = ARENA[:, at[0]:at[0] + n]
                at[0] += n
                assert at[0] <= ARENA_COLS, at[0]
                return v if dt == F32 else v.bitcast(dt)
            return carve

        x_loaded, const_loaded, out_stored = sem("x_loaded"), sem("const_loaded"), sem("out_stored")
        x_done = sem("x_done")
        pool_const = sem("pool_const")
        xn_set = sem("xn_set")
        ln_mean, ln_cen, ln_sq, ln_var, ln_sd, ln_rs, ln_bc, ln_out = [sem(n) for n in (
            "ln_mean", "ln_cen", "ln_sq", "ln_var", "ln_sd", "ln_rs", "ln_bc", "ln_out")]

        def ln_tensor_mean(pe, k, src):
            pe.wait_ge(ln_out, k + 1)
            pe.matmul(PS[:, 6, :], AVG[:, :], src, start=True, stop=True).then_inc(ln_mean, 1)

        def ln_tensor_var(pe, k):
            pe.wait_ge(ln_sq, k + 1)
            for t in range(NT):
                mm = pe.matmul(PS[:, 7, t:t + 1], LN_Q[:, t * P:(t + 1) * P], AVG[:, 0:1], start=True, stop=True)
            mm.then_inc(ln_var, 1)

        def ln_tensor_out(pe, k):
            pe.wait_ge(ln_rs, k + 1)
            for t in range(NT):
                mm = pe.matmul(PS[:, 6, t * P:(t + 1) * P], LN_R[:, t:t + 1].to_broadcast([P, P]), IDF[:, :],
                               start=True, stop=True)
            mm.then_inc(ln_bc, 1)

        def ln_tensor(pe, k, src):
            ln_tensor_mean(pe, k, src)
            ln_tensor_var(pe, k)
            ln_tensor_out(pe, k)

        def ln_scalar_square(act, k):
            act.wait_ge(ln_cen, k + 1)
            act.activation(LN_Q[:, :], LN_C[:, :], ACT.Square).then_inc(ln_sq, 1)

        def ln_scalar_sd(act, k):
            act.wait_ge(ln_var, k + 1)
            act.activation(LN_S[:, :], PS[:, 7, 0:NT], ACT.Sqrt, bias=EPSC[:, 0:1]).then_inc(ln_sd, 1)

        def ln_scalar(act, k):
            ln_scalar_square(act, k)
            ln_scalar_sd(act, k)

        def ln_vector_center(dve, k, src):
            dve.wait_ge(ln_mean, k + 1)
            dve.tensor_tensor(LN_C[:, :], src, PS[:, 6, :], ALU.subtract).then_inc(ln_cen, 1)

        def ln_vector_rs(dve, k):
            dve.wait_ge(ln_sd, k + 1)
            dve.reciprocal(LN_R[:, :], LN_S[:, :]).then_inc(ln_rs, 1)

        def ln_vector_out(dve, k, dst):
            dve.wait_ge(ln_bc, k + 1)
            dve.tensor_tensor(dst, LN_C[:, :], PS[:, 6, :], ALU.mult).then_inc(ln_out, 1)

        def ln_vector(dve, k, src, dst):
            ln_vector_center(dve, k, src)
            ln_vector_rs(dve, k)
            ln_vector_out(dve, k, dst)

        def ln4_tensor(pe, k):
            for b in range(B):
                pe.matmul(PS[:, b, :], AVG[:, :], X[:, b, :], start=True, stop=True).then_inc(ln_mean, 1)
            for b in range(B):
                pe.wait_ge(ln_sq, k + b + 1)
                for t in range(NT):
                    mm = pe.matmul(PS[:, 4, b * NT + t:b * NT + t + 1], SQ4[:, b, t * P:(t + 1) * P], AVG[:, 0:1], start=True, stop=True)
                mm.then_inc(ln_var, 1)
            pe.wait_ge(ln_rs, k + B)
            for b in range(B):
                for t in range(NT):
                    mm = pe.matmul(PS[:, b, t * P:(t + 1) * P], LN4_R[:, b * NT + t:b * NT + t + 1].to_broadcast([P, P]), IDF[:, :],
                                   start=True, stop=True)
                mm.then_inc(ln_bc, 1)

        def ln4_scalar(act, k):
            for b in range(B):
                act.wait_ge(ln_cen, k + b + 1)
                act.activation(SQ4[:, b, :], XN4[:, b, :], ACT.Square).then_inc(ln_sq, 1)
            act.wait_ge(ln_var, k + B)
            act.activation(LN4_S[:, :], PS[:, 4, 0:B * NT], ACT.Sqrt, bias=EPSC[:, 0:1]).then_inc(ln_sd, B)

        def ln4_vector(dve, k):
            for b in range(B):
                dve.wait_ge(ln_mean, k + b + 1)
                dve.tensor_tensor(XN4[:, b, :], X[:, b, :], PS[:, b, :], ALU.subtract).then_inc(ln_cen, 1)
            dve.wait_ge(ln_sd, k + B)
            dve.reciprocal(LN4_R[:, :], LN4_S[:, :]).then_inc(ln_rs, B)
            for b in range(B):
                dve.wait_ge(ln_bc, k + b + 1)
                dve.wait_ge(ln_cen, k + b + 1)
                dve.tensor_tensor(XN4[:, b, :], XN4[:, b, :], PS[:, b, :], ALU.mult).then_inc(ln_out, 1)

        def set_xn(dve, b):
            dve.tensor_scalar(xn, XN4[:, b, :], 1.0, None, ALU.mult).then_inc(xn_set, 1)

        L0W = sb("L0W", [P, 4, P])
        L0B = sb("L0B", [P, 3])
        BVROW = sb("BVROW", [1, P])
        ONEROW = sb("ONEROW", [1, P])
        MSK_Q = sb("MSK_Q", [P, NT, S2], U8)
        MSK_T = sb("MSK_T", [S2, T], U8)
        PAD_Q = sb("PAD_Q", [P, B, S2], U8)
        PAD_T = sb("PAD_T", [S2, B], U8)
        l0_loaded = sem("l0_loaded")
        c = carver()
        XM_Q = c(T)
        XM_K = c(S2)
        XM_C = c(S2)
        XM_KB = c(H0 * S2).rearrange("p (h k) -> p h k", h=H0)
        VSTEP = P + DK0
        XM_VB = c(H0 * VSTEP)
        XM_MQ32 = c(NT * S2).rearrange("p (t k) -> p t k", t=NT)
        XM_MQ = c(NT * S2, BF16).rearrange("p (t k) -> p t k", t=NT)
        XM_MT32 = c(T)
        XM_MT = c(T, BF16)
        XM_PADQ = c(B * S2).rearrange("p (b k) -> p b k", b=B)
        XM_PADT = c(B)
        XM_NM = c(NT * H0).rearrange("p (t h) -> p t h", t=NT)
        XM_NMB = c(T, BF16)
        XM_SEL = c(H0, BF16)
        XM_P = [c(T), c(T)]
        XM_RC = c(T)
        XM_CX = c(T)
        HG = [(0, 6), (6, 12), (12, 16)]
        l0_ctx, l0_proj, l0_q, l0_k, l0_v, l0_mask, l0_kb = [sem(n) for n in (
            "l0_ctx", "l0_proj", "l0_q", "l0_k", "l0_v", "l0_mask", "l0_kb")]
        l0_score, l0_max, l0_turn, l0_nmt, l0_st, l0_exp, l0_pv, l0_cx, l0_wo = [sem(n) for n in (
            "l0_score", "l0_max", "l0_turn", "l0_nmt", "l0_st", "l0_exp", "l0_pv", "l0_cx", "l0_wo")]
        l0_vec, l0_masks_vec = sem("l0_vec"), sem("l0_masks_vec")

        def l0x_tensor(pe):
            pe.wait_ge(l0_loaded, 16 * 8)
            pe.wait_ge(l0_masks_vec, 7)
            ln4_tensor(pe, 0)
            with pe.Fori(0, B) as b:
                pe.wait_ge(xn_set, b + 1)
                pe.wait_ge(l0_ctx, b + 1)
                pe.matmul(PS[:, 3, 0:S2], L0W[:, 1, :], XM_C, start=True, stop=True).then_inc(l0_proj, 1)
                pe.matmul(PS[0:S2, 4, 0:P], XM_C, L0W[:, 2, :], start=True, stop=False)
                pe.matmul(PS[0:S2, 4, 0:P], ONEROW[0:1, 0:S2], BVROW[:, :], start=False, stop=True).then_inc(l0_proj, 1)
                pe.matmul(PS[:, 5, :], L0W[:, 0, :], xn, start=True, stop=True).then_inc(l0_proj, 1)
                pe.wait_ge(l0_q, b + 1)
                pe.wait_ge(l0_kb, b + 1)
                pe.wait_ge(l0_mask, 2 * b + 2)
                for t in range(NT):
                    if t:
                        pe.wait_ge(l0_max, b * NT + t)
                    for g, (h0, h1) in enumerate(HG):
                        o = PS[:, g, 0:(h1 - h0) * S2]
                        pe.matmul(o, XM_Q[:, t * P:(t + 1) * P], XM_KB[:, h0:h1, :], start=True, stop=False)
                        mm = pe.matmul(o, IDB[:, :], over(XM_MQ[:, t, :], h1 - h0),
                                       start=False, stop=True)
                    mm.then_inc(l0_score, 1)
                pe.wait_ge(l0_max, b * NT + NT)
                for t in range(NT):
                    mm = pe.transpose(PS[0:H0, 5, t * P:(t + 1) * P], XM_NM[:, t, :], IDF[:, :])
                mm.then_inc(l0_turn, 1)
                pe.wait_ge(l0_nmt, 2 * b + 2)
                pe.wait_ge(l0_v, 2 * b + 2)
                for h in range(H0):
                    o = PS[0:S2, 3 + h % 2, :]
                    if h >= 2:
                        pe.wait_ge(l0_exp, b * H0 + h - 1)
                    pe.matmul(o, XM_KB[:, h, :], XM_Q, start=True, stop=False)
                    pe.matmul(o, IDB[0:S2, 0:S2], XM_MT[0:S2, :], start=False, stop=False)
                    pe.matmul(o, XM_SEL[:, h:h + 1].to_broadcast([P, S2]), XM_NMB, start=False, stop=True).then_inc(l0_st, 1)
                    if h >= 1:
                        l0x_pv(pe, b, h - 1)
                l0x_pv(pe, b, H0 - 1)
                pe.wait_ge(l0_cx, 2 * b + 2)
                pe.matmul(PS[:, 0, :], L0W[:, 3, :], XM_CX, start=True, stop=True).then_inc(l0_wo, 1)

        def l0x_pv(pe, b, h):
            pe.wait_ge(l0_exp, b * H0 + h + 1)
            pe.matmul(PS[:, 1 + h // 8, :], XM_VB[0:S2, h * P:(h + 1) * P], XM_P[h % 2][0:S2, :],
                      start=h % 8 == 0, stop=h % 8 == 7).then_inc(l0_pv, 1)

        def l0x_scalar(act):
            ln4_scalar(act, 0)
            with act.Fori(0, B) as b:
                for h in range(H0):
                    act.wait_ge(l0_st, b * H0 + h + 1)
                    if h >= 2:
                        act.wait_ge(l0_pv, b * H0 + h - 1)
                    act.activation(XM_P[h % 2][0:S2, :], PS[0:S2, 3 + h % 2, :], ACT.Exp).then_inc(l0_exp, 1)

        def l0x_vector(dve):
            st = Steps(dve, l0_masks_vec)
            dve.wait_ge(l0_loaded, 16 * 8)
            st.body(0, 7)
            st.done(dve.memset(XM_NMB, 0.0))
            st.done(dve.tensor_tensor(XM_SEL, IDB[:, 0:H0], IDB[:, 32:32 + H0], ALU.add))
            st.done(dve.tensor_scalar(XM_MQ32, MSK_Q[:, :, :], NEG, None, ALU.mult))
            st.done(dve.tensor_scalar(XM_MT32[0:S2, :], MSK_T[:, :], NEG, None, ALU.mult))
            st.done(dve.tensor_scalar(XM_PADQ, PAD_Q[:, :, :], NEG, None, ALU.mult))
            st.done(dve.tensor_scalar(XM_PADT[0:S2, :], PAD_T[:, :], NEG, None, ALU.mult))
            st.done(dve.memset(XM_VB, 0.0))
            st.settle()
            for h in range(H0):
                at = h * P + 64 + DK0 * (h % 8)
                dve.memset(XM_VB[:, at:at + DK0], 1.0)
            ln4_vector(dve, 0)
            dve.wait_ge(ln_out, 1 + B)
            with dve.Fori(0, B) as b:
                st = Steps(dve, l0_vec)
                st.body(b, 2)
                set_xn(dve, b)
                dve.tensor_tensor(XM_MQ, XM_MQ32, over(XM_PADQ[:, b, :], NT), ALU.min).then_inc(l0_mask, 1)
                dve.tensor_scalar(XM_MT[0:S2, :], XM_MT32[0:S2, :], XM_PADT[0:S2, bass.ts(b, 1)], None, ALU.min).then_inc(l0_mask, 1)
                dve.wait_ge(l0_proj, 3 * b + 2)
                dve.tensor_scalar(XM_K, PS[:, 3, 0:S2], L0B[:, 1:2], None, ALU.add).then_inc(l0_k, 1)
                dve.wait_ge(l0_k, b + 1)
                dve.tensor_tensor(XM_KB, over(XM_K, H0),
                                  along(HMASK[:, :], S2),
                                  ALU.mult).then_inc(l0_kb, 1)
                for g in range(2):
                    vg = XM_VB[0:S2, g * 8 * P:g * 8 * P + 8 * VSTEP].rearrange("p (h e) -> p h e", e=VSTEP)[:, :, 0:DK0]
                    dve.tensor_copy(vg, PS[0:S2, 4, g * 64:(g + 1) * 64].rearrange("p (h e) -> p h e", e=DK0)).then_inc(l0_v, 1)
                dve.wait_ge(l0_proj, 3 * b + 3)
                dve.tensor_scalar(XM_Q, PS[:, 5, :], L0B[:, 0:1], DK0 ** -0.5, ALU.add, ALU.mult).then_inc(l0_q, 1)
                for t in range(NT):
                    dve.wait_ge(l0_score, b * NT + t + 1)
                    for g, (h0, h1) in enumerate(HG):
                        ins = dve.tensor_reduce(XM_NM[:, t, h0:h1],
                                                PS[:, g, 0:(h1 - h0) * S2].rearrange("p (h k) -> p h k", k=S2),
                                                AX, ALU.max, negate=True)
                    ins.then_inc(l0_max, 1)
                dve.wait_ge(l0_turn, b + 1)
                dve.tensor_copy(XM_NMB[0:H0, :], PS[0:H0, 5, :]).then_inc(l0_nmt, 1)
                dve.wait_ge(l0_nmt, 2 * b + 1)
                dve.tensor_tensor(XM_NMB[32:32 + H0, :], PS[0:H0, 5, :], XM_NMB[0:H0, :], ALU.subtract).then_inc(l0_nmt, 1)
                for g in range(2):
                    dve.wait_ge(l0_pv, b * H0 + 8 * g + 8)
                    if g:
                        dve.wait_ge(l0_cx, 2 * b + g)
                    st.done(dve.reciprocal(XM_RC[0:64, :], PS[64:P, 1 + g, :]))
                    st.settle()
                    dve.tensor_tensor(XM_CX[64 * g:64 * g + 64, :], PS[0:64, 1 + g, :], XM_RC[0:64, :],
                                      ALU.mult).then_inc(l0_cx, 1)
                dve.wait_ge(l0_wo, b + 2)
                dve.scalar_tensor_tensor(out=X[:, b, :], in0=PS[:, 0, :], scalar=L0B[:, 2:3], in1=X[:, b, :],
                                         op0=ALU.add, op1=ALU.add).then_inc(x_done, 1)
                st.end()

        def l0x_pool(pool):
            pool.wait_ge(x_loaded, 16)
            pool.memset(XM_C, 0.0).then_inc(l0_wo, 1)
            with pool.Fori(0, B) as b:
                pool.wait_ge(l0_wo, b + 1)
                pool.tensor_copy(XM_C, CT[:, b, :]).then_inc(l0_ctx, 1)

        NE, CAP = 8, 128
        MOEW = sb("MOEW", [P, 8192])
        GW0 = sb("GW0", [P, NE])
        E_G = MOEW[:, 0:2048].rearrange("p (e c m) -> p e c m", e=NE, c=2)
        E_U = MOEW[:, 2048:4096].rearrange("p (e c m) -> p e c m", e=NE, c=2)
        E_D = MOEW[:, 4096:6144].rearrange("p (e c m) -> p e c m", e=NE, c=2)
        l0f_loaded = sem("l0f_loaded")
        c = carver()
        F_XA = XN4
        F_E = c(B * NT * NE).rearrange("p (t e) -> p t e", e=NE)
        F_M = c(B * NT)
        F_S = c(B * NT)
        F_R = c(B * NT)
        F_AFF = c(NT * B * NE).rearrange("p (t j) -> p t j", t=NT)
        F_A = c(T)
        F_W = c(T)
        F_M8 = c(8)
        F_G = c(T)
        F_GB = c(B * T).rearrange("p (b n) -> p b n", b=B)
        F_PB, F_MID, F_R0 = c(T, BF16), c(T, BF16), c(T)
        F_SEL = c(NE, BF16)
        F_SG = [c(T), c(T)]
        F_T = [c(T), c(T)]
        F_H = [c(T), c(T)]
        f_logit, f_neg, f_sub, f_exp, f_sum, f_aff, f_turn, f_gate, f_gb = [sem(n) for n in (
            "f_logit", "f_neg", "f_sub", "f_exp", "f_sum", "f_aff", "f_turn", "f_gate", "f_gb")]
        f_gs = sem("f_gs")
        f_bc, f_gu, f_silu, f_h, f_down, f_vec, f_topk = [sem(n) for n in (
            "f_bc", "f_gu", "f_silu", "f_h", "f_down", "f_vec", "f_topk")]
        N0 = NE * 2

        def l0f_tensor(pe):
            pe.wait_ge(l0f_loaded, 16 * 4)
            ln4_tensor(pe, 4)
            pe.wait_ge(ln_out, 5 + B)
            for j in range(B * NT):
                b, t = j // NT, j % NT
                mm = pe.matmul(PS[:, 5, j * NE:(j + 1) * NE], XN4[:, b, t * P:(t + 1) * P], GW0[:, :], start=True, stop=True)
            mm.then_inc(f_logit, 1)
            pe.wait_ge(f_aff, 1)
            for t in range(NT):
                mm = pe.transpose(PS[0:B * NE, 1, t * P:(t + 1) * P], F_AFF[:, t, :], IDF[:, :])
            mm.then_inc(f_turn, 1)
            with pe.Fori(0, B) as b:
                for i in range(N0):
                    e, h = i // 2, i % 2
                    if i >= 2:
                        pe.wait_ge(f_h, b * N0 + i - 1)
                    pe.matmul(PS[:, 2 + i % 2, :], E_G[:, e, h, :], F_XA[:, b, :], start=True, stop=True)
                    pe.matmul(PS[:, [4, 6][i % 2], :], E_U[:, e, h, :], F_XA[:, b, :], start=True, stop=True).then_inc(f_gu, 1)
                    if i == 0:
                        continue
                    if i == 1 or h == 0:
                        if i == 1:
                            pe.wait_ge(f_gs, 5 * b + 5)
                        if e >= 2:
                            pe.wait_ge(f_h, b * N0 + 2 * (e - 1))
                        pe.matmul(PS[:, 5 * (e % 2), :], F_SEL[:, e:e + 1].to_broadcast([P, P]), F_PB, start=True, stop=True).then_inc(f_bc, 1)
                    l0f_down(pe, b, i - 1)
                l0f_down(pe, b, N0 - 1)

        def l0f_down(pe, b, i):
            pe.wait_ge(f_h, b * N0 + i + 1)
            pe.matmul(PS[:, 1, :], E_D[:, i // 2, i % 2, :], F_H[i % 2], start=i == 0, stop=i == N0 - 1).then_inc(f_down, 1)

        def l0f_scalar(act):
            ln4_scalar(act, 4)
            act.wait_ge(f_sub, 1)
            act.activation(F_E, F_E, ACT.Exp).then_inc(f_exp, 1)
            with act.Fori(0, B) as b:
                for i in range(N0):
                    act.wait_ge(f_gu, b * N0 + i + 1)
                    if i >= 2:
                        act.wait_ge(f_h, b * N0 + i - 1)
                    act.activation(F_SG[i % 2], PS[:, 2 + i % 2, :], ACT.Silu).then_inc(f_silu, 1)

        def l0f_vector(dve):
            st = Steps(dve, f_vec)
            ln4_vector(dve, 4)
            dve.wait_ge(f_logit, 1)
            lg = PS[:, 5, 0:B * NT * NE].rearrange("p (t e) -> p t e", e=NE)
            dve.tensor_reduce(F_M, lg, AX, ALU.max, negate=True).then_inc(f_neg, 1)
            dve.wait_ge(f_neg, 1)
            dve.tensor_tensor(F_E, lg, along(F_M, NE), ALU.add).then_inc(f_sub, 1)
            dve.wait_ge(f_exp, 1)
            st.done(dve.tensor_reduce(F_S, F_E, AX, ALU.add))
            st.settle()
            st.done(dve.reciprocal(F_R, F_S))
            st.settle()
            dve.tensor_tensor(F_AFF.rearrange("p t (b e) -> p b t e", b=B), F_E.rearrange("p (b t) e -> p b t e", b=B),
                              along(F_R, NE).rearrange("p (b t) e -> p b t e", b=B), ALU.mult).then_inc(f_aff, 1)
            dve.wait_ge(f_turn, 1)
            tk = Steps(dve, f_topk)
            tk.done(dve.tensor_copy(F_A[0:B * NE, :], PS[0:B * NE, 1, :]))
            tk.done(dve.tensor_copy(F_W[0:B * NE, :], PS[0:B * NE, 1, :]))
            tk.done(dve.tensor_tensor(F_SEL, IDB[:, 0:NE], IDB[:, 32:32 + NE], ALU.add))
            tk.settle()
            tk.done(dve.tensor_tensor(F_SEL, F_SEL, IDB[:, 64:64 + NE], ALU.add))
            tk.done(dve.memset(F_PB, 0.0))
            for r in range(CAP // 8):
                tk.done(dve.max(F_M8[0:B * NE, :], F_W[0:B * NE, :]))
                tk.settle()
                tk.done(dve.match_replace(out=F_W[0:B * NE, :], in_to_replace=F_M8[0:B * NE, :], in_values=F_W[0:B * NE, :], imm_value=-1.0))
                tk.settle()
            dve.scalar_tensor_tensor(out=F_G[0:B * NE, :], in0=F_W[0:B * NE, :], scalar=0.0, in1=F_A[0:B * NE, :],
                                     op0=ALU.is_lt, op1=ALU.mult).then_inc(f_gate, 1)
            dve.wait_ge(f_gb, 16 * B)
            with dve.Fori(0, B) as b:
                gate, r0, mid = F_GB[0:NE, b, :], F_R0[0:NE, :], F_MID[0:NE, :]
                dve.tensor_scalar(F_PB[0:NE, :], gate, 1.0, None, ALU.mult).then_inc(f_gs, 1)
                dve.wait_ge(f_gs, 5 * b + 1)
                dve.tensor_tensor(r0, gate, F_PB[0:NE, :], ALU.subtract).then_inc(f_gs, 1)
                dve.wait_ge(f_gs, 5 * b + 2)
                dve.tensor_scalar(mid, r0, 1.0, None, ALU.mult).then_inc(f_gs, 1)
                dve.wait_ge(f_gs, 5 * b + 3)
                dve.tensor_tensor(F_PB[64:64 + NE, :], r0, mid, ALU.subtract).then_inc(f_gs, 1)
                dve.tensor_scalar(F_PB[32:32 + NE, :], mid, 1.0, None, ALU.mult).then_inc(f_gs, 1)
                for i in range(N0):
                    dve.wait_ge(f_silu, b * N0 + i + 1)
                    st2 = F_T[i % 2]
                    dve.tensor_tensor(st2, F_SG[i % 2], PS[:, [4, 6][i % 2], :], ALU.mult).then_inc(f_neg, 1)
                    dve.wait_ge(f_neg, b * N0 + i + 2)
                    dve.wait_ge(f_bc, b * NE + i // 2 + 1)
                    if i >= 2:
                        dve.wait_ge(f_down, b * N0 + i - 1)
                    dve.tensor_tensor(F_H[i % 2], st2, PS[:, 5 * (i // 2 % 2), :], ALU.mult).then_inc(f_h, 1)
                dve.wait_ge(f_down, (b + 1) * N0)
                dve.tensor_tensor(X[:, b, :], X[:, b, :], PS[:, 1, :], ALU.add).then_inc(x_done, 1)

        L1W = sb("L1W", [P, 7, P])
        L1CW = sb("L1CW", [P, 2])
        L1G = sb("L1G", [P, 1])
        PTR_I = sb("PTR_I", [P, B * NT], I32)
        IDS_I = sb("IDS_I", [P, B, S2], I32)
        IOTA = sb("IOTA", [P, S2])
        l1x_loaded = sem("l1x_loaded")
        c = carver()
        A_C = c(S2)
        A_Q = c(2 * T).rearrange("p (j n) -> p j n", j=2)
        A_K = c(2 * S2).rearrange("p (j k) -> p j k", j=2)
        A_V = c(2 * P).rearrange("p (j d) -> p j d", j=2)
        A_PTR = c(B * NT)
        A_IX = c(3 * B * NT).rearrange("p (w b t) -> p w b t", w=3, b=B)
        A_IDS = c(B * S2).rearrange("p (b k) -> p b k", b=B)
        A_OH = c(3 * NT * S2).rearrange("p (w k) -> p w k", w=3 * NT)
        A_T = c(3 * NT * S2).rearrange("p (w k) -> p w k", w=3 * NT)
        A_L = c(2 * 3 * NT).rearrange("p (j w) -> p j w", j=2)
        A_N = c(16 * NT).rearrange("p (i t) -> p i t", t=NT)
        A_M = c(2 * NT).rearrange("p (j t) -> p j t", j=2)
        A_P = c(2 * NT * S2).rearrange("p (j t k) -> p j t k", j=2, t=NT)
        A_PT = c(2 * T).rearrange("p (j n) -> p j n", j=2)
        A_CX = c(T)
        A_W = c(2)
        A_WM = c(4)
        a_ctx, a_proj, a_q, a_kv, a_score, a_sub, a_exp, a_p, a_turn, a_pt, a_cx, a_cxs, a_out, a_vec, a_pre, a_we = [
            sem(n) for n in ("a_ctx", "a_proj", "a_q", "a_kv", "a_score", "a_sub", "a_exp", "a_p", "a_turn", "a_pt",
                             "a_cx", "a_cxs", "a_out", "a_vec", "a_pre", "a_we")]
        PSC = PS[:, 0:2, :].rearrange("p g (u j z) -> p (g u) j z", u=2, j=2)[:, :, :, 0:S2]

        def l1x_tensor(pe):
            pe.wait_ge(l1x_loaded, 16 * 6)
            ln4_tensor(pe, 8)
            with pe.Fori(0, B) as b:
                pe.wait_ge(xn_set, b + 5)
                pe.wait_ge(a_ctx, b + 1)
                for j in range(2):
                    pe.matmul(PS[:, 4, j * P:j * P + S2], L1W[:, 2 + j, :], A_C, start=True, stop=True)
                for j in range(2):
                    mm = pe.matmul(PS[0:S2, 5, j * P:(j + 1) * P], A_C, L1W[:, 4 + j, :], start=True, stop=True)
                mm.then_inc(a_proj, 1)
                for j in range(2):
                    mm = pe.matmul(PS[:, 2 + j, :], L1W[:, j, :], xn, start=True, stop=True)
                mm.then_inc(a_proj, 1)
                pe.wait_ge(a_q, 2 * b + 2)
                pe.wait_ge(a_kv, b + 1)
                for t in range(NT):
                    for j in range(2):
                        mm = pe.matmul(PSC[:, t, j, :], A_Q[:, j, t * P:(t + 1) * P], A_K[:, j, :], start=True, stop=True)
                mm.then_inc(a_score, 1)
                pe.wait_ge(a_p, b + 1)
                for j in range(2):
                    for t in range(NT):
                        mm = pe.transpose(PS[0:S2, 2 + j, t * P:(t + 1) * P], A_P[:, j, t, :], IDF[:, :])
                mm.then_inc(a_turn, 1)
                pe.wait_ge(a_pt, 2 * b + 2)
                for j in range(2):
                    mm = pe.matmul(PS[:, 4, :], A_V[0:S2, j, :], A_PT[0:S2, j, :], start=j == 0, stop=j == 1)
                mm.then_inc(a_cx, 1)
                pe.wait_ge(a_cxs, b + 1)
                pe.matmul(PS[:, 5, :], L1W[:, 6, :], A_CX, start=True, stop=True).then_inc(a_out, 1)

        def l1x_scalar(act):
            act.wait_ge(a_sub, 1)
            act.activation(A_W, A_W, ACT.Exp).then_inc(a_we, 1)
            ln4_scalar(act, 8)
            with act.Fori(0, B) as b:
                act.wait_ge(a_proj, 2 * b + 2)
                for j in range(2):
                    act.activation(A_Q[:, j, :], PS[:, 2 + j, :], ACT.Copy, scale=P ** -0.5).then_inc(a_q, 1)
                act.wait_ge(a_sub, b + 2)
                act.activation(A_L, A_L, ACT.Exp).then_inc(a_exp, 1)
                act.wait_ge(a_turn, b + 1)
                for j in range(2):
                    act.activation(A_PT[0:S2, j, :], PS[0:S2, 2 + j, :], ACT.Copy).then_inc(a_pt, 1)
                act.wait_ge(a_cx, b + 1)
                act.activation(A_CX, PS[:, 4, :], ACT.Copy).then_inc(a_cxs, 1)

        def l1x_vector(dve):
            dve.wait_ge(l1x_loaded, 16 * 6)
            pre = Steps(dve, a_pre)

            def once(ins):
                pre.done(ins)
                pre.settle()
            once(dve.tensor_reduce(A_WM[:, 0:1], L1CW[:, :], AX, ALU.max, negate=True))
            dve.tensor_scalar(A_W, L1CW[:, :], A_WM[:, 0:1], None, ALU.add).then_inc(a_sub, 1)
            dve.wait_ge(a_we, 1)
            once(dve.tensor_reduce(A_WM[:, 1:2], A_W, AX, ALU.add))
            once(dve.reciprocal(A_WM[:, 2:3], A_WM[:, 1:2]))
            once(dve.tensor_scalar(A_W, A_W, A_WM[:, 2:3], None, ALU.mult))
            once(dve.tensor_copy(A_PTR, PTR_I[:, :]))
            once(dve.tensor_copy(A_IDS, IDS_I[:, :, :]))
            for w in range(3):
                ix = A_IX[:, w, :, :]
                once(dve.tensor_scalar(ix, A_PTR.rearrange("p (b t) -> p b t", b=B), float(w), float(S2 - 1), ALU.add, ALU.min))
                once(dve.tensor_scalar(ix, ix, 0.0, None, ALU.max))
            st = Steps(dve, a_vec)
            ln4_vector(dve, 8)
            dve.wait_ge(ln_out, 9 + B)
            with dve.Fori(0, B) as b:
                st.body(b, 45)

                def step(ins):
                    st.done(ins)
                    st.settle()
                set_xn(dve, b)
                dve.wait_ge(a_proj, 2 * b + 1)
                step(dve.tensor_copy(A_K, PS[:, 4, 0:2 * P].rearrange("p (j z) -> p j z", j=2)[:, :, 0:S2]))
                for j in range(2):
                    ins = dve.tensor_scalar(A_V[0:S2, j, :], PS[0:S2, 5, j * P:(j + 1) * P], A_W[0:S2, j:j + 1], None, ALU.mult)
                    if j == 0:
                        step(ins)
                ins.then_inc(a_kv, 1)
                for w in range(3):
                    step(dve.tensor_tensor(A_OH[:, w * NT:(w + 1) * NT, :], over(IOTA[:, :], NT), along(A_IX[:, w, b, :], S2), ALU.is_equal))
                step(dve.tensor_tensor(A_T[:, 0:NT, :], A_OH[:, 0:NT, :], over(A_IDS[:, b, :], NT), ALU.mult))
                rel, acc = A_N[:, 0, :], A_N[:, 1, :]
                step(dve.tensor_reduce(rel, A_T[:, 0:NT, :], AX, ALU.add))
                dve.wait_ge(a_score, b + 1)
                for j in range(2):
                    s = PSC[:, :, j, :].rearrange("p t (o k) -> p o t k", o=1).to_broadcast([P, 3, NT, S2])
                    step(dve.tensor_tensor(A_T.rearrange("p (w t) k -> p w t k", w=3), A_OH.rearrange("p (w t) k -> p w t k", w=3), s, ALU.mult))
                    step(dve.tensor_reduce(A_L[:, j, :], A_T, AX, ALU.add))
                l_rel, v1, v2 = [A_L[:, 0, w * NT:(w + 1) * NT] for w in range(3)]
                plus, most, less, imply, diff, xor = [A_N[:, i, :] for i in range(2, 8)]
                none, tmp = A_N[:, 8, :], A_N[:, 9, :]
                step(dve.tensor_tensor(plus, v1, v2, ALU.add))
                step(dve.tensor_tensor(most, v1, v2, ALU.max))
                step(dve.tensor_scalar(less, v1, -1.0, None, ALU.mult))
                step(dve.tensor_tensor(imply, less, v2, ALU.max))
                step(dve.tensor_tensor(diff, v1, v2, ALU.subtract))
                step(dve.scalar_tensor_tensor(out=xor, in0=diff, scalar=-1.0, in1=diff, op0=ALU.mult, op1=ALU.max))
                step(dve.tensor_scalar(tmp, rel, 4.0, None, ALU.is_gt))
                step(dve.scalar_tensor_tensor(out=none, in0=rel, scalar=0.0, in1=tmp, op0=ALU.is_lt, op1=ALU.max))
                step(dve.tensor_tensor(acc, none, l_rel, ALU.mult))
                for rule, term in enumerate((plus, most, less, imply, xor)):
                    step(dve.scalar_tensor_tensor(out=tmp, in0=rel, scalar=float(rule), in1=term, op0=ALU.is_equal, op1=ALU.mult))
                    step(dve.tensor_tensor(l_rel if rule == 4 else acc, acc, tmp, ALU.add))
                L = A_L.rearrange("p j (w t) -> p j w t", w=3)
                step(dve.tensor_tensor(A_M, L[:, :, 0, :], L[:, :, 1, :], ALU.max))
                step(dve.tensor_tensor(A_M, A_M, L[:, :, 2, :], ALU.max))
                for w in range(3):
                    ins = dve.tensor_tensor(L[:, :, w, :], L[:, :, w, :], A_M, ALU.subtract)
                    if w < 2:
                        step(ins)
                ins.then_inc(a_sub, 1)
                dve.wait_ge(a_exp, b + 1)
                step(dve.tensor_tensor(A_M, L[:, :, 0, :], L[:, :, 1, :], ALU.add))
                step(dve.tensor_tensor(A_M, A_M, L[:, :, 2, :], ALU.add))
                step(dve.reciprocal(A_M, A_M))
                for w in range(3):
                    step(dve.tensor_tensor(L[:, :, w, :], L[:, :, w, :], A_M, ALU.mult))
                for j in range(2):
                    step(dve.tensor_tensor(A_T, A_OH, along(A_L[:, j, :], S2), ALU.mult))
                    step(dve.tensor_tensor(A_P[:, j, :, :], A_T[:, 0:NT, :], A_T[:, NT:2 * NT, :], ALU.add))
                    ins = dve.tensor_tensor(A_P[:, j, :, :], A_P[:, j, :, :], A_T[:, 2 * NT:3 * NT, :], ALU.add)
                    if j == 0:
                        step(ins)
                ins.then_inc(a_p, 1)
                dve.wait_ge(a_out, b + 1)
                dve.scalar_tensor_tensor(out=X[:, b, :], in0=PS[:, 5, :], scalar=L1G[:, 0:1], in1=X[:, b, :],
                                         op0=ALU.mult, op1=ALU.add).then_inc(x_done, 1)
                st.end()

        def l1x_pool(pool):
            with pool.Fori(0, B) as b:
                pool.wait_ge(x_done, b + 8)
                pool.tensor_copy(A_C, CT[:, b, :]).then_inc(a_ctx, 1)

        DEPTH, NH, DH, WIN = 6, 16, 64, 32
        NPAIR = NH // 2
        DI = 341
        FF = [(0, 128), (128, 128), (256, DI - 256)]
        SPAN = P + WIN
        Y = sb("Y", [P, B, T + 1])
        WQKV = sb("WQKV", [P, 2 * 3 * T])
        W_QKV = WQKV[:, :].rearrange("p (g s n) -> p g s n", g=2, s=3)
        WO = sb("WO", [P, NPAIR, P])
        W1 = sb("W1", [P, 2 * DI])
        W2 = sb("W2", [P, 3, P])
        LNGB = sb("LNGB", [P, 2])
        B1 = sb("B1", [P, 3, 2])
        B2 = sb("B2", [P, 1])
        ROPE = sb("ROPE", [P, 4, NT, DH])
        QKS = sb("QKS", [P, 4, DH])
        BANDS = sb("BANDS", [P, 3, SPAN], BF16)
        BANDS32 = sb("BANDS32", [P, 3, SPAN])
        V_ALL = MOEW[:, :].rearrange("p (t h e) -> p t h e", t=NT, h=NH)
        NMSEL = sb("NMSEL", [P, 8], BF16)
        l1_const, w_qkv, w_o, w_ff, w_qks = sem("l1_const"), [sem("w_qkv0"), sem("w_qkv1")], sem("w_o"), sem("w_ff"), sem("w_qks")
        c = carver()
        L_SH = c(T)
        L_TAB = c(4 * NT * DH).rearrange("p (i t d) -> p i t d", i=4, t=NT)
        L_QT = c(NPAIR * (T + WIN)).rearrange("p (h n) -> p h n", h=NPAIR)
        L_KT = c(NPAIR * (WIN + T)).rearrange("p (h n) -> p h n", h=NPAIR)
        L_QB = c(4 * T, BF16).rearrange("p (h n) -> p h n", h=4)
        L_KB = c(4 * (WIN + T), BF16).rearrange("p (h n) -> p h n", h=4)
        L_CX = c(NPAIR * T).rearrange("p (h n) -> p h n", h=NPAIR)
        L_P = [c(NT * SPAN).rearrange("p (t n) -> p t n", t=NT) for _ in range(4)]
        L_DN = [c(T), c(T)]
        L_NM = c(NT * 8).rearrange("p (t h) -> p t h", t=NT)
        L_NMB = c(T + WIN, BF16)
        L_ONE = c(1)
        L_ONE4 = L_ONE.rearrange("p (o u) -> p o u", o=1)
        L_SS, L_SD = c(64), c(64)
        L_RAW, L_SQ, L_T2 = [[c(T), c(T)] for _ in range(3)]
        L_QK = [c(T) for _ in range(8)]
        L_SF = L_XG = L_CX[:, 4, :]
        L_H = [L_CX[:, 5 + m, :] for m in range(3)]
        (p_sh, p_proj, p_raw, p_sq, p_t1, p_t12, p_add, p_ss, p_sd, p_rn, p_qk, p_turn, p_tev, p_cast, p_v, p_s, p_max,
         p_st, p_exp, p_pv, p_den, p_rd, p_cx, p_out, p_y, p_sf, p_xg, p_ga, p_gelu, p_h, p_tab, p_pre) = [
            sem("p_" + n) for n in (
                "sh proj raw sq t1 t12 add ss sd rn qk turn tev cast v s max "
                "st exp pv den rd cx out y sf xg ga gelu h tab pre").split()]
        PROJ, TURN, PV0 = 4, 5, 6
        NJ, NV = 8, NT
        NP = NJ + NV
        NPT = 20

        ORDER = {
            "pe": [
                "S0 P0 S1 P1 S2 P2 P3 S3 P4 M P5 T0 P6 T1 P7 C0 P8 C1 P9 T2 P10 P11 C2 P12 P13 P14 P15 T3 P16 P17 C3",
                "P0 P1 S0 P2 F0 P3 S1 F1 P4 S2 P5 F2 S3 P6 F3 M P7 F4 T0 P8 F5 T1 F6 P9 F7 P10 C0 P11 C1 T2 P12 P13 C2 T3 P14 C3 P15 P16 P17",
            ],
            "act": [
                "P0 P1 P2 P3 P4 P5 T0 P6 T1 P7 C0 P8 P9 C1 T2 P10 P11 P12 P13 P14 C2 P15 T3 P16 P17 C3",
                "P0 P1 P2 P3 P4 F1 P5 F2 P6 F4 P7 T0 F5 P8 F6 P9 P10 T1 C0 C1 P11 T2 P12 C2 P13 T3 P14 C3 P15 P16 P17",
            ],
            "dve": [
                "N S0 S1 P0 P1 S2 P2 S3 M P3 P4 P5 P6 P7 P9 P10 D0 P11 D1 P12 D2 D3",
                "S0 P0 P1 P2 F0 S1 P3 F1 S2 P4 F2 S3 F3 M P5 F4 P6 P7 F5 P9 P10 F6 P11 F7 P12 D0 D1 D2 D3",
            ],
        }

        def order(engine, g, projecting, ff):
            return [(w[0], int(w[1:] or 0)) for w in ORDER[engine][1 - g].split()
                    if (projecting or w[0] not in "PN") and (ff or w[0] != "F")]

        def through_units(eng, half_batch, feed):
            def two(i, b, l, nb, nl, new_layer):
                half_batch(1, 2 * i + 1, i + 1, nb, nl, None, new_layer)
                half_batch(0, 2 * i + 2, i + 1, nb, nl, (i, b, l), new_layer)

            nc.disable_value_cache = True
            half_batch(0, 0, 0, 0, 0, None, False)
            with eng.Fori(0, DEPTH - 1) as l:
                with eng.Fori(0, B - 1) as b:
                    two(l * B + b, b, l, b + 1, l, False)
                two(l * B + B - 1, B - 1, l, 0, l + 1, True)
            with eng.Fori(0, B - 1) as b:
                two((DEPTH - 1) * B + b, b, DEPTH - 1, b + 1, DEPTH - 1, False)
            last = DEPTH * B - 1
            half_batch(1, 2 * last + 1, None, None, None, None, False)
            feed(last, B - 1, DEPTH - 1)
            nc.disable_value_cache = False

        def score_tiles(g):
            return PS[:, 2 * g:2 * g + 2, :].rearrange("p g (u z) -> p (g u) z", u=2)[:, :, 0:SPAN]

        def is_first(u):
            return isinstance(u, int) and u == 0

        def turn_bank(j):
            return PROJ if j >= 3 and j % 2 else TURN

        def half(h):
            return slice(DH * (h % 2), DH * (h % 2) + DH)

        def l1f_tensor(pe):
            ln4_tensor(pe, 12)
            pe.wait_ge(p_pre, 8)
            pe.wait_ge(ln_out, 17)
            for p in range(NPT):
                l1f_project(pe, 0, 0, 0, 0, p)

            def half_batch(g, u, pi, nb, nl, ff, new_layer):
                for what, n in order("pe", g, pi is not None, ff):
                    if what == "P":
                        l1f_project(pe, u + 1, 1 - g, pi, nl, n)
                    elif what == "S":
                        if n == 0:
                            pe.wait_ge(p_cast, 8 * u + 8)
                            pe.wait_ge(p_v, NV * u + NV)
                        else:
                            pe.wait_ge(p_max, 10 * u + 2 * n)
                        for t in range(NT):
                            for v in range(2):
                                r = half(v)
                                pe.matmul(score_tiles(v)[:, t, :], L_QB[r, n, t * P:(t + 1) * P], L_KB[r, n, t * P:t * P + SPAN],
                                          start=t % 2 == 0, stop=False, skip_group_check=True)
                        for v in range(2):
                            for t in range(NT):
                                mm = pe.matmul(score_tiles(v)[:, t, :], IDB[:, :], BANDS[:, 1 if t else 0, :],
                                               start=False, stop=t % 2 == 1, skip_group_check=True)
                            mm.then_inc(p_s, 1)
                    elif what == "M":
                        pe.wait_ge(p_max, 10 * u + 8)
                        for t in range(NT):
                            mm = pe.transpose(PS[0:8, 0, t * P:(t + 1) * P], L_NM[:, t, :], IDF[:, :])
                        mm.then_inc(p_s, 1)
                    elif what == "T":
                        if n == 0:
                            pe.wait_ge(p_max, 10 * u + 10)
                        else:
                            pe.wait_ge(p_exp, 8 * u + 2 * n)
                        pair = 4 * g + n
                        for t in range(NT):
                            for v in range(2):
                                r = half(v)
                                pe.matmul(score_tiles(v)[:, t, :], L_KT[r, pair, WIN + t * P:WIN + (t + 1) * P],
                                          L_QT[r, pair, t * P:t * P + SPAN], start=t % 2 == 0, stop=False,
                                          skip_group_check=True)
                        for v in range(2):
                            s, h = score_tiles(v), 2 * n + v
                            for t in range(NT):
                                pe.matmul(s[:, t, :], IDB[:, :], BANDS[:, 2, :], start=False, stop=False, skip_group_check=True)
                                mm = pe.matmul(s[:, t, :], NMSEL[:, h:h + 1].to_broadcast([P, P]), L_NMB[:, t * P:t * P + SPAN],
                                               start=False, stop=t % 2 == 1, skip_group_check=True)
                            mm.then_inc(p_st, 1)
                    elif what == "C":
                        if n == 0 and ff:
                            pe.wait_ge(p_y, 2 * ff[0] + 3)
                        elif n == 0 and not is_first(u):
                            pe.wait_ge(p_den, 8 * u)
                        l1f_pv(pe, u, g, 2 * n)
                        l1f_pv(pe, u, g, 2 * n + 1)
                    elif what == "F":
                        l1f_ff_tensor(pe, ff[0], ff[2], n)

            def feed(i, b, l):
                for n in range(8):
                    l1f_ff_tensor(pe, i, l, n)
            through_units(pe, half_batch, feed)

        def l1f_project(pe, u, g, i, l, p):
            if p < NP:
                if p == 0:
                    pe.wait_ge(w_qkv[g], 16 * l + 16)
                    pe.wait_ge(p_sh, i + 1)
                    if not is_first(u):
                        pe.wait_ge(p_tev, NJ * u)
                elif p <= NJ:
                    pe.wait_ge(p_raw, NJ * u + p)
                else:
                    pe.wait_ge(p_v, NV * u + p - NJ)
                t, q = (p // 2, p % 2) if p < NJ else (p - NJ, 2)
                pe.matmul(PS[:, PROJ, :], L_SH[:, t * P:(t + 1) * P], W_QKV[:, g, q, :], start=True, stop=True).then_inc(p_proj, 1)
            j = p - 10
            if 0 <= j < NJ:
                pe.wait_ge(p_qk, NJ * u + j + 1)
                if j in (1, 2) or (j == 0 and not is_first(u)):
                    pe.wait_ge(p_tev, NJ * u + j)
                elif j == 3:
                    pe.wait_ge(p_v, NV * u + NV)
                elif j >= 4:
                    pe.wait_ge(p_tev, NJ * u + j - 1)
                for h in range(4):
                    mm = pe.transpose(PS[:, turn_bank(j), h * P:(h + 1) * P], L_QK[j][:, h * P:(h + 1) * P], IDF[:, :])
                mm.then_inc(p_turn, 1)

        def l1f_pv(pe, u, g, h):
            pe.wait_ge(p_exp, 8 * u + h + 1)
            if h >= 2:
                pe.wait_ge(p_den, 8 * u + h - 1)
            for t in range(NT):
                w = min(SPAN, T - t * P)
                mm = pe.matmul(PS[:, PV0 + h % 2, t * P:t * P + w], V_ALL[:, t, 8 * g + h, :], L_P[h % 4][:, t, 0:w],
                               start=t == 0, stop=t == NT - 1, skip_group_check=True)
            mm.then_inc(p_pv, 1)

        def l1f_ff_tensor(pe, i, l, s):
            if s == 0:
                pe.wait_ge(w_o, 16 * l + 16)
                pe.wait_ge(p_den, 16 * i + 16)
                pe.wait_ge(p_cx, 8 * i + 8)
                for h in range(NPAIR):
                    mm = pe.matmul(PS[:, 7, :], WO[:, h, :], L_CX[:, h, :], start=h == 0, stop=h == NPAIR - 1)
                mm.then_inc(p_out, 1)
            elif s == 1:
                pe.wait_ge(p_sf, i + 1)
                ln_tensor_mean(pe, i + 16, L_SF)
            elif s == 2:
                ln_tensor_var(pe, i + 16)
            elif s == 3:
                ln_tensor_out(pe, i + 16)
            elif s < 7:
                m, (m0, mw) = s - 4, FF[s - 4]
                if m == 0:
                    pe.wait_ge(w_ff, 112 * l + 112)
                    pe.wait_ge(p_xg, i + 1)
                else:
                    pe.wait_ge(p_h, 3 * i + m)
                pe.matmul(PS[0:mw, 6, :], W1[:, DI + m0:DI + m0 + mw], L_XG, start=True, stop=True)
                pe.matmul(PS[0:mw, 7, :], W1[:, m0:m0 + mw], L_XG, start=True, stop=True).then_inc(p_ga, 1)
            else:
                pe.wait_ge(p_h, 3 * i + 3)
                for m, (m0, mw) in enumerate(FF):
                    mm = pe.matmul(PS[:, 6, :], W2[0:mw, m, :], L_H[m][0:mw, :], start=m == 0, stop=m == 2)
                mm.then_inc(p_out, 1)

        def l1f_scalar(act):
            ln4_scalar(act, 12)
            for p in range(NPT):
                l1f_project_scalar(act, 0, 0, p)

            def half_batch(g, u, pi, nb, nl, ff, new_layer):
                for what, n in order("act", g, pi is not None, ff):
                    if what == "P":
                        l1f_project_scalar(act, u + 1, 1 - g, n)
                    elif what == "T":
                        for h in (2 * n, 2 * n + 1):
                            act.wait_ge(p_st, 8 * u + h + 1)
                            if h >= 4:
                                act.wait_ge(p_pv, 8 * u + h - 3)
                            act.activation(L_P[h % 4], score_tiles(h % 2), ACT.Exp).then_inc(p_exp, 1)
                    elif what == "C":
                        if n == 0 and ff:
                            act.wait_ge(p_out, 2 * ff[0] + 1)
                        l1f_leave(act, u, g, 2 * n)
                        l1f_leave(act, u, g, 2 * n + 1)
                    elif what == "F":
                        l1f_ff_scalar(act, ff[0], n)

            def feed(i, b, l):
                for n in range(8):
                    l1f_ff_scalar(act, i, n)
            through_units(act, half_batch, feed)

        def l1f_ff_scalar(act, i, s):
            if s == 1:
                ln_scalar_square(act, i + 16)
            elif s == 2:
                ln_scalar_sd(act, i + 16)
            elif 4 <= s < 7:
                m, (m0, mw) = s - 4, FF[s - 4]
                act.wait_ge(p_ga, 3 * i + m + 1)
                act.activation(L_H[m][0:mw, :], PS[0:mw, 6, :], ACT.Gelu, bias=B1[0:mw, m, 1:2]).then_inc(p_gelu, 1)

        def l1f_project_scalar(act, u, g, p):
            if p < NP:
                act.wait_ge(p_proj, NP * u + p + 1)
            if p < NJ:
                if p >= 2 or not is_first(u):
                    act.wait_ge(p_ss, NJ * u + p - 1)
                act.activation(L_SQ[p % 2], PS[:, PROJ, :], ACT.Square).then_inc(p_sq, 1)
                if p >= 2 or not is_first(u):
                    act.wait_ge(p_add, NJ * u + p - 1)
                act.activation(L_RAW[p % 2], PS[:, PROJ, :], ACT.Copy).then_inc(p_raw, 1)
            elif p < NP:
                src = PS[:, PROJ, :].rearrange("p (h u d) -> p h u d", u=2, d=DH)
                dst = V_ALL[:, p - NJ, 8 * g:8 * g + 8, :].rearrange("p (h u) e -> p h u e", u=2)
                act.activation(dst[:, :, 0, 0:DH], src[:, :, 0, :], ACT.Copy)
                act.activation(dst[:, :, 1, DH:P], src[:, :, 1, :], ACT.Copy).then_inc(p_v, 1)
            if p == NJ:
                act.wait_ge(p_ss, NJ * u + NJ)
                act.activation(L_SD, L_SS, ACT.Sqrt).then_inc(p_sd, 1)
            j = p - 10
            if 0 <= j < NJ:
                t, dst = j // 2, (L_QT, L_KT)[j % 2]
                t0 = t * P + (WIN if j % 2 else 0)
                act.wait_ge(p_turn, NJ * u + j + 1)
                act.activation(dst[:, 4 * g:4 * g + 4, t0:t0 + P], PS[:, turn_bank(j), :].rearrange("p (h n) -> p h n", h=4),
                               ACT.Copy).then_inc(p_tev, 1)

        def l1f_leave(act, u, g, h):
            act.wait_ge(p_pv, 8 * u + h + 1)
            k = h // 2
            if h % 2 == 0 and (k >= 2 or not is_first(u)):
                act.wait_ge(p_cx, 4 * u + k - 1)
            r, other = half(h), half(h + 1)
            act.activation(L_DN[k % 2][r, :], PS[other, PV0 + h % 2, :], ACT.Copy)
            act.activation(L_CX[r, 4 * g + k, :], PS[r, PV0 + h % 2, :], ACT.Copy).then_inc(p_den, 1)

        def l1f_vector(dve):
            dve.wait_ge(l1_const, 16 * 2)
            dve.memset(Y[:, :, 0:1], 0.0).then_inc(p_y, 1)
            dve.memset(L_KT[:, :, 0:WIN], 0.0).then_inc(p_pre, 1)
            dve.memset(L_KB[:, :, 0:WIN], 0.0).then_inc(p_pre, 1)
            dve.memset(V_ALL, 1.0).then_inc(p_pre, 1)
            dve.memset(L_NMB, 0.0).then_inc(p_pre, 1)
            dve.memset(L_ONE, 1.0).then_inc(p_pre, 1)
            dve.memset(L_QT[:, :, T:T + WIN], 0.0).then_inc(p_pre, 1)
            dve.tensor_copy(BANDS[:, :, :], BANDS32[:, :, :]).then_inc(p_pre, 1)
            dve.tensor_tensor(NMSEL[:, :], IDB[:, 0:8], IDB[:, 32:40], ALU.add).then_inc(p_pre, 1)
            ln4_vector(dve, 12)
            dve.wait_ge(ln_out, 13 + B)
            dve.wait_ge(p_y, 1)
            dve.tensor_scalar(Y[:, :, 1:T + 1], XN4, 1.0, None, ALU.mult).then_inc(p_pre, 1)
            dve.wait_ge(p_pre, 9)
            dve.wait_ge(p_y, 1)
            l1f_tables(dve, 0)
            l1f_shift(dve, 0, L_SH, p_sh)
            for p in range(NPT):
                l1f_project_vector(dve, 0, p)

            def half_batch(g, u, pi, nb, nl, ff, new_layer):
                for what, n in order("dve", g, pi is not None, ff):
                    if what == "P":
                        l1f_project_vector(dve, u + 1, n)
                    elif what == "N":
                        dve.wait_ge(p_proj, NP * (u + 1))
                        dve.wait_ge(p_y, u)
                        l1f_shift(dve, nb, L_SH, p_sh)
                        if new_layer:
                            dve.wait_ge(p_add, NJ * (u + 1))
                            l1f_tables(dve, nl)
                    elif what == "S":
                        for h in (2 * n, 2 * n + 1):
                            dve.wait_ge(p_s, 9 * u + h + 1)
                            dve.tensor_reduce(L_NM[:, :, h], score_tiles(h % 2), AX, ALU.max, negate=True).then_inc(p_max, 1)
                    elif what == "M":
                        dve.wait_ge(p_s, 9 * u + 9)
                        dve.tensor_scalar(L_NMB[0:8, 0:T], PS[0:8, 0, :], 1.0, None, ALU.mult).then_inc(p_max, 1)
                        dve.wait_ge(p_max, 10 * u + 9)
                        dve.tensor_tensor(L_NMB[32:40, 0:T], PS[0:8, 0, :], L_NMB[0:8, 0:T], ALU.subtract).then_inc(p_max, 1)
                    elif what == "D":
                        l1f_divide(dve, u, g, n)
                    elif what == "F":
                        l1f_ff_vector(dve, *ff, n)

            def feed(i, b, l):
                for n in range(8):
                    l1f_ff_vector(dve, i, b, l, n)
            through_units(dve, half_batch, feed)
            dve.wait_ge(p_y, 2 * DEPTH * B + 1)
            with dve.Fori(0, B) as b:
                dve.tensor_tensor(X[:, b, :], X[:, b, :], Y[:, b, 1:T + 1], ALU.add).then_inc(x_done, 1)

        def l1f_tables(dve, l):
            dve.wait_ge(w_qks, 16 * l + 16)
            for k in range(4):
                dve.tensor_tensor(L_TAB[:, k, :, :], ROPE[:, k, :, :], over(QKS[:, k, :], NT), ALU.mult).then_inc(p_tab, 1)
            dve.wait_ge(p_tab, 4 * l + 4)

        def l1f_shift(dve, b, dst, done):
            dve.tensor_scalar(dst[0:64, :], Y[0:64, b, 1:T + 1], 1.0, None, ALU.mult)
            dve.tensor_scalar(dst[64:P, :], Y[64:P, b, 0:T], 1.0, None, ALU.mult).then_inc(done, 1)

        def l1f_project_vector(dve, u, p):
            if p < NJ:
                t, q = p // 2, p % 2
                dve.wait_ge(p_raw, NJ * u + p + 1)
                if p >= 2 or not is_first(u):
                    dve.wait_ge(p_add, NJ * u + p - 1)
                raw = L_RAW[p % 2].rearrange("p (h u d) -> p h u d", h=8, u=2)
                t2 = L_T2[p % 2].rearrange("p (h u d) -> p h u d", h=8, u=2)
                sin = L_TAB[:, 2 * q + 1, t, :].rearrange("p (u d) -> p u d", u=2)
                for v in range(2):
                    ins = dve.tensor_tensor(t2[:, :, v, :], raw[:, :, 1 - v, :], over(sin[:, v, :], 8), ALU.mult)
                ins.then_inc(p_t12, 1)
                dve.wait_ge(p_sq, NJ * u + p + 1)
                if p == 0 and not is_first(u):
                    dve.wait_ge(p_sd, u)
                dve.tensor_reduce(L_SS[:, 8 * p:8 * p + 8], L_SQ[p % 2].rearrange("p (h d) -> p h d", h=8), AX, ALU.add).then_inc(p_ss, 1)
            if p == NJ + 1:
                dve.wait_ge(p_sd, u + 1)
                dve.tensor_scalar(L_SD, L_SD, 1e-12, None, ALU.max).then_inc(p_rn, 1)
                dve.wait_ge(p_rn, 2 * u + 1)
                dve.reciprocal(L_SD, L_SD).then_inc(p_rn, 1)
                dve.wait_ge(p_rn, 2 * u + 2)
            if NJ < p <= NJ + 4:
                for j in (2 * (p - NJ - 1), 2 * (p - NJ - 1) + 1):
                    dve.wait_ge(p_add, NJ * u + j + 1)
                    qk = L_QK[j].rearrange("p (h d) -> p h d", h=8)
                    dve.tensor_tensor(qk, qk, along(L_SD[:, 8 * j:8 * j + 8], DH), ALU.mult).then_inc(p_qk, 1)

        def l1f_divide(dve, u, g, k):
            dve.wait_ge(p_den, 8 * u + 2 * k + 2)
            dn, cx = L_DN[k % 2], L_CX[:, 4 * g + k, :]
            dve.reciprocal(dn, dn).then_inc(p_rd, 1)
            dve.wait_ge(p_rd, 4 * u + k + 1)
            dve.tensor_tensor(cx, cx, dn, ALU.mult).then_inc(p_cx, 1)

        def l1f_ff_vector(dve, i, b, l, s):
            if s == 0:
                dve.wait_ge(p_out, 2 * i + 1)
                dve.tensor_tensor(Y[:, b, 1:T + 1], Y[:, b, 1:T + 1], PS[:, 7, :], ALU.add).then_inc(p_y, 1)
                dve.wait_ge(p_y, 2 * i + 2)
                l1f_shift(dve, b, L_SF, p_sf)
            elif s == 1:
                dve.wait_ge(p_sf, i + 1)
                ln_vector_center(dve, i + 16, L_SF)
            elif s == 2:
                ln_vector_rs(dve, i + 16)
            elif s == 3:
                ln_vector_out(dve, i + 16, xn)
                dve.wait_ge(w_ff, 112 * l + 112)
                dve.wait_ge(ln_out, i + 18)
                dve.tensor_scalar(L_XG, xn, LNGB[:, 0:1], LNGB[:, 1:2], ALU.mult, ALU.add).then_inc(p_xg, 1)
            elif s < 7:
                m, (m0, mw) = s - 4, FF[s - 4]
                dve.wait_ge(p_gelu, 3 * i + m + 1)
                dve.scalar_tensor_tensor(out=L_H[m][0:mw, :], in0=PS[0:mw, 7, :], scalar=B1[0:mw, m, 0:1],
                                         in1=L_H[m][0:mw, :], op0=ALU.add, op1=ALU.mult).then_inc(p_h, 1)
            else:
                dve.wait_ge(p_out, 2 * i + 2)
                dve.scalar_tensor_tensor(out=Y[:, b, 1:T + 1], in0=PS[:, 6, :], scalar=B2[:, 0:1], in1=Y[:, b, 1:T + 1],
                                         op0=ALU.add, op1=ALU.add).then_inc(p_y, 1)

        def l1f_pool(pool):
            for p in range(NPT):
                l1f_project_pool(pool, 0, 0, 0, p)

            def half_batch(g, u, pi, nb, nl, ff, new_layer):
                if pi is not None:
                    for p in range(NPT):
                        l1f_project_pool(pool, u + 1, 1 - g, nl, p)
            through_units(pool, half_batch, lambda i, b, l: None)

        def l1f_project_pool(pool, u, g, l, p):
            if p < NJ:
                t, q = p // 2, p % 2
                if p == 0:
                    pool.wait_ge(p_tab, 4 * l + 4)
                pool.wait_ge(p_raw, NJ * u + p + 1)
                if not is_first(u):
                    pool.wait_ge(p_turn, NJ * u + p - 7)
                pool.tensor_tensor(L_QK[p].rearrange("p (h d) -> p h d", h=8), L_RAW[p % 2].rearrange("p (h d) -> p h d", h=8),
                                   over(L_TAB[:, 2 * q, t, :], 8), ALU.mult).then_inc(p_t1, 1)
                pool.wait_ge(p_t1, NJ * u + p + 1)
                pool.wait_ge(p_t12, NJ * u + p + 1)
                pool.tensor_tensor(L_QK[p], L_QK[p], L_T2[p % 2], ALU.add).then_inc(p_add, 1)
            j = p - 11
            if 0 <= j < NJ:
                src, dst = ((L_QT, L_QB), (L_KT, L_KB))[j % 2]
                t0 = (j // 2) * P + (WIN if j % 2 else 0)
                pool.wait_ge(p_tev, NJ * u + j + 1)
                if j == 0 and not is_first(u):
                    pool.wait_ge(p_s, 9 * u)
                if j == 0 and is_first(u):
                    pool.wait_ge(p_pre, 8)
                pool.tensor_tensor(dst[:, :, t0:t0 + P], src[:, 4 * g:4 * g + 4, t0:t0 + P],
                                   L_ONE4.to_broadcast([P, 4, P]), ALU.mult).then_inc(p_cast, 1)

        late_at = [0]

        def late(rows, cols):
            late_at[0] += cols
            assert late_at[0] <= 3 * NH * DH
            return WQKV[0:rows, late_at[0] - cols:late_at[0]]
        L2W = late(P, 4 * P).rearrange("p (i d) -> p i d", i=4)
        L2B = late(P, 2)
        L2BV = late(1, P)
        MASKF = late(P, NT * S2).rearrange("p (t k) -> p t k", t=NT)
        VCTX = late(S2, B * P).rearrange("p (b d) -> p b d", b=B)
        l2x_loaded = sem("l2x_loaded")
        c = carver()
        C_C = c(S2)
        C_Q = c(T)
        C_K = c(S2)
        C_V = c(P)
        C_S = c(NT * S2).rearrange("p (t k) -> p t k", t=NT)
        C_M = c(NT)
        C_SUM = c(NT)
        C_R = c(NT)
        C_PT = c(T)
        C_CX = c(T)
        C_MASK = c(NT * S2).rearrange("p (t k) -> p t k", t=NT)
        (c_ctx, c_proj, c_q, c_kv, c_score, c_max, c_sub, c_exp, c_vec, c_p, c_turn, c_pt, c_cx, c_cxs, c_out) = [sem("c_" + n) for n in (
            "ctx proj q kv score max sub exp vec p turn pt cx cxs out").split()]
        CS = PS[:, 0, :].rearrange("p (t z) -> p t z", t=NT)[:, :, 0:S2]

        def cross_tensor(pe, b, k, ln, project):
            pe.wait_ge(xn_set, k + 9 if project else k + 13)
            pe.wait_ge(c_ctx, k + 1)
            if project:
                pe.matmul(PS[:, 4, 0:S2], L2W[:, 1, :], C_C, start=True, stop=True)
                pe.matmul(PS[0:S2, 5, 0:P], C_C, L2W[:, 2, :], start=True, stop=False)
                pe.matmul(PS[0:S2, 5, 0:P], ONEROW[0:1, 0:S2], L2BV, start=False, stop=True).then_inc(c_proj, 1)
                pe.matmul(PS[:, 2, :], L2W[:, 0, :], xn, start=True, stop=True).then_inc(c_proj, 1)
                pe.wait_ge(c_q, k + 1)
                pe.wait_ge(c_kv, k + 1)
            q, keys = (C_Q, C_K) if project else (xn, C_C)
            for t in range(NT):
                mm = pe.matmul(CS[:, t, :], q[:, t * P:(t + 1) * P], keys, start=True, stop=True)
            mm.then_inc(c_score, 1)
            pe.wait_ge(c_p, k + 1)
            for t in range(NT):
                mm = pe.transpose(PS[0:S2, 3, t * P:(t + 1) * P], C_S[:, t, :], IDF[:, :])
            mm.then_inc(c_turn, 1)
            pe.wait_ge(c_pt, k + 1)
            pe.matmul(PS[:, 4, :], C_V[0:S2, :], C_PT[0:S2, :], start=True, stop=True).then_inc(c_cx, 1)
            if project:
                pe.wait_ge(c_cxs, k + 1)
                pe.matmul(PS[:, 5, :], L2W[:, 3, :], C_CX, start=True, stop=True).then_inc(c_out, 1)

        def cross_scalar(act, b, k, ln, project):
            act.wait_ge(c_sub, k + 1)
            act.activation(C_S, C_S, ACT.Exp).then_inc(c_exp, 1)
            act.wait_ge(c_turn, k + 1)
            act.activation(C_PT[0:S2, :], PS[0:S2, 3, :], ACT.Copy).then_inc(c_pt, 1)
            if project:
                act.wait_ge(c_cx, k + 1)
                act.activation(C_CX, PS[:, 4, :], ACT.Copy).then_inc(c_cxs, 1)

        def cross_vector(dve, b, k, ln, project):
            set_xn(dve, b)
            if project:
                dve.wait_ge(c_proj, 2 * k + 1)
                dve.tensor_copy(C_K, PS[:, 4, 0:S2])
                dve.tensor_copy(C_V[0:S2, :], PS[0:S2, 5, 0:P]).then_inc(c_kv, 1)
                dve.wait_ge(c_proj, 2 * k + 2)
                dve.tensor_scalar(C_Q, PS[:, 2, :], L2B[:, 0:1], P ** -0.5, ALU.add, ALU.mult).then_inc(c_q, 1)
            dve.wait_ge(c_score, k + 1)
            scores = CS
            if not project:
                for t in range(NT):
                    ins = dve.scalar_tensor_tensor(out=C_S[:, t, :], in0=CS[:, t, :], scalar=P ** 0.5, in1=C_MASK[:, t, :], op0=ALU.mult, op1=ALU.add)
                ins.then_inc(c_q, 1)
                dve.wait_ge(c_q, k + 1)
                scores = C_S
            dve.tensor_reduce(C_M, scores, AX, ALU.max, negate=True).then_inc(c_max, 1)
            dve.wait_ge(c_max, k + 1)
            dve.tensor_tensor(C_S, scores, along(C_M, S2), ALU.add).then_inc(c_sub, 1)
            dve.wait_ge(c_exp, k + 1)
            dve.tensor_reduce(C_SUM, C_S, AX, ALU.add).then_inc(c_vec, 1)
            dve.wait_ge(c_vec, 2 * k + 1)
            dve.reciprocal(C_R, C_SUM).then_inc(c_vec, 1)
            dve.wait_ge(c_vec, 2 * k + 2)
            dve.tensor_tensor(C_S, C_S, along(C_R, S2), ALU.mult).then_inc(c_p, 1)
            if project:
                dve.wait_ge(c_out, k + 1)
                dve.scalar_tensor_tensor(out=X[:, b, :], in0=PS[:, 5, :], scalar=L2B[:, 1:2], in1=X[:, b, :],
                                         op0=ALU.add, op1=ALU.add).then_inc(x_done, 1)
            else:
                dve.wait_ge(c_cx, k + 1)
                dve.tensor_tensor(X[:, b, :], X[:, b, :], PS[:, 4, :], ALU.add).then_inc(x_done, 1)

        def l2x_tensor(pe):
            pe.wait_ge(l2x_loaded, 16 * 5)
            ln4_tensor(pe, 40)
            with pe.Fori(0, B) as b:
                cross_tensor(pe, b, b, 40, True)

        def l2x_scalar(act):
            ln4_scalar(act, 40)
            with act.Fori(0, B) as b:
                cross_scalar(act, b, b, 40, True)

        def l2x_vector(dve):
            dve.wait_ge(l2x_loaded, 16 * 5)
            ln4_vector(dve, 40)
            dve.wait_ge(ln_out, 41 + B)
            with dve.Fori(0, B) as b:
                cross_vector(dve, b, b, 40, True)

        def l2x_pool(pool):
            with pool.Fori(0, B) as b:
                pool.wait_ge(x_done, b + 16)
                pool.tensor_copy(C_C, CT[:, b, :]).then_inc(c_ctx, 1)

        DF, NC = 512, 4
        M_W1 = MOEW[:, 0:4096].rearrange("p (e c m) -> p e c m", e=NE, c=NC)
        M_W2 = MOEW[:, 4096:8192].rearrange("p (e c m) -> p e c m", e=NE, c=NC)
        M_B1 = sb("M_B1", [P, 2, NE, NC])
        M_B2 = sb("M_B2", [NE, 2, P])
        M_GW = sb("M_GW", [P, 2, NE])
        M_GB = sb("M_GB", [1, 2, NE])
        RANK = sb("RANK", [P, NE])
        moe_loaded, moe_w = sem("moe_loaded"), sem("moe_w")

        def carve_moe(c):
            d = {}
            for n in "E S1 S2 T1 T2".split():
                d[n] = c(NT * NE).rearrange("p (t e) -> p t e", t=NT)
            for n in "M SUM R M1 M2 MX".split():
                d[n] = c(NT)
            d["GT"], d["R0"] = c(T), c(T)
            d["GB"], d["MID"] = c(T, BF16), c(T, BF16)
            d["SEL"] = c(NE, BF16)
            d["SG"], d["H"] = [c(T), c(T)], [c(T), c(T)]
            return d
        (m_logit, m_max, m_sub, m_exp, m_vec, m_w, m_turn, m_gt, m_bc, m_z, m_act, m_h, m_down) = [sem("m_" + n) for n in (
            "logit max sub exp vec w turn gt bc z act h down").split()]
        NM = NE * NC

        def moe_parts(dve, d, vec0):
            dve.tensor_tensor(d["SEL"], IDB[:, 0:NE], IDB[:, 32:32 + NE], ALU.add).then_inc(m_vec, 1)
            dve.wait_ge(m_vec, vec0 + 1)
            dve.tensor_tensor(d["SEL"], d["SEL"], IDB[:, 64:64 + NE], ALU.add)
            dve.memset(d["GB"], 0.0).then_inc(m_vec, 1)
            dve.wait_ge(m_vec, vec0 + 2)

        def moe_tensor(pe, k, s, d, src):
            for t in range(NT):
                o = PS[:, 0, t * NE:(t + 1) * NE]
                pe.matmul(o, src[:, t * P:(t + 1) * P], M_GW[:, s, :], start=True, stop=False)
                mm = pe.matmul(o, ONEROW[:, :], M_GB[:, s, :], start=False, stop=True)
            mm.then_inc(m_logit, 1)
            pe.wait_ge(m_w, k + 1)
            for t in range(NT):
                mm = pe.transpose(PS[0:NE, 4, t * P:(t + 1) * P], d["E"][:, t, :], IDF[:, :])
            mm.then_inc(m_turn, 1)
            pe.wait_ge(m_gt, 6 * k + 1)
            pe.matmul(PS[:, 1, :], M_B2[:, s, :], d["GT"][0:NE, :], start=True, stop=False)
            for i in range(NM):
                e, c = i // NC, i % NC
                if i >= 2:
                    pe.wait_ge(m_act, k * NM + i - 1)
                pe.matmul(PS[:, 2 + i % 2, :], M_W1[:, e, c, :], src, start=True, stop=True).then_inc(m_z, 1)
                if i == 0:
                    continue
                if i == 1 or c == 0:
                    if i == 1:
                        pe.wait_ge(m_gt, 6 * k + 6)
                    if e >= 2:
                        pe.wait_ge(m_h, k * NM + NC * (e - 1))
                    pe.matmul(PS[:, 5 * (e % 2), :], d["SEL"][:, e:e + 1].to_broadcast([P, P]), d["GB"],
                              start=True, stop=True).then_inc(m_bc, 1)
                moe_down(pe, k, d, i - 1)
            moe_down(pe, k, d, NM - 1)

        def moe_down(pe, k, d, i):
            pe.wait_ge(m_h, k * NM + i + 1)
            pe.matmul(PS[:, 1, :], M_W2[:, i // NC, i % NC, :], d["H"][i % 2], start=False, stop=i == NM - 1).then_inc(m_down, 1)

        def moe_scalar(act, k, s, d, func):
            act.wait_ge(m_sub, k + 1)
            act.activation(d["E"], d["E"], ACT.Exp).then_inc(m_exp, 1)
            for i in range(NM):
                e, c = i // NC, i % NC
                act.wait_ge(m_z, k * NM + i + 1)
                if i >= 2:
                    act.wait_ge(m_h, k * NM + i - 1)
                act.activation(d["SG"][i % 2], PS[:, 2 + i % 2, :], func, bias=M_B1[:, s, e, c:c + 1]).then_inc(m_act, 1)

        def moe_vector(dve, k, s, d, vec0, top2):
            n = [0]

            def step(ins):
                n[0] += 1
                ins.then_inc(m_vec, 1)
                dve.wait_ge(m_vec, vec0 + n[0])
            E, S1, S2_, T1, T2 = d["E"], d["S1"], d["S2"], d["T1"], d["T2"]
            dve.wait_ge(m_logit, k + 1)
            lg = PS[:, 0, 0:NT * NE].rearrange("p (t e) -> p t e", t=NT)
            dve.tensor_reduce(d["M"], lg, AX, ALU.max, negate=True).then_inc(m_max, 1)
            dve.wait_ge(m_max, k + 1)
            dve.tensor_tensor(E, lg, along(d["M"], NE), ALU.add).then_inc(m_sub, 1)
            dve.wait_ge(m_exp, k + 1)
            step(dve.tensor_reduce(d["SUM"], E, AX, ALU.add))
            step(dve.reciprocal(d["R"], d["SUM"]))
            ins = dve.tensor_tensor(E, E, along(d["R"], NE), ALU.mult)
            if top2:
                step(ins)
                rank = over(RANK[:, :], NT)
                for sel, m, src in ((S1, d["M1"], E), (S2_, d["M2"], T2)):
                    step(dve.tensor_reduce(m, src, AX, ALU.max))
                    step(dve.tensor_tensor(T1, src, along(m, NE), ALU.is_equal))
                    step(dve.tensor_tensor(T1, T1, rank, ALU.mult))
                    step(dve.tensor_reduce(d["MX"], T1, AX, ALU.max))
                    step(dve.tensor_tensor(sel, T1, along(d["MX"], NE), ALU.is_equal))
                    if sel is S1:
                        step(dve.tensor_scalar(T2, S1, -2.0, None, ALU.mult))
                        step(dve.tensor_tensor(T2, T2, E, ALU.add))
                step(dve.tensor_tensor(d["SUM"], d["M1"], d["M2"], ALU.add))
                step(dve.reciprocal(d["R"], d["SUM"]))
                step(dve.tensor_tensor(S1, S1, S2_, ALU.add))
                step(dve.tensor_tensor(S1, S1, E, ALU.mult))
                ins = dve.tensor_tensor(E, S1, along(d["R"], NE), ALU.mult)
            ins.then_inc(m_w, 1)
            assert n[0] == (19 if top2 else 2), n[0]
            dve.wait_ge(m_turn, k + 1)
            gt, r0, gb, mid = d["GT"][0:NE, :], d["R0"][0:NE, :], d["GB"], d["MID"][0:NE, :]
            dve.tensor_copy(gt, PS[0:NE, 4, :]).then_inc(m_gt, 1)
            dve.tensor_copy(gb[0:NE, :], PS[0:NE, 4, :]).then_inc(m_gt, 1)
            dve.wait_ge(m_gt, 6 * k + 2)
            dve.tensor_tensor(r0, gt, gb[0:NE, :], ALU.subtract).then_inc(m_gt, 1)
            dve.wait_ge(m_gt, 6 * k + 3)
            dve.tensor_scalar(mid, r0, 1.0, None, ALU.mult).then_inc(m_gt, 1)
            dve.wait_ge(m_gt, 6 * k + 4)
            dve.tensor_tensor(gb[64:64 + NE, :], r0, mid, ALU.subtract).then_inc(m_gt, 1)
            dve.tensor_scalar(gb[32:32 + NE, :], mid, 1.0, None, ALU.mult).then_inc(m_gt, 1)
            for i in range(NM):
                dve.wait_ge(m_act, k * NM + i + 1)
                if i % NC == 0:
                    dve.wait_ge(m_bc, k * NE + i // NC + 1)
                if i >= 2:
                    dve.wait_ge(m_down, k * NM + i - 1)
                dve.tensor_tensor(d["H"][i % 2], d["SG"][i % 2], PS[:, 5 * (i // NC % 2), :], ALU.mult).then_inc(m_h, 1)
            dve.wait_ge(m_down, k * NM + NM)

        c = carver()
        G2 = carve_moe(c)

        def l2f_tensor(pe):
            pe.wait_ge(moe_loaded, 16 * 9)
            pe.wait_ge(moe_w, 16 * 2)
            ln4_tensor(pe, 44)
            with pe.Fori(0, B) as b:
                pe.wait_ge(xn_set, b + 13)
                moe_tensor(pe, b, 0, G2, xn)

        def l2f_scalar(act):
            act.wait_ge(moe_loaded, 16 * 9)
            ln4_scalar(act, 44)
            with act.Fori(0, B) as b:
                moe_scalar(act, b, 0, G2, ACT.Gelu)

        def l2f_vector(dve):
            dve.wait_ge(moe_loaded, 16 * 9)
            moe_parts(dve, G2, 0)
            ln4_vector(dve, 44)
            dve.wait_ge(ln_out, 45 + B)
            with dve.Fori(0, B) as b:
                set_xn(dve, b)
                moe_vector(dve, b, 0, G2, 19 * b + 2, True)
                dve.tensor_tensor(X[:, b, :], X[:, b, :], PS[:, 1, :], ALU.add).then_inc(x_done, 1)

        def l3x_tensor(pe):
            ln4_tensor(pe, 48)
            with pe.Fori(0, B) as b:
                cross_tensor(pe, b, b + 4, 48, False)

        def l3x_scalar(act):
            ln4_scalar(act, 48)
            with act.Fori(0, B) as b:
                cross_scalar(act, b, b + 4, 48, False)

        def l3x_vector(dve):
            dve.tensor_scalar(C_MASK, MASKF[:, :, :], -1.0e9, None, ALU.mult).then_inc(c_kv, 1)
            dve.wait_ge(c_kv, 5)
            ln4_vector(dve, 48)
            dve.wait_ge(ln_out, 49 + B)
            with dve.Fori(0, B) as b:
                cross_vector(dve, b, b + 4, 48, False)

        def l3x_pool(pool):
            with pool.Fori(0, B) as b:
                pool.wait_ge(x_done, b + 24)
                pool.tensor_copy(C_V[0:S2, :], VCTX[:, b, :])
                pool.tensor_copy(C_C, CT[:, b, :]).then_inc(c_ctx, 1)

        CONVW = late(P, 3 * P).rearrange("p (k d) -> p k d", k=3)
        WQKV3 = late(P, 3 * P).rearrange("p (i d) -> p i d", i=3)
        WO3 = late(P, P)
        B3 = late(P, 8)
        BV3 = late(1, P)
        l3_loaded = sem("l3_loaded")
        c = carver()
        H_KM = c(4 * T).rearrange("p (m n) -> p m n", m=4)
        H_QB = c(T, BF16)
        H_KB = c(4 * T, BF16).rearrange("p (m n) -> p m n", m=4)
        H_M4 = c(4)
        VROW3 = H0 * VSTEP
        H_VB = c(NT * VROW3).rearrange("p (t z) -> p t z", t=NT)
        H_P = [c(2 * T).rearrange("p (u n) -> p u n", u=2) for _ in range(2)]
        H_C1, H_Q, H_K, H_CX = c(T), c(T), c(T), c(T)
        H_N1, H_XR = c(T), c(T)
        H_RC = H_K
        H_NM = c(NT * H0).rearrange("p (t h) -> p t h", t=NT)
        H_NMB = [c(T, BF16), c(T, BF16)]
        G3 = carve_moe(c)
        (h_conv, h_c1, h_proj, h_ev, h_km, h_s, h_max, h_mturn, h_nmt, h_st, h_exp, h_pv, h_rc, h_cx, h_wo, h_r, h_n1, h_ev2, h_cb) = [
            sem("h_" + n) for n in "conv c1 proj ev km s max mturn nmt st exp pv rc cx wo r n1 ev2 cb".split()]
        NPR = H0 * NT // 2
        HP = NPR // 2

        def l3f_tensor(pe):
            nc.disable_value_cache = True
            pe.wait_ge(l3_loaded, 16 * 5)
            pe.wait_ge(moe_w, 16 * 4)
            pe.wait_ge(h_ev2, 1)
            ln4_tensor(pe, 52)
            with pe.Fori(0, B) as b:
                k0 = 2 * b + 56
                pe.wait_ge(xn_set, b + 21)
                for k in range(3):
                    mm = pe.matmul(PS[:, 0, :], CONVW[:, k, :], XN[:, k:k + T], start=k == 0, stop=k == 2)
                mm.then_inc(h_conv, 1)
                pe.wait_ge(h_c1, b + 1)
                for j in range(2):
                    pe.matmul(PS[:, 1 + j, :], WQKV3[:, j, :], H_C1, start=True, stop=True)
                for t in range(NT):
                    o = PS[:, 7, t * P:(t + 1) * P]
                    pe.matmul(o, H_C1[:, t * P:(t + 1) * P], WQKV3[:, 2, :], start=True, stop=False)
                    mm = pe.matmul(o, ONEROW[:, :], BV3, start=False, stop=True)
                mm.then_inc(h_proj, 1)
                pe.wait_ge(h_ev, b + 1)
                for k in range(HP):
                    if k % (2 * NT) == 0:
                        pe.wait_ge(h_cb, 7 * b + 2 + k // (2 * NT))
                    if k >= 2:
                        pe.wait_ge(h_max, b * NPR + k - 1)
                    l3f_score(pe, k, 2 * (k % 2))
                l3f_turn(pe, b, 0)
                for k in range(NPR):
                    if k >= 2:
                        pe.wait_ge(h_exp, b * NPR + k - 1)
                    m, t, s0 = k // (2 * NT), k // 2 % NT, 2 * (k % 2)
                    for s in (s0, s0 + 1):
                        r = slice(32 * s, 32 * s + 32)
                        pe.matmul(PS[:, s, :], H_KM[r, m, t * P:(t + 1) * P], H_Q[r, :], start=True, stop=False)
                    for s in (s0, s0 + 1):
                        col = (4 * m + s) % 8
                        mm = pe.matmul(PS[:, s, :], NMSEL[:, col:col + 1].to_broadcast([P, P]), H_NMB[k // HP],
                                       start=False, stop=True)
                    mm.then_inc(h_st, 1)
                    if k < HP:
                        if k == 0:
                            pe.wait_ge(h_cb, 7 * b + 5)
                        else:
                            pe.wait_ge(h_max, b * NPR + HP + k)
                        l3f_score(pe, HP + k, 6)
                    if k >= 1:
                        l3f_pv(pe, b, k - 1)
                    if k == HP - 1:
                        l3f_turn(pe, b, 1)
                l3f_pv(pe, b, NPR - 1)
                pe.wait_ge(h_cx, 2 * b + 2)
                pe.matmul(PS[:, 0, :], WO3, H_CX, start=True, stop=True).then_inc(h_wo, 1)
                pe.wait_ge(h_r, 2 * b + 1)
                ln_tensor(pe, k0, H_XR)
                pe.wait_ge(h_n1, b + 1)
                moe_tensor(pe, b + 4, 1, G3, H_N1)
                pe.wait_ge(h_r, 2 * b + 2)
                ln_tensor(pe, k0 + 1, H_XR)
            nc.disable_value_cache = False

        def l3f_score(pe, k, bank):
            m, t, s0 = k // (2 * NT), k // 2 % NT, 2 * (k % 2)
            for v in range(2):
                r = slice(32 * (s0 + v), 32 * (s0 + v) + 32)
                mm = pe.matmul(PS[:, bank + v, :], H_QB[r, t * P:(t + 1) * P], H_KB[r, m, :], start=True, stop=True)
            mm.then_inc(h_s, 1)

        def l3f_turn(pe, b, g):
            pe.wait_ge(h_max, b * NPR + (g + 1) * HP)
            for t in range(NT):
                mm = pe.transpose(PS[0:8, 6, t * P:(t + 1) * P], H_NM[:, t, 8 * g:8 * g + 8], IDF[:, :])
            mm.then_inc(h_mturn, 1)
            pe.wait_ge(h_nmt, 4 * b + 2 * g + 2)

        def l3f_pv(pe, b, k):
            pe.wait_ge(h_exp, b * NPR + k + 1)
            m, t, s0 = k // (2 * NT), k // 2 % NT, 2 * (k % 2)
            for v in range(2):
                h = 4 * (s0 + v) + m
                mm = pe.matmul(PS[:, 4 + h // 8, :], H_VB[:, t, h * P:(h + 1) * P], H_P[k % 2][:, v, :],
                               start=k < 2 and v == 0, stop=k >= NPR - 2 and v == 1)
            mm.then_inc(h_pv, 1)

        def l3f_scalar(act):
            nc.disable_value_cache = True
            ln4_scalar(act, 52)
            with act.Fori(0, B) as b:
                k0 = 2 * b + 56
                act.wait_ge(h_ev, b + 1)
                act.activation(H_QB, H_Q, ACT.Copy).then_inc(h_cb, 1)
                for m in range(4):
                    act.wait_ge(h_km, 4 * b + m + 1)
                    act.activation(H_KB[:, m, :], H_KM[:, m, :], ACT.Copy).then_inc(h_cb, 1)
                for k in range(NPR):
                    act.wait_ge(h_st, b * NPR + k + 1)
                    if k >= 2:
                        act.wait_ge(h_pv, b * NPR + k - 1)
                    act.activation(H_P[k % 2], PS[:, 2 * (k % 2):2 * (k % 2) + 2, :], ACT.Exp).then_inc(h_exp, 1)
                act.wait_ge(h_pv, b * NPR + NPR)
                for g in range(2):
                    act.activation(H_RC[64 * g:64 * g + 64, :], PS[64:P, 4 + g, :], ACT.Copy).then_inc(h_cb, 1)
                ln_scalar(act, k0)
                moe_scalar(act, b + 4, 1, G3, ACT.Relu)
                ln_scalar(act, k0 + 1)
            nc.disable_value_cache = False

        def l3f_vector(dve):
            nc.disable_value_cache = True
            dve.wait_ge(l3_loaded, 16 * 5)
            dve.memset(H_VB, 0.0).then_inc(h_rc, 1)
            dve.wait_ge(h_rc, 1)
            for h in range(H0):
                at = h * P + 64 + DK0 * (h % 8)
                dve.memset(H_VB[:, :, at:at + DK0], 1.0)
            dve.memset(H_NMB[0], 0.0)
            dve.memset(H_NMB[1], 0.0)
            dve.tensor_reduce(H_M4, HMASK[:, :].rearrange("p (s m) -> p m s", m=4), AX, ALU.add).then_inc(h_ev2, 1)
            dve.wait_ge(h_ev2, 1)
            moe_parts(dve, G3, 78)
            ln4_vector(dve, 52)
            dve.wait_ge(ln_out, 53 + B)
            with dve.Fori(0, B) as b:
                k0 = 2 * b + 56
                set_xn(dve, b)
                dve.wait_ge(h_conv, b + 1)
                dve.tensor_scalar(H_C1, PS[:, 0, :], B3[:, 0:1], None, ALU.add).then_inc(h_c1, 1)
                dve.wait_ge(h_proj, b + 1)
                dve.tensor_scalar(H_K, PS[:, 2, :], B3[:, 2:3], None, ALU.add).then_inc(h_rc, 1)
                dve.tensor_scalar(H_Q, PS[:, 1, :], B3[:, 1:2], DK0 ** -0.5, ALU.add, ALU.mult).then_inc(h_ev, 1)
                dve.wait_ge(h_rc, 2 * b + 2)
                for m in range(4):
                    dve.tensor_scalar(H_KM[:, m, :], H_K, H_M4[:, m:m + 1], None, ALU.mult).then_inc(h_km, 1)
                for t in range(NT):
                    for g in range(2):
                        vg = H_VB[:, t, g * 8 * P:g * 8 * P + 8 * VSTEP].rearrange("p (h e) -> p h e", e=VSTEP)[:, :, 0:DK0]
                        dve.tensor_copy(vg, PS[:, 7, t * P + g * 64:t * P + (g + 1) * 64].rearrange("p (h e) -> p h e", e=DK0))
                for k in range(NPR):
                    m, t, s0 = k // (2 * NT), k // 2 % NT, 2 * (k % 2)
                    bank = s0 if k < HP else 6
                    dve.wait_ge(h_s, b * NPR + k + 1)
                    dve.tensor_reduce(H_NM[:, t, 4 * m + s0:4 * m + s0 + 2], PS[:, bank:bank + 2, :], AX, ALU.max, negate=True).then_inc(h_max, 1)
                    if k % HP == HP - 1:
                        g = k // HP
                        dve.wait_ge(h_mturn, 2 * b + g + 1)
                        dve.tensor_scalar(H_NMB[g][0:8, :], PS[0:8, 6, :], 1.0, None, ALU.mult).then_inc(h_nmt, 1)
                        dve.wait_ge(h_nmt, 4 * b + 2 * g + 1)
                        dve.tensor_tensor(H_NMB[g][32:40, :], PS[0:8, 6, :], H_NMB[g][0:8, :], ALU.subtract).then_inc(h_nmt, 1)
                dve.wait_ge(h_km, 4 * b + 4)
                dve.wait_ge(h_cb, 7 * b + 7)
                dve.reciprocal(H_RC, H_RC).then_inc(h_rc, 1)
                dve.wait_ge(h_rc, 2 * b + 3)
                for g in range(2):
                    dve.tensor_tensor(H_CX[64 * g:64 * g + 64, :], PS[0:64, 4 + g, :], H_RC[64 * g:64 * g + 64, :], ALU.mult).then_inc(h_cx, 1)
                dve.wait_ge(h_wo, b + 1)
                dve.scalar_tensor_tensor(out=H_XR, in0=PS[:, 0, :], scalar=B3[:, 3:4], in1=H_C1,
                                         op0=ALU.add, op1=ALU.add).then_inc(h_r, 1)
                dve.wait_ge(h_r, 2 * b + 1)
                ln_vector(dve, k0, H_XR, H_N1)
                dve.wait_ge(ln_out, k0 + 2)
                dve.tensor_scalar(H_N1, H_N1, B3[:, 4:5], B3[:, 5:6], ALU.mult, ALU.add).then_inc(h_n1, 1)
                dve.wait_ge(h_n1, b + 1)
                moe_vector(dve, b + 4, 1, G3, 2 * b + 80, False)
                dve.tensor_tensor(H_XR, H_N1, PS[:, 1, :], ALU.add).then_inc(h_r, 1)
                dve.wait_ge(h_r, 2 * b + 2)
                ln_vector(dve, k0 + 1, H_XR, H_CX)
                dve.wait_ge(ln_out, k0 + 3)
                dve.tensor_scalar(H_Q, H_CX, B3[:, 6:7], B3[:, 7:8], ALU.mult, ALU.add).then_inc(h_ev2, 1)
                dve.wait_ge(h_ev2, b + 2)
                dve.tensor_tensor(X[:, b, :], X[:, b, :], H_Q, ALU.add).then_inc(x_done, 1)
                dve.wait_ge(x_done, b + 29)
            nc.disable_value_cache = False

        block = ctx.enter_context(nc.Block())

        @block.sync
        def _(sp):
            sp.dma_start(X[:, :, :], a["xT"]).then_inc(x_loaded, 16)
            for dst, name in ((CT[:, :, :], "ctxT"), (AVG[:, :], "c_avg"), (IDF[:, :], "c_ident"),
                              (HMASK[:, :], "c_hmask"), (EPSC[:, :], "c_eps")):
                sp.dma_start(dst, a[name]).then_inc(const_loaded, 16)
            for dst, name in ((L0W[:, :, :], "L0_W"), (L0B[:, :], "L0_b"), (BVROW[:, :], "L0_bv"), (ONEROW[:, :], "c_onerow"),
                              (MSK_Q[:, :, :], "mask_q"), (MSK_T[:, :], "mask_t"), (PAD_Q[:, :, :], "pad_q"),
                              (PAD_T[:, :], "pad_t")):
                src = a[name]
                if name == "pad_q":
                    src = bass.AP(tensor=src.tensor, offset=0, ap=[[0, P], [S2, B], [1, S2]])
                sp.dma_start(dst, src).then_inc(l0_loaded, 16)
            for dst, name in ((GW0[:, :], "L0F_gate"), (E_G, "L0F_g"), (E_U, "L0F_u"), (E_D, "L0F_d")):
                sp.dma_start(dst, a[name]).then_inc(l0f_loaded, 16)
            sp.wait_ge(f_gate, 1)
            for b in range(B):
                sp.dma_start(F_GB[0:NE, b, :], F_G[b * NE:(b + 1) * NE, :]).then_inc(f_gb, 16)
            for dst, name, part in ((L1W[:, :, :], "L1X_W", 0), (L1CW[:, :], "L1X_cw", 2), (L1G[:, :], "L1X_gain", 1),
                                    (PTR_I[:, :], "ptr", 0), (IDS_I[:, :, :], "ids", -1), (IOTA[:, :], "c_iota", S2)):
                src = a[name]
                if part > 0:
                    src = bass.AP(tensor=src.tensor, offset=0, ap=[[0, P], [1, part]])
                elif part < 0:
                    src = bass.AP(tensor=src.tensor, offset=0, ap=[[0, P], [T, B], [1, S2]])
                sp.dma_start(dst, src).then_inc(l1x_loaded, 16)
            sp.dma_start(ROPE[:, :, :, :], a["c_rope"]).then_inc(l1_const, 16)
            sp.dma_start(BANDS32[:, :, :], a["c_bands"]).then_inc(l1_const, 16)

            def load_qkv(l, g):
                sp.dma_start(W_QKV[:, g, :, :], a["L1F_qkv"][l, :, g, :, :]).then_inc(w_qkv[g], 16)

            def load_qks(l):
                sp.dma_start(QKS[:, :, :], bass.AP(tensor=a["L1F_qks"].tensor, offset=l * 4 * DH, ap=[[0, P], [DH, 4], [1, DH]])).then_inc(w_qks, 16)

            def load_wo(l):
                sp.dma_start(WO[:, :, :], a["L1F_wo"][l, :, :, :]).then_inc(w_o, 16)

            def load_ff(l):
                sp.dma_start(W1[:, :], a["L1F_w1"][l, :, :]).then_inc(w_ff, 16)
                sp.dma_start(W2[:, 0:2, :], a["L1F_w2a"][l, :, :, :]).then_inc(w_ff, 16)
                sp.dma_start(W2[0:DI - 256, 2, :], a["L1F_w2b"][l, :, :]).then_inc(w_ff, 16)
                sp.dma_start(LNGB[:, :], a["L1F_lngb"][l, :, :]).then_inc(w_ff, 16)
                sp.dma_start(B1[:, 0:2, :], a["L1F_b1a"][l, :, :, :]).then_inc(w_ff, 16)
                sp.dma_start(B1[0:DI - 256, 2, :], a["L1F_b1b"][l, :, :]).then_inc(w_ff, 16)
                sp.dma_start(B2[:, :], a["L1F_b2"][l, :, :]).then_inc(w_ff, 16)

            load_qks(0)
            load_qkv(0, 0)
            load_qkv(0, 1)
            load_wo(0)
            load_ff(0)
            with sp.Fori(1, DEPTH) as l:
                sp.wait_ge(p_tab, 4 * l)
                load_qks(l)
                sp.wait_ge(p_proj, NP * (2 * B * l - 1))
                load_qkv(l, 0)
                sp.wait_ge(p_proj, NP * 2 * B * l)
                load_qkv(l, 1)
                sp.wait_ge(p_out, 2 * l * B)
                load_wo(l)
                sp.wait_ge(p_y, 2 * B * l + 1)
                load_ff(l)
            sp.wait_ge(p_proj, DEPTH * B * 2 * NP)
            for dst, name in ((L2W, "L2X_W"), (L2B, "L2X_b"), (L2BV, "L2X_bv"), (MASKF, "maskf"), (VCTX, "vctx")):
                sp.dma_start(dst, a[name]).then_inc(l2x_loaded, 16)
            for dst, name in ((M_B1[:, 0, :, :], "L2F_b1"), (M_B1[:, 1, :, :], "L3F_b1"), (M_B2[:, 0, :], "L2F_b2"), (M_B2[:, 1, :], "L3F_b2"),
                              (M_GW[:, 0, :], "L2F_gw"), (M_GW[:, 1, :], "L3F_gw"), (M_GB[:, 0, :], "L2F_gb"), (M_GB[:, 1, :], "L3F_gb"),
                              (RANK[:, :], "c_rank")):
                sp.dma_start(dst, a[name]).then_inc(moe_loaded, 16)
            sp.wait_ge(x_done, 16)
            sp.dma_start(M_W1, a["L2F_w1"]).then_inc(moe_w, 16)
            sp.dma_start(M_W2, a["L2F_w2"]).then_inc(moe_w, 16)
            for dst, name in ((CONVW, "L3F_conv"), (WQKV3, "L3F_wqkv"), (WO3, "L3F_wo"), (B3, "L3F_b"), (BV3, "L3F_bv")):
                sp.dma_start(dst, a[name]).then_inc(l3_loaded, 16)
            sp.wait_ge(x_done, 24)
            sp.dma_start(M_W1, a["L3F_w1"]).then_inc(moe_w, 16)
            sp.dma_start(M_W2, a["L3F_w2"]).then_inc(moe_w, 16)
            sp.wait_ge(x_done, 4 * 8)
            sp.dma_start(out, X[:, :, :]).then_inc(out_stored, 16)
            sp.wait_ge(out_stored, 16)

        @block.gpsimd
        def _(pool):
            pool.wait_ge(const_loaded, 16 * 5)
            pool.memset(XN[:, :], 0.0).then_inc(pool_const, 1)
            pool.tensor_copy(IDB[:, :], IDF[:, :]).then_inc(pool_const, 1)
            l0x_pool(pool)
            pool.wait_ge(x_done, 4 * 2)
            l1x_pool(pool)
            pool.wait_ge(x_done, 4 * 3)
            l1f_pool(pool)
            pool.wait_ge(x_done, 4 * 4)
            l2x_pool(pool)
            pool.wait_ge(x_done, 4 * 6)
            l3x_pool(pool)
        @block.scalar
        def _(act):
            act.wait_ge(const_loaded, 16 * 5)
            l0x_scalar(act)
            act.wait_ge(x_done, 4 * 1)
            l0f_scalar(act)
            act.wait_ge(x_done, 4 * 2)
            l1x_scalar(act)
            act.wait_ge(x_done, 4 * 3)
            l1f_scalar(act)
            act.wait_ge(x_done, 4 * 4)
            l2x_scalar(act)
            act.wait_ge(x_done, 4 * 5)
            l2f_scalar(act)
            act.wait_ge(x_done, 4 * 6)
            l3x_scalar(act)
            act.wait_ge(x_done, 4 * 7)
            l3f_scalar(act)
        @block.tensor
        def _(pe):
            pe.wait_ge(const_loaded, 16 * 5)
            pe.wait_ge(x_loaded, 16)
            pe.wait_ge(pool_const, 2)
            l0x_tensor(pe)
            pe.wait_ge(x_done, 4 * 1)
            l0f_tensor(pe)
            pe.wait_ge(x_done, 4 * 2)
            l1x_tensor(pe)
            pe.wait_ge(x_done, 4 * 3)
            l1f_tensor(pe)
            pe.wait_ge(x_done, 4 * 4)
            l2x_tensor(pe)
            pe.wait_ge(x_done, 4 * 5)
            l2f_tensor(pe)
            pe.wait_ge(x_done, 4 * 6)
            l3x_tensor(pe)
            pe.wait_ge(x_done, 4 * 7)
            l3f_tensor(pe)
        @block.vector
        def _(dve):
            dve.wait_ge(const_loaded, 16 * 5)
            dve.wait_ge(x_loaded, 16)
            dve.wait_ge(pool_const, 2)
            dve.memset(LN_C[:, :], 0.0).then_inc(ln_out, 1)
            dve.wait_ge(ln_out, 1)
            l0x_vector(dve)
            dve.wait_ge(x_done, 4 * 1)
            l0f_vector(dve)
            dve.wait_ge(x_done, 4 * 2)
            l1x_vector(dve)
            dve.wait_ge(x_done, 4 * 3)
            l1f_vector(dve)
            dve.wait_ge(x_done, 4 * 4)
            l2x_vector(dve)
            dve.wait_ge(x_done, 4 * 5)
            l2f_vector(dve)
            dve.wait_ge(x_done, 4 * 6)
            l3x_vector(dve)
            dve.wait_ge(x_done, 4 * 7)
            l3f_vector(dve)


def kernel(**inputs):
    import numpy as np
    import concourse.bacc as bacc
    from concourse.bass_utils import run_bass_kernel_spmd

    v = {k: np.asarray(w) for k, w in inputs.items()}
    f = np.float32
    eye = np.eye(P, dtype=f)
    half = np.arange(0, 64, 2, dtype=f)
    pos = np.arange(T, dtype=f)
    freqs = pos[:, None] * (f(1.0) / f(10000.0) ** (half / f(64)))[None, :]
    base = (half + f(0.4 * 64)) / f(1.4 * 64)
    decay = base[None, :] ** ((pos - T // 2) / f(16))[:, None]
    cos, sin = np.cos(freqs), np.sin(freqs)
    qk = []
    for s, by in ((decay, f(8.0)), (f(1.0) / decay, f(1.0))):
        qk += [np.concatenate([cos * s, cos * s], 1) * by, np.concatenate([-sin * s, sin * s], 1) * by]
    rope = np.stack([x.reshape(NT, P, 64).transpose(1, 0, 2) for x in qk], 1).astype(f)
    r, s = np.arange(P)[:, None], np.arange(P + 32)[None, :]
    q_sees = (r + 32 - s >= 0) & (r + 32 - s <= 32)
    k_seen = (s - r >= 0) & (s - r <= 32)
    bands = np.stack([np.where(m, 0.0, NEG) for m in (q_sees & (s >= 32), q_sees, k_seen)], 1).astype(f)
    arrays = {
        "c_avg": np.full((P, P), 1 / P, f), "c_ident": eye, 
        "c_hmask": np.repeat(np.eye(H0, dtype=f), DK0, axis=0), "c_eps": np.full((P, 1), EPS, f),
        "c_onerow": np.ones((1, P), f),
        "xT": v["x"].transpose(2, 0, 1), "ctxT": v["ctx_1024"].transpose(2, 0, 1),
        "mask_q": v["mask_SxS2_bk1"].reshape(NT, P, S2).transpose(1, 0, 2),
        "mask_t": v["mask_SxS2_bk1"].T,
        "pad_q": v["mask_BxS2_bf0"], "pad_t": v["mask_BxS2_bf0"].T,
        "L0_W": np.stack([v["L0_xattn_" + n].T for n in ("Wq", "Wk", "Wv", "Wo")], 1),
        "L0_b": np.stack([v["L0_xattn_" + n] for n in ("bq", "bk", "bo")], 1),
        "L0_bv": v["L0_xattn_bv"][None, :],
        "L0F_gate": v["L0_ffn_gate_w"],
        "L0F_g": v["L0_ffn_Wg"].transpose(1, 0, 2).reshape(P, 8, 2, P),
        "L0F_u": v["L0_ffn_Wu"].transpose(1, 0, 2).reshape(P, 8, 2, P),
        "L0F_d": v["L0_ffn_Wd"].reshape(8, 2, P, P).transpose(2, 0, 1, 3),
        "L1X_W": np.stack([v["L1_xattn_" + n].T for n in ("Wqj", "Wqi", "Wkj", "Wki", "Wvj", "Wvi", "Wout")], 1),
        "L1X_cw": v["L1_xattn_council_weights"][None, :], "L1X_gain": v["L1_xattn_gain"].reshape(1, 1),
        "ptr": v["itok_BxS_0_4092"].reshape(B, NT, P).transpose(2, 0, 1).reshape(P, B * NT), "ids": v["itok_BxS_0_7"],
        "c_iota": np.arange(S2, dtype=f)[None, :],
        "c_rope": rope, "c_bands": bands,
        "L1F_qkv": v["L1_ffn_Wqkv"].reshape(6, P, 3, 2, T).transpose(0, 1, 3, 2, 4),
        "L1F_qks": np.stack([v["L1_ffn_q_scale"], np.roll(v["L1_ffn_q_scale"], 32, -1),
                             v["L1_ffn_k_scale"], np.roll(v["L1_ffn_k_scale"], 32, -1)], 1),
        "L1F_wo": v["L1_ffn_Wo"].reshape(6, 8, P, P).transpose(0, 2, 1, 3),
        "L1F_w1": v["L1_ffn_W1"], "L1F_w2a": v["L1_ffn_W2"][:, :256].reshape(6, 2, P, P).transpose(0, 2, 1, 3),
        "L1F_w2b": v["L1_ffn_W2"][:, 256:],
        "L1F_lngb": np.stack([v["L1_ffn_ln_g"], v["L1_ffn_ln_b"]], 2),
        "L1F_b1a": v["L1_ffn_b1"].reshape(6, 2, 341)[:, :, :256].reshape(6, 2, 2, P).transpose(0, 3, 2, 1),
        "L1F_b1b": v["L1_ffn_b1"].reshape(6, 2, 341)[:, :, 256:].transpose(0, 2, 1),
        "L1F_b2": v["L1_ffn_b2"][:, :, None],
        "L2X_W": np.stack([v["L2_xattn_" + n].T for n in ("Wq", "Wk", "Wv", "Wo")], 1),
        "L2X_b": np.stack([v["L2_xattn_bq"], v["L2_xattn_bo"]], 1), "L2X_bv": v["L2_xattn_bv"][None, :],
        "maskf": v["mask_SxS2_fk1"].reshape(NT, P, S2).transpose(1, 0, 2), "vctx": v["ctx_1024"].transpose(1, 0, 2),
        "c_rank": np.repeat(8 - np.arange(8, dtype=f)[None, :], P, 0),
        **{n + k: w for n, g, gb, w1, b1, w2, b2 in (
            ("L2F", "L2_ffn_Wg", "L2_ffn_bg", "L2_ffn_W1", "L2_ffn_b1", "L2_ffn_W2", "L2_ffn_b2"),
            ("L3F", "L3_ffn_gate_w", "L3_ffn_gate_b", "L3_ffn_w1", "L3_ffn_b1", "L3_ffn_w2", "L3_ffn_b2")) for k, w in (
            ("_gw", v[g]), ("_gb", v[gb][None, :]), ("_w1", v[w1].transpose(1, 0, 2).reshape(P, 8, 4, P)),
            ("_b1", v[b1].reshape(8, 4, P).transpose(2, 0, 1)), ("_w2", v[w2].reshape(8, 4, P, P).transpose(2, 0, 1, 3)),
            ("_b2", v[b2]))},
        "L3F_conv": v["L3_ffn_conv_w"].transpose(1, 2, 0),
        "L3F_wqkv": v["L3_ffn_wqkv"].reshape(3, P, P).transpose(2, 0, 1), "L3F_wo": v["L3_ffn_wo"].T,
        "L3F_b": np.stack([v["L3_ffn_conv_b"], v["L3_ffn_bqkv"][0:P], v["L3_ffn_bqkv"][P:2 * P], v["L3_ffn_bo"],
                           v["L3_ffn_ln1_g"], v["L3_ffn_ln1_b"], v["L3_ffn_ln2_g"], v["L3_ffn_ln2_b"]], 1),
        "L3F_bv": v["L3_ffn_bqkv"][None, 2 * P:],
    }
    nc = bacc.Bacc("TRN2", target_bir_lowering=False, num_devices=1)
    arrays = {k: np.ascontiguousarray(w) for k, w in arrays.items()}
    aps = {k: nc.dram_tensor(k, w.shape, mybir.dt.from_np(w.dtype), kind="ExternalInput").ap() for k, w in arrays.items()}
    out = nc.dram_tensor("out", (P, B, T), F32, kind="ExternalOutput").ap()
    build(nc, aps, out)
    r = run_bass_kernel_spmd(nc, [arrays], core_ids=[0])
    return np.ascontiguousarray(r.results[0]["out"].transpose(1, 2, 0))
```
